# Optimizing a Trainium2 kernel written in Bass

```python
import numpy as np
import jax
import jax.numpy as jnp

def _softmax(x, axis=-1):
    return jax.nn.softmax(x, axis=axis)

def _gelu(x):
    return jax.nn.gelu(x, approximate=True)

def _silu(x):
    return jax.nn.silu(x)

def _sigmoid(x):
    return jax.nn.sigmoid(x)

def _layernorm(x, axis=-1, eps=1e-05):
    m = jnp.mean(x, axis=axis, keepdims=True)
    v = jnp.var(x, axis=axis, keepdims=True)
    return (x - m) / jnp.sqrt(v + eps)

def _scatter_add(tgt, idx, src, axis=0):
    return tgt.at[idx].add(src)

def _segment_sum(src, seg, n):
    return jax.ops.segment_sum(src, seg, n)
kernel_name = 'mk_hybrid_d1_jaxref_r8_f18a81'

def setup_inputs(seed: int=0):
    np.random.seed(seed)
    _w = jnp.asarray

    def _L0_attn_a_setup():
        import jax, jax.numpy as jnp
        import numpy as np
        D_MODEL = 256
        N_HEADS = 16
        DN = 128
        DR = 64
        DV = 128
        KV_RANK = 64
        HI = 4
        DI = 64
        B, S = (2, 256)
        ROPE_THETA = 10000.0
        NEG = -1000000000.0

        def _rope_cos_sin(seq_len, dim, dtype):
            inv_freq = 1.0 / ROPE_THETA ** (jnp.arange(0, dim, 2, dtype=jnp.float32) / dim)
            ang = jnp.arange(seq_len, dtype=jnp.float32)[:, None] * inv_freq[None, :]
            emb = jnp.concatenate([ang, ang], axis=-1)
            return (jnp.cos(emb).astype(dtype), jnp.sin(emb).astype(dtype))

        def _rotate_half(x):
            x1, x2 = jnp.split(x, 2, axis=-1)
            return jnp.concatenate([-x2, x1], axis=-1)

        def _apply_rope(x, cos, sin):
            return x * cos + _rotate_half(x) * sin

        def _rmsnorm(x, w, eps=1e-06):
            var = jnp.mean(x * x, axis=-1, keepdims=True)
            return x * jax.lax.rsqrt(var + eps) * w
        key = jax.random.key(seed)
        ks = jax.random.split(key, 16)
        sc = lambda fan_in: 1.0 / np.sqrt(fan_in)
        return {'hidden_states': jax.random.normal(ks[0], (B, S, D_MODEL), jnp.float32), 'Wq_idx': jax.random.normal(ks[1], (D_MODEL, HI * DI), jnp.float32) * sc(D_MODEL), 'bq_idx': jnp.zeros((HI * DI,), jnp.float32), 'Wk_idx': jax.random.normal(ks[2], (D_MODEL, HI * DI), jnp.float32) * sc(D_MODEL), 'bk_idx': jnp.zeros((HI * DI,), jnp.float32), 'idx_w': jax.random.normal(ks[3], (HI,), jnp.float32) * 0.1, 'w_ctrl': jax.random.normal(ks[4], (D_MODEL,), jnp.float32) * sc(D_MODEL), 'b_ctrl': jnp.zeros((), jnp.float32), 'Wq': jax.random.normal(ks[5], (D_MODEL, N_HEADS * (DN + DR)), jnp.float32) * sc(D_MODEL), 'W_dkv': jax.random.normal(ks[6], (D_MODEL, KV_RANK + DR), jnp.float32) * sc(D_MODEL), 'kv_norm_w': jnp.ones((KV_RANK,), jnp.float32), 'W_ukv': jax.random.normal(ks[7], (KV_RANK, N_HEADS * (DN + DV)), jnp.float32) * sc(KV_RANK), 'Wo': jax.random.normal(ks[8], (N_HEADS * DV, D_MODEL), jnp.float32) * sc(N_HEADS * DV)}
    _L0_attn_a_in = _L0_attn_a_setup()

    def _L0_attn_b_setup():
        import jax, jax.numpy as jnp
        import numpy as np
        HIDDEN = 256
        HEADS = 16
        HEAD_DIM = HIDDEN // HEADS
        KV_DIM = 128
        SLOPE = 0.0625

        def alibi_bias(seq_len):
            i = jnp.arange(seq_len)[:, None]
            j = jnp.arange(seq_len)[None, :]
            return jnp.where(j <= i, -SLOPE * (i - j).astype(jnp.float32), -jnp.inf)
        key = jax.random.key(seed)
        ks = jax.random.split(key, 6)
        B, S = (2, 256)
        s = 0.02
        return {'hidden_states': jax.random.normal(ks[0], (B, S, HIDDEN), jnp.float32), 'w_dkv': jax.random.normal(ks[1], (KV_DIM, HIDDEN), jnp.float32) * s, 'w_q': jax.random.normal(ks[2], (HIDDEN, HIDDEN), jnp.float32) * s, 'w_uk': jax.random.normal(ks[3], (HIDDEN, KV_DIM), jnp.float32) * s, 'w_uv': jax.random.normal(ks[4], (HIDDEN, KV_DIM), jnp.float32) * s, 'w_o': jax.random.normal(ks[5], (HIDDEN, HIDDEN), jnp.float32) * s}
    _L0_attn_b_in = _L0_attn_b_setup()

    def _L0_ffn_setup():
        import jax, jax.numpy as jnp
        import numpy as np
        BS, SLEN, DIM, HID, E, TOPK = (4, 256, 256, 224, 8, 2)
        key = jax.random.key(seed)
        ks = jax.random.split(key, 9)
        s = 0.02
        return {'x': jax.random.normal(ks[0], (BS, SLEN, DIM), jnp.float32), 'gate_w': jax.random.normal(ks[1], (DIM, E), jnp.float32) * s, 'w1': jax.random.normal(ks[2], (E, DIM, HID), jnp.float32) * s, 'w2': jax.random.normal(ks[3], (E, HID, DIM), jnp.float32) * s, 'w3': jax.random.normal(ks[4], (E, DIM, HID), jnp.float32) * s, 'sw1': jax.random.normal(ks[5], (DIM, HID), jnp.float32) * s, 'sw2': jax.random.normal(ks[6], (HID, DIM), jnp.float32) * s, 'sw3': jax.random.normal(ks[7], (DIM, HID), jnp.float32) * s, 'expert_bias': jnp.zeros((E,), jnp.float32)}
    _L0_ffn_in = _L0_ffn_setup()
    _d = {'L0_attn_a_hidden_states': _L0_attn_a_in['hidden_states'], 'L0_attn_a_Wq_idx': _L0_attn_a_in['Wq_idx'], 'L0_attn_a_bq_idx': _L0_attn_a_in['bq_idx'], 'L0_attn_a_Wk_idx': _L0_attn_a_in['Wk_idx'], 'L0_attn_a_bk_idx': _L0_attn_a_in['bk_idx'], 'L0_attn_a_idx_w': _L0_attn_a_in['idx_w'], 'L0_attn_a_w_ctrl': _L0_attn_a_in['w_ctrl'], 'L0_attn_a_b_ctrl': _L0_attn_a_in['b_ctrl'], 'L0_attn_a_Wq': _L0_attn_a_in['Wq'], 'L0_attn_a_W_dkv': _L0_attn_a_in['W_dkv'], 'L0_attn_a_kv_norm_w': _L0_attn_a_in['kv_norm_w'], 'L0_attn_a_W_ukv': _L0_attn_a_in['W_ukv'], 'L0_attn_a_Wo': _L0_attn_a_in['Wo'], 'L0_attn_b_w_dkv': _L0_attn_b_in['w_dkv'], 'L0_attn_b_w_q': _L0_attn_b_in['w_q'], 'L0_attn_b_w_uk': _L0_attn_b_in['w_uk'], 'L0_attn_b_w_uv': _L0_attn_b_in['w_uv'], 'L0_attn_b_w_o': _L0_attn_b_in['w_o'], 'L0_ffn_gate_w': _L0_ffn_in['gate_w'], 'L0_ffn_w1': _L0_ffn_in['w1'], 'L0_ffn_w2': _L0_ffn_in['w2'], 'L0_ffn_w3': _L0_ffn_in['w3'], 'L0_ffn_sw1': _L0_ffn_in['sw1'], 'L0_ffn_sw2': _L0_ffn_in['sw2'], 'L0_ffn_sw3': _L0_ffn_in['sw3'], 'L0_ffn_expert_bias': _L0_ffn_in['expert_bias']}
    _x0 = _d['L0_attn_a_hidden_states']
    _d['L0_attn_a_hidden_states'] = jax.random.normal(jax.random.fold_in(jax.random.key(seed), 1), (1, 2048, 256), dtype=_x0.dtype)
    del _x0
    return _d

def reference(L0_attn_a_hidden_states, L0_attn_a_Wq_idx, L0_attn_a_bq_idx, L0_attn_a_Wk_idx, L0_attn_a_bk_idx, L0_attn_a_idx_w, L0_attn_a_w_ctrl, L0_attn_a_b_ctrl, L0_attn_a_Wq, L0_attn_a_W_dkv, L0_attn_a_kv_norm_w, L0_attn_a_W_ukv, L0_attn_a_Wo, L0_attn_b_w_dkv, L0_attn_b_w_q, L0_attn_b_w_uk, L0_attn_b_w_uv, L0_attn_b_w_o, L0_ffn_gate_w, L0_ffn_w1, L0_ffn_w2, L0_ffn_w3, L0_ffn_sw1, L0_ffn_sw2, L0_ffn_sw3, L0_ffn_expert_bias):

    def _L0_attn_a_ref(hidden_states, Wq_idx, bq_idx, Wk_idx, bk_idx, idx_w, w_ctrl, b_ctrl, Wq, W_dkv, kv_norm_w, W_ukv, Wo):
        import jax, jax.numpy as jnp
        import numpy as np
        D_MODEL = 256
        N_HEADS = 16
        DN = 128
        DR = 64
        DV = 128
        KV_RANK = 64
        HI = 4
        DI = 64
        B, S = (2, 256)
        ROPE_THETA = 10000.0
        NEG = -1000000000.0

        def _rope_cos_sin(seq_len, dim, dtype):
            inv_freq = 1.0 / ROPE_THETA ** (jnp.arange(0, dim, 2, dtype=jnp.float32) / dim)
            ang = jnp.arange(seq_len, dtype=jnp.float32)[:, None] * inv_freq[None, :]
            emb = jnp.concatenate([ang, ang], axis=-1)
            return (jnp.cos(emb).astype(dtype), jnp.sin(emb).astype(dtype))

        def _rotate_half(x):
            x1, x2 = jnp.split(x, 2, axis=-1)
            return jnp.concatenate([-x2, x1], axis=-1)

        def _apply_rope(x, cos, sin):
            return x * cos + _rotate_half(x) * sin

        def _rmsnorm(x, w, eps=1e-06):
            var = jnp.mean(x * x, axis=-1, keepdims=True)
            return x * jax.lax.rsqrt(var + eps) * w
        b, s, d = hidden_states.shape
        pooled = jnp.mean(hidden_states, axis=1)
        frac = jax.nn.sigmoid(pooled @ w_ctrl + b_ctrl)
        adaptive_k = jnp.clip(jnp.round(frac * s), 1, s).astype(jnp.int32)
        qi = (hidden_states @ Wq_idx + bq_idx).reshape(b, s, HI, DI)
        ki = (hidden_states @ Wk_idx + bk_idx).reshape(b, s, HI, DI)
        dots = jax.nn.relu(jnp.einsum('bqhd,bkhd->bhqk', qi, ki))
        index_scores = jnp.einsum('bhqk,h->bqk', dots, idx_w)
        sorted_desc = jnp.sort(index_scores, axis=-1)[..., ::-1]
        kth_idx = jnp.broadcast_to((adaptive_k - 1)[:, None, None], (b, s, 1))
        thr = jnp.take_along_axis(sorted_desc, kth_idx, axis=-1)
        top_k_mask = index_scores >= thr
        sparse_add = jnp.where(top_k_mask, 0.0, NEG)[:, None, :, :]
        causal = jnp.where(jnp.tril(jnp.ones((s, s), bool)), 0.0, NEG)[None, None]
        combined_mask = jnp.minimum(causal, sparse_add)
        q = (hidden_states @ Wq).reshape(b, s, N_HEADS, DN + DR)
        q_nope, q_rope = (q[..., :DN], q[..., DN:])
        ckv = hidden_states @ W_dkv
        c, k_rope = (ckv[..., :KV_RANK], ckv[..., KV_RANK:])
        kv = (_rmsnorm(c, kv_norm_w) @ W_ukv).reshape(b, s, N_HEADS, DN + DV)
        k_nope, v = (kv[..., :DN], kv[..., DN:])
        cos, sin = _rope_cos_sin(s, DR, hidden_states.dtype)
        q_rope = _apply_rope(q_rope, cos[None, :, None, :], sin[None, :, None, :])
        k_rope = _apply_rope(k_rope, cos[None], sin[None])
        q_full = jnp.concatenate([q_nope, q_rope], axis=-1)
        k_full = jnp.concatenate([k_nope, jnp.broadcast_to(k_rope[:, :, None, :], (b, s, N_HEADS, DR))], axis=-1)
        scale = 1.0 / np.sqrt(DN + DR)
        scores = jnp.einsum('bqhd,bkhd->bhqk', q_full, k_full) * scale + combined_mask
        attn = jax.nn.softmax(scores, axis=-1)
        out = jnp.einsum('bhqk,bkhd->bqhd', attn, v).reshape(b, s, N_HEADS * DV)
        return out @ Wo

    def _L0_attn_b_ref(hidden_states, w_dkv, w_q, w_uk, w_uv, w_o):
        import jax, jax.numpy as jnp
        import numpy as np
        HIDDEN = 256
        HEADS = 16
        HEAD_DIM = HIDDEN // HEADS
        KV_DIM = 128
        SLOPE = 0.0625

        def alibi_bias(seq_len):
            i = jnp.arange(seq_len)[:, None]
            j = jnp.arange(seq_len)[None, :]
            return jnp.where(j <= i, -SLOPE * (i - j).astype(jnp.float32), -jnp.inf)
        B, S, _ = hidden_states.shape
        scale = HEAD_DIM ** (-0.5)
        c_kv = hidden_states @ w_dkv.T
        q = (hidden_states @ w_q.T).reshape(B, S, HEADS, HEAD_DIM)
        k = (c_kv @ w_uk.T).reshape(B, S, HEADS, HEAD_DIM)
        v = (c_kv @ w_uv.T).reshape(B, S, HEADS, HEAD_DIM)
        scores = jnp.einsum('bqhd,bkhd->bhqk', q, k) * scale
        scores = scores + alibi_bias(S)[None, None]
        attn = jax.nn.softmax(scores, axis=-1)
        out = jnp.einsum('bhqk,bkhd->bqhd', attn, v).reshape(B, S, HIDDEN)
        return out @ w_o.T

    def _L0_ffn_ref(x, gate_w, w1, w2, w3, sw1, sw2, sw3, expert_bias):
        import jax, jax.numpy as jnp
        import numpy as np
        BS, SLEN, DIM, HID, E, TOPK = (4, 256, 256, 224, 8, 2)
        bs, slen, dim = x.shape
        T = bs * slen
        xf = x.reshape(T, dim)
        scores = jax.nn.softmax((xf @ gate_w).astype(jnp.float32), axis=-1)
        _, sel = jax.lax.top_k(scores + expert_bias[None, :], TOPK)
        top_scores = jnp.take_along_axis(scores, sel, axis=1)
        flat_sel = sel.reshape(-1)
        counts = jnp.bincount(flat_sel, length=E).astype(jnp.int32)
        order = jnp.argsort(flat_sel, stable=True)
        top_scores_sorted = top_scores.reshape(-1)[order]
        token_idx = order // TOPK
        routed_in = xf[token_idx] * top_scores_sorted[:, None]
        h = jax.nn.silu(jax.lax.ragged_dot(routed_in, w1, counts)) * jax.lax.ragged_dot(routed_in, w3, counts)
        routed_out = jax.lax.ragged_dot(h, w2, counts)
        out = jax.nn.silu(xf @ sw1) * (xf @ sw3) @ sw2
        out = out.at[token_idx].add(routed_out)
        return out.reshape(bs, slen, dim)
    x = L0_attn_a_hidden_states
    x = x + _L0_attn_a_ref(_layernorm(x, axis=-1), L0_attn_a_Wq_idx, L0_attn_a_bq_idx, L0_attn_a_Wk_idx, L0_attn_a_bk_idx, L0_attn_a_idx_w, L0_attn_a_w_ctrl, L0_attn_a_b_ctrl, L0_attn_a_Wq, L0_attn_a_W_dkv, L0_attn_a_kv_norm_w, L0_attn_a_W_ukv, L0_attn_a_Wo)
    x = x + _L0_ffn_ref(_layernorm(x, axis=-1), L0_ffn_gate_w, L0_ffn_w1, L0_ffn_w2, L0_ffn_w3, L0_ffn_sw1, L0_ffn_sw2, L0_ffn_sw3, L0_ffn_expert_bias)
    x = x + _L0_attn_b_ref(_layernorm(x, axis=-1), L0_attn_b_w_dkv, L0_attn_b_w_q, L0_attn_b_w_uk, L0_attn_b_w_uv, L0_attn_b_w_o)
    x = x + _L0_ffn_ref(_layernorm(x, axis=-1), L0_ffn_gate_w, L0_ffn_w1, L0_ffn_w2, L0_ffn_w3, L0_ffn_sw1, L0_ffn_sw2, L0_ffn_sw3, L0_ffn_expert_bias)
    return x

_drawn_inputs = setup_inputs


def setup_inputs(seed=0):
    import zlib

    import numpy as np

    out = dict(_drawn_inputs(seed))
    spreads = {'L0_attn_a_bq_idx': (0.0, 0.1),
     'L0_attn_a_bk_idx': (0.0, 0.1),
     'L0_attn_a_kv_norm_w': (1.0, 0.2),
     'L0_ffn_expert_bias': (0.0, 0.8)}
    factors = {'L0_attn_a_w_ctrl': 8.0,
     'L0_attn_b_w_dkv': 8.0,
     'L0_attn_b_w_q': 8.0,
     'L0_attn_b_w_uk': 8.0,
     'L0_attn_b_w_uv': 8.0,
     'L0_attn_b_w_o': 8.0,
     'L0_ffn_gate_w': 8.0,
     'L0_ffn_w1': 8.0,
     'L0_ffn_w2': 8.0,
     'L0_ffn_w3': 8.0}
    for name, (base, spread) in spreads.items():
        noise = np.random.default_rng([zlib.crc32(name.encode()), seed]).standard_normal(out[name].shape)
        drawn = base * np.exp(spread * noise) if base else spread * noise
        out[name] = jnp.asarray(drawn.astype(out[name].dtype))
    for name, factor in factors.items():
        out[name] = (out[name] * factor).astype(out[name].dtype)
    return out
```

```python
from contextlib import ExitStack

import concourse.bass as bass
from concourse import mybir

F32 = mybir.dt.float32
F32R = mybir.dt.float32r
BF16 = mybir.dt.bfloat16
U32 = mybir.dt.uint32
I32 = mybir.dt.int32
ALU = mybir.AluOpType
ACT = mybir.ActivationFunctionType
AX = mybir.AxisListType

P = 128
S = 2048
D = 256
NT = S // P
KC = D // P
CH = 512
NCH = S // CH
LN_EPS = 1e-5
NEG = -1.0e9

HA, DN, DR, DV, RANK = 16, 128, 64, 128, 64
HALF = DR // 2
HI, DI = 4, 64
RMS_EPS = 1e-6
SCALE_A = 1.0 / float(DN + DR) ** 0.5
HB = 16
DHB = D // HB
SLOPE = 0.0625
KVB = 128
SCALE_B = float(DHB) ** -0.5
R_LO, R_HI2, R_ALIBI, R_MAX = 32, 64, 80, 96
HIDE = -1.0e30
E, HID, TOPK = 8, 224, 2
EE = E + 1
HH = HID // 2

GT = 8
TOP = 8
PROBES = 7
PROBE_STEPS = GT // 2 + 1 + 2 + 4 + 8
NEAR, EDGE = 0.4, 0.002
HALVINGS = 64
HALVING_STEPS = 2 + GT + 2 + 2
BIG = 3.0e38
ROUND = 12582912.0

TRI = [t * (t + 1) // 2 * P for t in range(NT + 1)]
CHUNKS = [(t + 4) // 4 for t in range(NT)]
BASE = [HA * sum(CHUNKS[:t]) for t in range(NT + 1)]


class Chain:

    def __init__(self, eng, sem):
        self.eng, self.sem, self.n = eng, sem, 0

    def step(self, ins):
        ins.then_inc(self.sem, 1)
        self.n += 1

    def wait(self, back=0):
        self.eng.wait_ge(self.sem, self.n - back if back else self.n)


class Phase(ExitStack):

    def __init__(self, nc, tag):
        super().__init__()
        self.nc, self.tag, self.used = nc, tag, []

    def sb(self, name, shape, dt=F32):
        return self.enter_context(self.nc.sbuf_tensor(f"{self.tag}_{name}", shape, dt))

    def sem(self, name):
        self.used.append(self.enter_context(self.nc.semaphore(f"{self.tag}_{name}")))
        return self.used[-1]

    def __exit__(self, kind, *rest):
        if kind is None:
            with self.nc.Block() as block:
                @block.gpsimd
                def _(pool):
                    for one in self.used:
                        pool.sem_clear(one)
        return super().__exit__(kind, *rest)


def layernorm(nc, tag, x, xT, bank, ident):
    with Phase(nc, tag) as phase:
        sb, sem = phase.sb, phase.sem

        stats = sb("stats", [P, NT, 6])
        mean = sb("mean", [P, NT])
        half = sb("half", [P, NT])
        var = sb("var", [P, NT])
        std = sb("std", [P, NT])
        rstd = sb("rstd", [P, NT])
        xn = [sb(f"xn{p}", [P, D]) for p in range(2)]
        stats_done = sem("stats_done")
        dve_step = sem("dve_step")
        var_ready = sem("var_ready")
        std_ready = sem("std_ready")
        xn_ready = sem("xn_ready")
        turned = sem("turned")
        stored = sem("stored")

        with nc.Block() as block:
            @block.vector
            def _(dve):
                with dve.Fori(0, NT) as t:
                    nc.vector.bn_stats(stats[:, t, :], x[:, t, :]).then_inc(stats_done, 1)
                dve.wait_ge(stats_done, NT)
                chain = Chain(dve, dve_step)
                chain.step(nc.vector.tensor_tensor(mean[:], stats[:, :, 1], stats[:, :, 4], ALU.add))
                chain.step(nc.vector.tensor_tensor(half[:], stats[:, :, 1], stats[:, :, 4], ALU.subtract))
                chain.step(nc.vector.tensor_tensor(var[:], stats[:, :, 2], stats[:, :, 5], ALU.add))
                chain.wait()
                chain.step(nc.vector.tensor_scalar(mean[:], mean[:], 0.5, None, ALU.mult))
                chain.step(nc.vector.tensor_scalar(half[:], half[:], 0.5, None, ALU.mult))
                chain.step(nc.vector.tensor_scalar(var[:], var[:], 1.0 / D, LN_EPS, ALU.mult, ALU.add))
                chain.wait()
                chain.step(nc.vector.tensor_tensor(half[:], half[:], half[:], ALU.mult))
                chain.wait()
                nc.vector.tensor_tensor(var[:], var[:], half[:], ALU.add).then_inc(var_ready, 1)
                dve.wait_ge(std_ready, 1)
                chain.step(nc.vector.reciprocal(rstd[:], std[:]))
                chain.wait()
                with dve.Fori(0, NT // 2) as i:
                    for p in range(2):
                        t = i * 2 + p
                        dve.wait_ge(turned, t + 1)
                        nc.vector.tensor_scalar(xn[p][:], x[:, t, :], mean[:, bass.ds(t, 1)], rstd[:, bass.ds(t, 1)],
                                                ALU.subtract, ALU.mult).then_inc(xn_ready, 1)

            @block.scalar
            def _(act):
                act.wait_ge(var_ready, 1)
                nc.scalar.activation(std[:], var[:], ACT.Sqrt).then_inc(std_ready, 1)
                act.sem_inc(stored, 2)
                with act.Fori(0, NT // 2) as i:
                    for p in range(2):
                        t = i * 2 + p
                        act.wait_ge(turned, t + 3)
                        nc.scalar.activation(xT[:, :, bass.ds(t * P, P)],
                                             bank[p][:, 0:D].rearrange("p (c n) -> p c n", c=KC),
                                             ACT.Copy).then_inc(stored, 1)

            @block.tensor
            def _(pe):
                pe.sem_inc(turned, 2)
                with pe.Fori(0, NT // 2) as i:
                    for p in range(2):
                        t = i * 2 + p
                        pe.wait_ge(xn_ready, t + 1)
                        pe.wait_ge(stored, t + 1)
                        for c in range(KC):
                            last = nc.tensor.transpose(bank[p][:, c * P:(c + 1) * P], xn[p][:, c * P:(c + 1) * P],
                                                       ident[:])
                        last.then_inc(turned, 1)


def index_mask(nc, arg, x, xT, bank, const, bias, empty, filled):
    with Phase(nc, "ix") as phase:
        sb, sem = phase.sb, phase.sem

        k_stack = sb("k_stack", [P, HI, S], F32R)
        k_lo = sb("k_lo", [P, HI // 2, S], F32R)
        q_stack = sb("q_stack", [P, HI, GT * P], F32R)
        kth = sb("kth", [P, 1])
        weight = sb("weight", [P, HI])
        w_q = sb("w_q", [P, KC, HI, 2, DI])
        b_q = sb("b_q", [P, HI])

        def high(h):
            return slice(h % 2 * DI, h % 2 * DI + DI)

        def low(h):
            return high(h + 1)

        with Phase(nc, "ixp") as inner:
            sbi, semi = inner.sb, inner.sem

            w_k = sbi("w_k", [P, KC, HI, 2, DI])
            b_k = sbi("b_k", [P, HI])
            ctrl = sbi("ctrl", [P, KC])
            ctrl_wide = sbi("ctrl_wide", [P, KC, P])
            bctrl = sbi("bctrl", [P, 1])
            pooled = sbi("pooled", [P, KC])
            z = sbi("z", [P, 1])
            ez = sbi("ez", [P, 1])
            loaded = semi("loaded")
            projected = semi("projected")
            high_done = semi("high_done")
            low_done = semi("low_done")
            pooled_ready = semi("pooled_ready")
            z_ready = semi("z_ready")
            zs_ready = semi("zs_ready")
            ez_ready = semi("ez_ready")
            dve_step = semi("dve_step")
            LOADS = 8 + 4 + 3
            with nc.Block() as block:
                @block.sync
                def _(sp):
                    for w, b, name in ((w_k, b_k, "k"), (w_q, b_q, "q")):
                        for half in range(2):
                            for c in range(KC):
                                sp.dma_start(w[:, c, :, half, :], arg[f"W{name}_idx"][c * P:(c + 1) * P, :].rearrange(
                                    "p (h d) -> p h d", h=HI)).then_inc(loaded, 16)
                    for half in range(2):
                        rows = slice(half * DI, half * DI + DI)
                        sp.dma_start(b_k[rows, :], arg["bk_idx"]).then_inc(loaded, 16)
                        sp.dma_start(b_q[rows, :], arg["bq_idx"]).then_inc(loaded, 16)
                    sp.dma_start(ctrl[:], arg["w_ctrl"]).then_inc(loaded, 16)
                    sp.dma_start(bctrl[:], arg["b_ctrl"].partition_broadcast(P)).then_inc(loaded, 16)
                    sp.dma_start(weight[:], arg["idx_w"].partition_broadcast(P)).then_inc(loaded, 16)
                    sp.wait_ge(loaded, LOADS * 16)

                @block.tensor
                def _(pe):
                    pe.wait_ge(loaded, LOADS * 16)
                    for n in range(HI * NCH):
                        h, c = divmod(n, NCH)
                        if n >= 4:
                            pe.wait_ge(low_done, n - 3)
                        for k in range(KC):
                            last = nc.tensor.matmul(bank[n % 4][:], w_k[:, k, h, :, :].rearrange("p a d -> p (a d)"),
                                                    xT[:, k, c * CH:(c + 1) * CH], start=k == 0, stop=k == KC - 1)
                        last.then_inc(projected, 1)
                    pe.wait_ge(pooled_ready, 1)
                    for k in range(KC):
                        last = nc.tensor.matmul(bank[4][:, 0:1], ctrl_wide[:, k, :], pooled[:, k:k + 1],
                                                start=k == 0, stop=k == KC - 1)
                    last.then_inc(z_ready, 1)

                @block.scalar
                def _(act):
                    act.wait_ge(loaded, LOADS * 16)
                    for n in range(HI * NCH):
                        h, c = divmod(n, NCH)
                        act.wait_ge(projected, n + 1)
                        nc.scalar.activation(k_stack[:, h, c * CH:(c + 1) * CH], bank[n % 4][:], ACT.Identity,
                                             bias=b_k[:, h:h + 1]).then_inc(high_done, 1)
                    act.wait_ge(zs_ready, 1)
                    nc.scalar.activation(ez[:], z[:], ACT.Exp, scale=-1.0).then_inc(ez_ready, 1)

                @block.vector
                def _(dve):
                    chain = Chain(dve, dve_step)
                    dve.wait_ge(loaded, LOADS * 16)
                    for k in range(KC):
                        chain.step(nc.vector.tensor_copy(ctrl_wide[:, k, :], ctrl[:, k:k + 1].to_broadcast([P, P])))
                    chain.wait()
                    nc.vector.tensor_reduce(pooled[:], xT[:], AX.X, ALU.add).then_inc(pooled_ready, 1)
                    for n in range(HI * NCH):
                        h, c = divmod(n, NCH)
                        rows, cols = high(h), slice(c * CH, (c + 1) * CH)
                        dve.wait_ge(high_done, n + 1)
                        nc.vector.scalar_tensor_tensor(out=k_lo[rows, h // 2, cols], in0=bank[n % 4][rows, :],
                                                       scalar=b_k[rows, h:h + 1], in1=k_stack[rows, h, cols].bitcast(F32),
                                                       op0=ALU.add, op1=ALU.subtract).then_inc(low_done, 1)
                    dve.wait_ge(z_ready, 1)
                    nc.vector.scalar_tensor_tensor(out=z[:], in0=bank[4][:, 0:1], scalar=1.0 / S, in1=bctrl[:],
                                                   op0=ALU.mult, op1=ALU.add).then_inc(zs_ready, 1)
                    dve.wait_ge(ez_ready, 1)
                    chain.step(nc.vector.tensor_scalar(ez[:], ez[:], 1.0, None, ALU.add))
                    chain.wait()
                    chain.step(nc.vector.reciprocal(ez[:], ez[:]))
                    chain.wait()
                    chain.step(nc.vector.tensor_scalar(ez[:], ez[:], float(S), None, ALU.mult))
                    chain.wait()
                    chain.step(nc.vector.tensor_scalar(ez[:], ez[:], ROUND, None, ALU.add))
                    chain.wait()
                    chain.step(nc.vector.tensor_scalar(ez[:], ez[:], ROUND, None, ALU.subtract))
                    chain.wait()
                    chain.step(nc.vector.tensor_scalar(kth[:], ez[:], 1.0, float(S), ALU.max, ALU.min))
                    chain.wait()

        scores = sb("scores", [P, GT, S])
        qs = [sb(f"qs{p}", [P, HI, P], F32R) for p in range(2)]
        spare = x[:].rearrange("p t d -> p (t d)")
        relu = spare[:, 0:2 * (HI - 1) * CH].rearrange("p (a h n) -> p a h n", a=2, h=HI - 1)
        masked = spare[:, 0:S]
        junk_act = spare[:, S:S + S // 2].bitcast(BF16)
        row = {name: sb(name, [P, GT]) for name in (
            "low", "high", "lo", "hi", "above", "at_least", "at_lo", "at_hi", "tiny", "zeros", "count", "signs", "nonzero",
            "part", "step", "mid", "neg_mid", "outside", "rank", "bad", "more", "thr")}
        flag = {name: sb(name, [P, GT], U32) for name in ("pos", "neg", "at_zero", "enough", "short")}
        aim = sb("aim", [P, 1])
        shift = sb("shift", [P, GT])
        places = sb("places", [P, TOP])
        best = sb("best", [P, GT, TOP])
        pick = sb("pick", [P, GT, TOP])
        bad_row = sb("bad_row", [P, 1])
        unsolved = sb("unsolved", [P, 1], I32)
        top = sb("top", [P, NT])
        for g in range(NT // GT):
            index_scores(nc, f"ixs{g}", g, xT, bank, w_q, b_q, q_stack, k_stack, k_lo, qs, relu, weight, scores, high, low)
            index_threshold(nc, f"ixt{g}", g, bank, const, scores, kth, masked, junk_act, row, flag, aim, shift,
                            places, best, pick, bad_row, unsolved, top, bias, empty, filled)


def index_scores(nc, tag, g, xT, bank, w_q, b_q, q_stack, k_stack, k_lo, qs, relu, weight, scores, high, low):
    with Phase(nc, tag) as phase:
        sem = phase.sem

        projected = sem("projected")
        high_done = sem("high_done")
        low_done = sem("low_done")
        staged = sem("staged")
        pool_go = sem("pool_go")
        dotted = sem("dotted")
        first_used = sem("first_used")
        relu_done = sem("relu_done")
        summed = sem("summed")
        QC = GT * P // CH
        with nc.Block() as block:
            @block.gpsimd
            def _(pool):
                pool.wait_ge(low_done, HI * QC)
                with pool.Fori(0, GT // 2) as i:
                    for p in range(2):
                        t = i * 2 + p
                        pool.wait_ge(dotted, (t + 1) * NCH * HI)
                        pool.sem_inc(pool_go, 1)
                        nc.gpsimd.tensor_copy(qs[p][:], q_stack[:, :, bass.ds(t * P, P)].bitcast(F32)).then_inc(staged, 1)

            @block.tensor
            def _(pe):
                pe.sem_inc(dotted, NCH * HI * 2)
                for n in range(HI * QC):
                    h, c = divmod(n, QC)
                    for k in range(KC):
                        last = nc.tensor.matmul(bank[n][:], w_q[:, k, h, :, :].rearrange("p a d -> p (a d)"),
                                                xT[:, k, g * GT * P + c * CH:g * GT * P + (c + 1) * CH],
                                                start=k == 0, stop=k == KC - 1)
                    last.then_inc(projected, 1)
                with pe.Fori(0, GT // 2) as i:
                    for p in range(2):
                        t = i * 2 + p
                        pe.wait_ge(staged, t + 1)
                        for c in range(NCH):
                            n = t * NCH + c
                            cols = slice(c * CH, (c + 1) * CH)
                            pe.wait_ge(first_used, n + 1)
                            pe.wait_ge(relu_done, n * (HI - 1) + 1 + HI - 2)
                            for h in range(HI):
                                out = bank[c % 2 * HI + h]
                                nc.tensor.matmul(out[:], qs[p][:, h, :], k_stack[:, h, cols], start=True, stop=False)
                                nc.tensor.matmul(out[:], qs[p][high(h), h, :], k_lo[high(h), h // 2, cols],
                                                 start=False, stop=True).then_inc(dotted, 1)

            @block.scalar
            def _(act):
                for n in range(HI * QC):
                    h, c = divmod(n, QC)
                    act.wait_ge(projected, n + 1)
                    nc.scalar.activation(q_stack[:, h, c * CH:(c + 1) * CH], bank[n][:], ACT.Identity,
                                         bias=b_q[:, h:h + 1]).then_inc(high_done, 1)
                act.sem_inc(relu_done, 2 * (HI - 1))
                with act.Fori(0, GT) as t:
                    for c in range(NCH):
                        n = t * NCH + c
                        act.wait_ge(summed, n * HI + HI)
                        for h in range(1, HI):
                            act.wait_ge(dotted, n * HI + h + 1 + NCH * HI * 2)
                            nc.scalar.activation(relu[:, c % 2, h - 1, :], bank[c % 2 * HI + h][:],
                                                 ACT.Relu).then_inc(relu_done, 1)

            @block.vector
            def _(dve):
                for n in range(HI * QC):
                    h, c = divmod(n, QC)
                    rows, cols = low(h), slice(c * CH, (c + 1) * CH)
                    dve.wait_ge(high_done, n + 1)
                    nc.vector.scalar_tensor_tensor(out=q_stack[rows, h, cols], in0=bank[n][rows, :],
                                                   scalar=b_q[rows, h:h + 1], in1=q_stack[rows, h, cols].bitcast(F32),
                                                   op0=ALU.add, op1=ALU.subtract).then_inc(low_done, 1)
                dve.sem_inc(first_used, 2)
                dve.sem_inc(summed, 2 * HI)
                with dve.Fori(0, GT) as t:
                    for c in range(NCH):
                        n = t * NCH + c
                        into = scores[:, t, c * CH:(c + 1) * CH]
                        dve.wait_ge(dotted, n * HI + 1 + NCH * HI * 2)
                        nc.vector.tensor_scalar(into, bank[c % 2 * HI][:], 0.0, weight[:, 0:1],
                                                ALU.max, ALU.mult).then_inc(first_used, 1)
                        dve.wait_ge(first_used, n + 3)
                        for h in range(1, HI):
                            dve.wait_ge(relu_done, n * (HI - 1) + h + 2 * (HI - 1))
                            if h > 1:
                                dve.wait_ge(summed, n * HI + h - 1 + 2 * HI)
                            last = nc.vector.scalar_tensor_tensor(
                                out=into, in0=relu[:, c % 2, h - 1, :], scalar=weight[:, h:h + 1], in1=into,
                                op0=ALU.mult, op1=ALU.add)
                            last.then_inc(summed, 1 if h < HI - 1 else 2)


def index_threshold(nc, tag, g, bank, const, scores, kth, masked, junk_act, row, flag, aim, shift, places, best, pick,
                    bad_row, unsolved, top, bias, empty, filled):
    own, other = slice(0, GT // 2), slice(GT // 2, GT)
    junk = [bias[:, TRI[g * GT] + p * S:TRI[g * GT] + (p + 1) * S] for p in range(2)]
    with Phase(nc, tag) as phase:
        sem = phase.sem

        dve_step = sem("dve_step")
        zero_step = sem("zero_step")
        mid_ready = sem("mid_ready")
        go = sem("go")
        sign_done = sem("sign_done")
        bad_ready = sem("bad_ready")
        summed = sem("summed")
        halved = sem("halved")
        with nc.Block() as block:
            @block.scalar
            def _(act):
                for j in range(GT):
                    if j:
                        act.wait_ge(zero_step, 2 * j)
                    nc.scalar.activation(junk_act, scores[:, j, :], ACT.Sign,
                                         accum_out=row["signs"][:, j:j + 1]).then_inc(zero_step, 1)
                    act.wait_ge(zero_step, 2 * j + 1)
                    nc.scalar.activation(junk_act, junk_act, ACT.Abs,
                                         accum_out=row["nonzero"][:, j:j + 1]).then_inc(zero_step, 1)
                act.wait_ge(zero_step, 2 * GT)
                with act.Fori(0, PROBES) as r:
                    act.wait_ge(mid_ready, r + 1)
                    for j in range(GT // 2, GT):
                        if j > GT // 2:
                            act.wait_ge(sign_done, r * (GT // 2) + j - GT // 2)
                        nc.scalar.activation(junk_act, scores[:, j, :], ACT.Sign, bias=row["neg_mid"][:, j:j + 1],
                                             accum_out=row["signs"][:, j:j + 1]).then_inc(sign_done, 1)

            @block.tensor
            def _(pe):
                pe.wait_ge(bad_ready, 1)
                nc.tensor.matmul(bank[7][:, 0:1], const["mean"][:], bad_row[:], start=True, stop=True).then_inc(summed, 1)

            @block.vector
            def _(dve):
                chain = Chain(dve, dve_step)
                step, wait = chain.step, chain.wait
                scalar, tensor, fill, copy = nc.vector.tensor_scalar, nc.vector.tensor_tensor, nc.vector.memset, nc.vector.tensor_copy
                at = {name: t[:] for name, t in {**row, **flag}.items()}

                def choose(into, where, value):
                    dve.sem_inc(go, 1)
                    step(nc.vector.copy_predicated(at[into], at[where], at[value]))

                def probe(first):
                    wait()
                    step(scalar(at["part"], at["at_lo"], aim[:, 0:1], None, ALU.subtract))
                    step(tensor(at["step"], at["at_lo"], at["at_hi"], ALU.subtract))
                    wait()
                    step(nc.vector.reciprocal(at["step"], at["step"]))
                    wait()
                    step(tensor(at["part"], at["part"], at["step"], ALU.mult))
                    wait()
                    if first:
                        step(scalar(at["part"], at["part"], NEAR, None, ALU.mult))
                        wait()
                        step(tensor(at["part"], at["part"], shift[:], ALU.add))
                        wait()
                    step(scalar(at["part"], at["part"], EDGE, 1.0 - EDGE, ALU.max, ALU.min))
                    step(tensor(at["step"], at["hi"], at["lo"], ALU.subtract))
                    wait()
                    step(tensor(at["step"], at["step"], at["part"], ALU.mult))
                    wait()
                    step(tensor(at["mid"], at["step"], at["lo"], ALU.add))
                    wait()
                    scalar(at["neg_mid"], at["mid"], -1.0, None, ALU.mult).then_inc(mid_ready, 1)

                step(nc.vector.tensor_reduce(at["low"], scores[:], AX.X, ALU.min))
                step(nc.vector.tensor_reduce(at["high"], scores[:], AX.X, ALU.max))
                step(fill(at["tiny"], 1.2e-38))
                step(fill(at["zeros"], 0.0))
                step(fill(at["at_lo"], float(S)))
                step(fill(at["at_hi"], 0.0))
                step(scalar(aim[:], kth[:], (TOP + 1) / 2.0, None, ALU.subtract))
                for n in range(TOP):
                    step(fill(places[:, n:n + 1], n + 1.0))
                wait()
                step(tensor(at["step"], at["high"], at["low"], ALU.subtract))
                wait()
                step(nc.vector.scalar_tensor_tensor(out=at["high"], in0=at["step"], scalar=2.0 ** -10, in1=at["high"],
                                                    op0=ALU.mult, op1=ALU.add))
                wait()
                step(scalar(at["high"], at["high"], 1e-30, None, ALU.add))
                dve.wait_ge(zero_step, 2 * GT)
                step(tensor(at["above"], at["nonzero"], at["signs"], ALU.add))
                step(tensor(at["at_least"], at["signs"], at["nonzero"], ALU.subtract))
                wait()
                step(scalar(at["above"], at["above"], 0.5, None, ALU.mult))
                step(scalar(at["at_least"], at["at_least"], 0.5, float(S), ALU.mult, ALU.add))
                step(copy(at["lo"], at["low"]))
                step(copy(at["hi"], at["high"]))
                wait()
                step(scalar(at["pos"], at["above"], kth[:, 0:1], None, ALU.is_ge))
                step(scalar(at["neg"], at["at_least"], kth[:, 0:1], None, ALU.is_lt))
                step(scalar(at["outside"], at["above"], kth[:, 0:1], None, ALU.is_ge))
                step(scalar(shift[:], at["at_least"], kth[:, 0:1], None, ALU.is_lt))
                wait()
                choose("lo", "pos", "tiny")
                choose("at_lo", "pos", "above")
                choose("hi", "neg", "zeros")
                choose("at_hi", "neg", "at_least")
                step(tensor(at["outside"], at["outside"], shift[:], ALU.add))
                wait()
                step(scalar(shift[:], shift[:], 1.0 - NEAR, None, ALU.mult))
                step(scalar(at["at_zero"], at["outside"], 0.5, None, ALU.is_lt))
                probe(first=True)
                before = chain.n
                with dve.Fori(0, PROBES) as r:
                    chain.n = r * PROBE_STEPS + before
                    dve.wait_ge(mid_ready, r + 1)
                    for j in range(GT // 2):
                        chain.wait(back=1 if j else 0)
                        step(scalar(junk[j % 2], scores[:, j, :], row["mid"][:, j:j + 1], 0.0, ALU.is_ge, ALU.add,
                                    accum_out=row["count"][:, j:j + 1]))
                    dve.wait_ge(sign_done, r * (GT // 2) + GT // 2)
                    step(scalar(row["count"][:, other], row["signs"][:, other], 0.5, S / 2.0, ALU.mult, ALU.add))
                    wait()
                    step(scalar(at["enough"], at["count"], kth[:, 0:1], None, ALU.is_ge))
                    step(scalar(at["short"], at["count"], kth[:, 0:1], None, ALU.is_lt))
                    wait()
                    choose("lo", "enough", "mid")
                    choose("at_lo", "enough", "count")
                    choose("hi", "short", "mid")
                    choose("at_hi", "short", "count")
                    probe(first=False)
                chain.n = before + PROBES * PROBE_STEPS
                wait()
                for j in range(GT):
                    if j < GT // 2:
                        step(scalar(junk[j % 2], scores[:, j, :], row["hi"][:, j:j + 1], None, ALU.is_ge))
                    else:
                        step(scalar(junk[j % 2], scores[:, j, :], row["hi"][:, j:j + 1], 0.0, ALU.is_ge, ALU.add,
                                    accum_out=row["at_hi"][:, j:j + 1]))
                    wait()
                    step(nc.vector.scalar_tensor_tensor(out=masked, in0=junk[j % 2], scalar=-BIG, in1=scores[:, j, :],
                                                        op0=ALU.mult, op1=ALU.add))
                    wait()
                    step(nc.vector.max(best[:, j, :], masked))
                wait()
                step(scalar(at["rank"], at["at_hi"], -1.0, kth[:, 0:1], ALU.mult, ALU.add))
                wait()
                wide = [P, GT, TOP]
                step(tensor(pick[:], places[:].unsqueeze(1).to_broadcast(wide), row["rank"][:].unsqueeze(2).to_broadcast(wide),
                            ALU.is_equal))
                step(scalar(at["bad"], at["rank"], TOP + 0.5, None, ALU.is_gt))
                step(scalar(at["more"], at["rank"], 0.5, None, ALU.is_lt))
                wait()
                step(tensor(pick[:], pick[:], best[:], ALU.mult))
                step(tensor(at["bad"], at["bad"], at["more"], ALU.add))
                wait()
                step(nc.vector.tensor_reduce(at["thr"], pick[:], AX.X, ALU.add))
                step(tensor(at["bad"], at["bad"], at["outside"], ALU.mult))
                wait()
                nc.vector.tensor_reduce(bad_row[:], at["bad"], AX.X, ALU.max).then_inc(bad_ready, 1)
                choose("thr", "at_zero", "zeros")
                dve.wait_ge(summed, 1)
                step(scalar(unsolved[:], bank[7][:, 0:1], 0.0, None, ALU.is_gt))
                wait()
                some = dve.value_load(unsolved[0:1, 0:1], min_val=0, max_val=1)
                with dve.If(some > 0):
                    halve = Chain(dve, halved)
                    halve.step(copy(at["lo"], at["low"]))
                    halve.step(copy(at["hi"], at["high"]))
                    start = halve.n
                    with dve.Fori(0, HALVINGS) as r:
                        halve.n = r * HALVING_STEPS + start
                        halve.wait()
                        halve.step(tensor(at["mid"], at["lo"], at["hi"], ALU.add))
                        halve.wait()
                        halve.step(scalar(at["mid"], at["mid"], 0.5, None, ALU.mult))
                        for j in range(GT):
                            halve.wait()
                            halve.step(scalar(junk[0], scores[:, j, :], row["mid"][:, j:j + 1], 0.0, ALU.is_ge, ALU.add,
                                              accum_out=row["count"][:, j:j + 1]))
                        halve.wait()
                        halve.step(scalar(at["enough"], at["count"], kth[:, 0:1], None, ALU.is_ge))
                        halve.step(scalar(at["short"], at["count"], kth[:, 0:1], None, ALU.is_lt))
                        halve.wait()
                        for into, where in (("lo", "enough"), ("hi", "short")):
                            dve.sem_inc(go, 1)
                            halve.step(nc.vector.copy_predicated(at[into], at[where], at["mid"]))
                    halve.n = start + HALVINGS * HALVING_STEPS
                    halve.wait()
                    halve.step(copy(at["thr"], at["lo"]))
                    halve.wait()
                for j in range(GT):
                    t = g * GT + j
                    step(scalar(bias[:, TRI[t]:TRI[t + 1]], scores[:, j, 0:(t + 1) * P], row["thr"][:, j:j + 1], NEG,
                                ALU.is_lt, ALU.mult))
                wait()
                for j in range(GT):
                    t = g * GT + j
                    diag = bias[:, TRI[t + 1] - P:TRI[t + 1]]
                    step(tensor(diag, diag, const["causal"][:], ALU.min))
                wait()
                for j in range(GT):
                    t = g * GT + j
                    step(nc.vector.tensor_reduce(top[:, t:t + 1], bias[:, TRI[t]:TRI[t + 1]], AX.X, ALU.max))
                wait()
                rows = slice(g * GT, (g + 1) * GT)
                step(scalar(empty[:, rows], top[:, rows], 0.5 * NEG, None, ALU.is_lt))
                step(scalar(filled[:, rows], top[:, rows], 0.5 * NEG, None, ALU.is_ge))


def prepare_a(nc, arg, x, xT, bank, const, keys, k_hi, k_lo, w_all, w_out, mean_c, rope):
    with Phase(nc, "pa") as phase:
        sb, sem = phase.sb, phase.sem

        wq_n = sb("wq_n", [P, HA, D])
        w_uk = sb("w_uk", [P, HA, RANK])
        w_uv = sb("w_uv", [P, HA, RANK])
        wo = sb("wo", [P, HA, D])
        w_dkv = sb("w_dkv", [P, KC, RANK + DR])
        norm_w = sb("norm_w", [P, RANK])
        cos = sb("cos", [P, NT, HALF])
        sin = sb("sin", [P, NT, HALF])
        raw = sb("raw", [P, NT, P])
        sq = sb("sq", [P, NT, RANK])
        ss = sb("ss", [P, NT])
        rms = sb("rms", [P, NT])
        tmp = [sb(f"tmp{n}", [P, NT, HALF]) for n in range(4)]
        weights_in = sem("weights_in")
        x_in = sem("x_in")
        dkv_in = sem("dkv_in")
        tables_in = sem("tables_in")
        kv_done = sem("kv_done")
        kv_stored = sem("kv_stored")
        absorbed = sem("absorbed")
        absorbed_stored = sem("absorbed_stored")
        dve_step = sem("dve_step")
        ss_ready = sem("ss_ready")
        rms_ready = sem("rms_ready")
        keys_ready = sem("keys_ready")
        turned = sem("turned")
        hi_done = sem("hi_done")
        lo_done = sem("lo_done")
        mean_done = sem("mean_done")
        pool_step = sem("pool_step")

        with nc.Block() as block:
            @block.sync
            def _(sp):
                sp.dma_start(w_dkv[:], arg["W_dkv"].rearrange("(c p) n -> p c n", p=P)).then_inc(dkv_in, 16)
                sp.dma_start(norm_w[:], arg["kv_norm_w"].partition_broadcast(P)).then_inc(tables_in, 16)
                sp.dma_start(cos[:], arg["cos_k"]).then_inc(tables_in, 16)
                sp.dma_start(sin[:], arg["sin_k"]).then_inc(tables_in, 16)
                sp.dma_start(wq_n[:], arg["Wq_nope_T"]).then_inc(weights_in, 16)
                sp.dma_start(w_uk[:], arg["W_uk_T"]).then_inc(weights_in, 16)
                sp.dma_start(w_uv[:], arg["W_uv_T"]).then_inc(weights_in, 16)
                sp.dma_start(wo[:], arg["Wo"]).then_inc(weights_in, 16)
                for c in range(KC):
                    sp.dma_start(w_all[:, c, :, RANK:], arg["Wq"][c * P:(c + 1) * P, :].rearrange(
                        "p (h d) -> p h d", h=HA)[:, :, DN:]).then_inc(weights_in, 16)
                sp.dma_start(rope[:, 0], arg["cos_q"]).then_inc(weights_in, 16)
                sp.dma_start(rope[:, 1], arg["sin_q"]).then_inc(weights_in, 16)
                sp.dma_start(x[:], arg["hidden"].rearrange("(t p) d -> p t d", p=P)).then_inc(x_in, 16)
                sp.wait_ge(weights_in, 8 * 16)
                sp.wait_ge(x_in, 16)

            @block.tensor
            def _(pe):
                pe.wait_ge(dkv_in, 16)
                for t in range(NT):
                    for k in range(KC):
                        last = nc.tensor.matmul(bank[t // 4][:, t % 4 * P:(t % 4 + 1) * P], xT[:, k, t * P:(t + 1) * P],
                                                w_dkv[:, k, :], start=k == 0, stop=k == KC - 1)
                    if t % 4 == 3:
                        last.then_inc(kv_done, 1)
                pe.wait_ge(weights_in, 8 * 16)
                for n in range(HA * KC):
                    h, c = n // KC, n % KC
                    last = nc.tensor.matmul(bank[4 + n // 8][:, n % 8 * RANK:(n % 8 + 1) * RANK],
                                            wq_n[:, h, c * P:(c + 1) * P], w_uk[:, h, :], start=True, stop=True)
                    if n % 8 == 7:
                        last.then_inc(absorbed, 1)
                for n in range(HA // 2):
                    if n % 2 == 0:
                        pe.wait_ge(absorbed_stored, n // 2 + 1)
                    for j in range(2):
                        last = nc.tensor.matmul(bank[4 + n // 2][j * RANK:(j + 1) * RANK, n % 2 * D:(n % 2 + 1) * D],
                                                w_uv[:, 2 * n + j, :], wo[:, 2 * n + j, :], start=True, stop=True)
                    if n % 2 == 1:
                        last.then_inc(absorbed, 1)
                pe.wait_ge(keys_ready, 1)
                for t in range(NT):
                    last = nc.tensor.transpose(bank[t // 4][:, t % 4 * P:(t % 4 + 1) * P], keys[:, t, :], const["ident"][:])
                    if t % 4 == 3:
                        last.then_inc(turned, 1)
                pe.wait_ge(absorbed_stored, 8)
                for t in range(NT):
                    last = nc.tensor.matmul(bank[4][:, 0:RANK], const["mean"][:], keys[:, t, 0:RANK],
                                            start=t == 0, stop=t == NT - 1)
                last.then_inc(mean_done, 1)

            @block.scalar
            def _(act):
                for n in range(4):
                    act.wait_ge(kv_done, n + 1)
                    nc.scalar.activation(raw[:, 4 * n:4 * n + 4, :], bank[n][:].rearrange("p (t n) -> p t n", t=4),
                                         ACT.Copy).then_inc(kv_stored, 1)
                act.wait_ge(ss_ready, 1)
                nc.scalar.activation(rms[:], ss[:], ACT.Sqrt).then_inc(rms_ready, 1)
                for n in range(4):
                    act.wait_ge(absorbed, n + 1)
                    for c in range(KC):
                        last = nc.scalar.activation(
                            w_all[:, c, 4 * n:4 * n + 4, 0:RANK],
                            bank[4 + n][:].rearrange("p (h c r) -> p c h r", c=KC, r=RANK)[:, c], ACT.Copy, scale=SCALE_A)
                    last.then_inc(absorbed_stored, 1)
                for n in range(4):
                    act.wait_ge(absorbed, 4 + n + 1)
                    nc.scalar.activation(w_out[:, 2 * n:2 * n + 2, :], bank[4 + n][:].rearrange("p (a n) -> p a n", a=2),
                                         ACT.Copy).then_inc(absorbed_stored, 1)
                for n in range(4):
                    act.wait_ge(turned, n + 1)
                    nc.scalar.activation(k_hi[:, n * CH:(n + 1) * CH], bank[n][:], ACT.Copy).then_inc(hi_done, 1)
                act.wait_ge(mean_done, 1)
                nc.scalar.activation(mean_c[:], bank[4][:, 0:RANK], ACT.Copy)

            @block.vector
            def _(dve):
                chain = Chain(dve, dve_step)
                dve.wait_ge(kv_stored, 4)
                dve.wait_ge(tables_in, 3 * 16)
                chain.step(nc.vector.tensor_tensor(sq[:], raw[:, :, 0:RANK], raw[:, :, 0:RANK], ALU.mult))
                chain.wait()
                chain.step(nc.vector.tensor_reduce(ss[:], sq[:], AX.X, ALU.add))
                chain.wait()
                nc.vector.tensor_scalar(ss[:], ss[:], 1.0 / RANK, RMS_EPS, ALU.mult, ALU.add).then_inc(ss_ready, 1)
                r1, r2 = raw[:, :, RANK:RANK + HALF], raw[:, :, RANK + HALF:]
                chain.step(nc.vector.tensor_tensor(tmp[0][:], r1, cos[:], ALU.mult))
                chain.step(nc.vector.tensor_tensor(tmp[1][:], r2, sin[:], ALU.mult))
                chain.step(nc.vector.tensor_tensor(tmp[2][:], r2, cos[:], ALU.mult))
                chain.step(nc.vector.tensor_tensor(tmp[3][:], r1, sin[:], ALU.mult))
                chain.wait()
                chain.step(nc.vector.tensor_tensor(keys[:, :, RANK:RANK + HALF], tmp[0][:], tmp[1][:], ALU.subtract))
                chain.step(nc.vector.tensor_tensor(keys[:, :, RANK + HALF:], tmp[2][:], tmp[3][:], ALU.add))
                dve.wait_ge(rms_ready, 1)
                chain.step(nc.vector.reciprocal(rms[:], rms[:]))
                chain.wait()
                chain.step(nc.vector.tensor_tensor(sq[:], raw[:, :, 0:RANK],
                                                   rms[:].unsqueeze(2).to_broadcast([P, NT, RANK]), ALU.mult))
                chain.wait()
                nc.vector.tensor_tensor(keys[:, :, 0:RANK], sq[:],
                                        norm_w[:].unsqueeze(1).to_broadcast([P, NT, RANK]), ALU.mult).then_inc(keys_ready, 1)
                for n in range(4):
                    dve.wait_ge(hi_done, n + 1)
                    part = slice(n * CH, (n + 1) * CH)
                    nc.vector.tensor_tensor(k_lo[:, part], bank[n][:], k_hi[:, part].bitcast(F32),
                                            ALU.subtract).then_inc(lo_done, 1)


def attention(nc, tag, x, bank, const, k_hi, k_lo, dv, values, bias_of, w_out, latent=None, plain=None):
    H = HA
    OUT = H * dv
    OC = OUT // P
    with Phase(nc, tag) as phase:
        sb, sem = phase.sb, phase.sem

        score_bank, prob_bank, out_bank = bank[0:4], bank[4:6], bank[6:8]
        prob = [sb(f"prob{p}", [P, S]) for p in range(2)]
        prob_t = [sb(f"prob_t{p}", [P, S]) for p in range(2)]
        q_one = [sb(f"q_one{p}", [P, P]) for p in range(2)]
        q_hi = [sb(f"q_hi{p}", [P, P], F32R) for p in range(2)]
        q_lo = [sb(f"q_lo{p}", [P, P], F32R) for p in range(2)]
        chunk_max = [sb(f"chunk_max{p}", [P, NCH]) for p in range(2)]
        neg_max = [sb(f"neg_max{p}", [P, 1]) for p in range(2)]
        total = [sb(f"total{p}", [P, 1]) for p in range(2)]
        inv = [sb(f"inv{p}", [P, 1]) for p in range(2)]
        o = sb("o", [P, OUT])
        o_t = sb("o_t", [P, OC, P])
        if latent:
            q_nat = sb("q_nat", [P, H, P])
            q_t = sb("q_t", [P, H * P])
            fill = sb("fill", [P, RANK])
            tmp = [sb(f"tmp{n}", [P, H, HALF]) for n in range(4)]

        q_staged = sem("q_staged")
        pool_step = sem("pool_step")
        pool_go = sem("pool_go")
        scores_ready = sem("scores_ready")
        evac_go = sem("evac_go")
        scores_out = sem("scores_out")
        max_ready = sem("max_ready")
        exp_done = sem("exp_done")
        turned = sem("turned")
        prob_out = sem("prob_out")
        pv_done = sem("pv_done")
        norm_step = sem("norm_step")
        o_ready = sem("o_ready")
        fill_ready = sem("fill_ready")
        o_turned = sem("o_turned")
        o_t_ready = sem("o_t_ready")
        out_done = sem("out_done")
        x_done = sem("x_done")
        q_proj = sem("q_proj")
        q_nat_ready = sem("q_nat_ready")
        roped = sem("roped")
        q_turned = sem("q_turned")
        q_t_ready = sem("q_t_ready")
        NS = 2 if latent else 1
        OB = (OC + 3) // 4

        def head(i, p):
            return i + p * (H // 2)

        with nc.Block() as block:
            @block.gpsimd
            def _(pool):
                steps = 1 if latent else 2

                def rope_queries(t):
                    pool.wait_ge(q_nat_ready, 4 * (t + 1))
                    cos = latent["rope"][:, 0, t, :].unsqueeze(1).to_broadcast([P, H, HALF])
                    sin = latent["rope"][:, 1, t, :].unsqueeze(1).to_broadcast([P, H, HALF])
                    r1, r2 = q_nat[:, :, RANK:RANK + HALF], q_nat[:, :, RANK + HALF:]
                    for n, (r, table) in enumerate(((r1, cos), (r2, sin), (r2, cos), (r1, sin))):
                        nc.gpsimd.tensor_tensor(tmp[n][:], r, table, ALU.mult).then_inc(roped, 1)
                    pool.wait_ge(roped, 6 * t + 4)
                    nc.gpsimd.tensor_tensor(r1, tmp[0][:], tmp[1][:], ALU.subtract).then_inc(roped, 1)
                    nc.gpsimd.tensor_tensor(r2, tmp[2][:], tmp[3][:], ALU.add).then_inc(roped, 1)

                def stage(t, i, p):
                    s = i * 2 + p
                    n = s + H * t
                    pool.sem_inc(pool_go, 1)
                    if latent:
                        one = q_t[:, bass.ds(head(i, p) * P, P)]
                    else:
                        one = q_one[p][:]
                        rows = plain["rows"][:, bass.ds(i, 1)].to_broadcast([P, P])
                        nc.gpsimd.tensor_tensor(one, plain["q"][:, p, t * P:(t + 1) * P], rows,
                                                ALU.mult).then_inc(pool_step, 1)
                        pool.wait_ge(pool_step, n * steps + 1)
                        pool.sem_inc(pool_go, 1)
                    nc.gpsimd.tensor_copy(q_hi[p][:], one).then_inc(pool_step, 1)
                    pool.wait_ge(pool_step, n * steps + steps)
                    pool.sem_inc(pool_go, 1)
                    nc.gpsimd.tensor_tensor(q_lo[p][:], one, q_hi[p][:].bitcast(F32), ALU.subtract).then_inc(q_staged, 1)

                if latent:
                    rope_queries(0)
                for t in range(NT):
                    if latent:
                        pool.wait_ge(q_t_ready, 4 * (t + 1))
                    for p in range(2):
                        if t:
                            pool.wait_ge(scores_ready, BASE[t])
                        stage(t, 0, p)
                    with pool.Fori(1, H // 2) as i:
                        for p in range(2):
                            pool.wait_ge(scores_ready, (i * 2 + p - 1) * CHUNKS[t] + BASE[t])
                            stage(t, i, p)
                    if latent and t + 1 < NT:
                        rope_queries(t + 1)

            @block.tensor
            def _(pe):
                pe.sem_inc(pv_done, 2)

                def project_queries(t):
                    for n in range(4):
                        for k in range(KC):
                            last = nc.tensor.matmul(score_bank[n][:], latent["xT"][:, k, t * P:(t + 1) * P],
                                                    latent["w"][:, k, 4 * n:4 * n + 4, :].rearrange("p h d -> p (h d)"),
                                                    start=k == 0, stop=k == KC - 1)
                        last.then_inc(q_proj, 1)

                def turn_queries(t):
                    pe.wait_ge(roped, 6 * (t + 1))
                    for h in range(H):
                        last = nc.tensor.transpose(score_bank[h // 4][:, h % 4 * P:(h % 4 + 1) * P], q_nat[:, h, :],
                                                   const["ident"][:])
                        if h % 4 == 3:
                            last.then_inc(q_turned, 1)

                def scores(t, i, p):
                    s = i * 2 + p
                    nch = CHUNKS[t]
                    pe.wait_ge(q_staged, s + H * t + 1)
                    for c in range(nch):
                        w = min(CH, (t + 1) * P - c * CH)
                        if nch <= 2:
                            pe.wait_ge(scores_out, s * nch + BASE[t] - 2 * nch + c + 1 + 4)
                            b = score_bank[2 * p + c]
                        else:
                            pe.wait_ge(scores_out, s * nch + BASE[t] - nch + c + 1 + 4)
                            b = score_bank[c]
                        cols = slice(c * CH, c * CH + w)
                        kh, kl = (k_hi[:, cols], k_lo[:, cols]) if latent else (k_hi[:, p, cols], k_lo[:, p, cols])
                        nc.tensor.matmul(b[:, 0:w], q_hi[p][:], kh, start=True, stop=False)
                        nc.tensor.matmul(b[:, 0:w], q_lo[p][:], kh, start=False, stop=False)
                        nc.tensor.matmul(b[:, 0:w], q_hi[p][:], kl, start=False, stop=True).then_inc(scores_ready, 1)

                def apply(t, i, p):
                    s = i * 2 + p
                    nch = CHUNKS[t]
                    pe.wait_ge(exp_done, s + H * t + 1)
                    for g in range(nch):
                        n = s * nch + BASE[t] + g
                        b = prob_bank[(p * nch + g + BASE[t]) % 2]
                        pe.wait_ge(prob_out, n + 1)
                        for j in range(4 * g, min(4 * g + 4, t + 1)):
                            last = nc.tensor.transpose(b[:, j % 4 * P:(j % 4 + 1) * P], prob[p][:, j * P:(j + 1) * P],
                                                       const["ident"][:])
                        last.then_inc(turned, 1)
                    pe.wait_ge(o_ready, s + H * t + 1)
                    for j in range(t + 1):
                        if j % 4 == 0:
                            pe.wait_ge(prob_out, s * nch + BASE[t] + j // 4 + 1 + 2)
                        last = nc.tensor.matmul(out_bank[p][:, 0:dv], prob_t[p][:, j * P:(j + 1) * P],
                                                values(j, head(i, p)), start=j == 0, stop=j == t)
                    last.then_inc(pv_done, 1)

                if latent:
                    project_queries(0)
                    turn_queries(0)
                for t in range(NT):
                    if latent and t + 1 < NT:
                        pe.wait_ge(q_t_ready, 4 * (t + 1))
                        project_queries(t + 1)
                        pe.wait_ge(q_nat_ready, 4 * (t + 2))
                    elif latent:
                        pe.wait_ge(q_t_ready, 4 * (t + 1))
                    pe.wait_ge(scores_out, BASE[t] + 4)
                    if t:
                        pe.wait_ge(x_done, t)
                    scores(t, 0, 0)
                    with pe.Fori(0, H // 2 - 1) as i:
                        scores(t, i, 1)
                        apply(t, i, 0)
                        scores(t, i + 1, 0)
                        apply(t, i, 1)
                    scores(t, H // 2 - 1, 1)
                    apply(t, H // 2 - 1, 0)
                    apply(t, H // 2 - 1, 1)
                    pe.wait_ge(o_ready, H * (t + 1) + 2)
                    for c in range(OC):
                        last = nc.tensor.transpose(score_bank[c // 4][:, c % 4 * P:(c % 4 + 1) * P],
                                                   o[:, c * P:(c + 1) * P], const["ident"][:])
                    last.then_inc(o_turned, 1)
                    pe.wait_ge(o_t_ready, OB * (t + 1))
                    for c in range(OC):
                        last = nc.tensor.matmul(score_bank[3][:, 0:D], o_t[:, c, :], w_out[:, c, :],
                                                start=c == 0, stop=c == OC - 1)
                    last.then_inc(out_done, 1)
                    if latent and t + 1 < NT:
                        pe.wait_ge(o_t_ready, OB * (t + 1))
                        pe.wait_ge(x_done, t + 1)
                        turn_queries(t + 1)

            @block.scalar
            def _(act):
                act.sem_inc(prob_out, 2)

                def store_projected(t):
                    for n in range(4):
                        act.wait_ge(q_proj, 4 * t + n + 1)
                        if t:
                            act.wait_ge(q_turned, 4 * t)
                        nc.scalar.activation(q_nat[:, 4 * n:4 * n + 4, :],
                                             score_bank[n][:].rearrange("p (h d) -> p h d", h=4),
                                             ACT.Copy).then_inc(q_nat_ready, 1)

                def store_turned(t):
                    if t:
                        act.wait_ge(q_staged, H * t)
                    for n in range(4):
                        act.wait_ge(q_turned, 4 * t + n + 1)
                        nc.scalar.activation(q_t[:, n * CH:(n + 1) * CH], score_bank[n][:],
                                             ACT.Copy).then_inc(q_t_ready, 1)

                def softmax_head(t, i, p):
                    s = i * 2 + p
                    L, nch = (t + 1) * P, CHUNKS[t]
                    act.wait_ge(max_ready, s + H * t + 1)
                    nc.scalar.activation(prob[p][:, 0:L], prob[p][:, 0:L], ACT.Exp, bias=neg_max[p][:, 0:1],
                                         accum_out=total[p][:, 0:1]).then_inc(exp_done, 1)
                    act.wait_ge(pv_done, s + H * t + 1)
                    for g in range(nch):
                        w = min(CH, L - g * CH)
                        act.wait_ge(turned, s * nch + BASE[t] + g + 1)
                        b = prob_bank[(p * nch + g + BASE[t]) % 2]
                        nc.scalar.activation(prob_t[p][:, g * CH:g * CH + w], b[:, 0:w], ACT.Copy).then_inc(prob_out, 1)

                if latent:
                    store_projected(0)
                    store_turned(0)
                for t in range(NT):
                    if latent and t + 1 < NT:
                        store_projected(t + 1)
                    with act.Fori(0, H // 2) as i:
                        for p in range(2):
                            softmax_head(t, i, p)
                    act.wait_ge(o_turned, t + 1)
                    if t:
                        act.wait_ge(out_done, t)
                    for n in range(OB):
                        cols = slice(4 * n, min(4 * n + 4, OC))
                        k = cols.stop - cols.start
                        nc.scalar.activation(o_t[:, cols, :], score_bank[n][:, 0:k * P].rearrange("p (c n) -> p c n", c=k),
                                             ACT.Copy).then_inc(o_t_ready, 1)
                    if latent and t + 1 < NT:
                        store_turned(t + 1)

            @block.vector
            def _(dve):
                dve.sem_inc(scores_out, 4)
                dve.sem_inc(o_ready, 2)

                def take_scores(t, i, p):
                    s = i * 2 + p
                    nch = CHUNKS[t]
                    for c in range(nch):
                        w = min(CH, (t + 1) * P - c * CH)
                        b = score_bank[2 * p + c] if nch <= 2 else score_bank[c]
                        if c == 0:
                            if isinstance(i, int) and i == 0:
                                if t:
                                    dve.wait_ge(turned, BASE[t])
                            else:
                                dve.wait_ge(turned, (s - 1) * nch + BASE[t])
                        dve.wait_ge(scores_ready, s * nch + BASE[t] + c + 1)
                        dve.sem_inc(evac_go, 1)
                        nc.vector.tensor_tensor_reduce(prob[p][:, c * CH:c * CH + w], b[:, 0:w], bias_of(t, c * CH, w),
                                                       1.0, -BIG, ALU.add, ALU.max,
                                                       chunk_max[p][:, c:c + 1]).then_inc(scores_out, 1)
                    dve.wait_ge(scores_out, (s + 1) * nch + BASE[t] + 4)
                    nc.vector.tensor_reduce(neg_max[p][:], chunk_max[p][:, 0:nch], AX.X, ALU.max,
                                            negate=True).then_inc(max_ready, 1)

                def normalise(t, i, p):
                    s = i * 2 + p
                    n = s + H * t
                    dve.wait_ge(exp_done, n + 1)
                    dve.wait_ge(o_ready, n + 1)
                    nc.vector.reciprocal(inv[p][:], total[p][:]).then_inc(norm_step, 1)
                    dve.wait_ge(norm_step, n * NS + 1)
                    into = o[:, bass.ds(head(i, p) * dv, dv)]
                    if latent:
                        nc.vector.tensor_tensor(inv[p][:], inv[p][:], latent["filled"][:, t:t + 1],
                                                ALU.mult).then_inc(norm_step, 1)
                        dve.wait_ge(norm_step, n * NS + 2)
                        dve.wait_ge(pv_done, n + 3)
                        nc.vector.scalar_tensor_tensor(out=into, in0=out_bank[p][:, 0:dv], scalar=inv[p][:, 0:1],
                                                       in1=fill[:], op0=ALU.mult, op1=ALU.add).then_inc(o_ready, 1)
                    else:
                        dve.wait_ge(pv_done, n + 3)
                        nc.vector.tensor_scalar(into, out_bank[p][:, 0:dv], inv[p][:, 0:1], None,
                                                ALU.mult).then_inc(o_ready, 1)

                for t in range(NT):
                    if t:
                        dve.wait_ge(o_turned, t)
                    if latent:
                        if t:
                            dve.wait_ge(o_ready, H * t + 2)
                        nc.vector.tensor_scalar(fill[:], latent["mean_c"][:], latent["empty"][:, t:t + 1], None,
                                                ALU.mult).then_inc(fill_ready, 1)
                        dve.wait_ge(fill_ready, t + 1)
                    take_scores(t, 0, 0)
                    if t == 0:
                        pass
                    take_scores(t, 0, 1)
                    normalise(t, 0, 0)
                    take_scores(t, 1, 0)
                    normalise(t, 0, 1)
                    with dve.Fori(1, H // 2 - 1) as i:
                        take_scores(t, i, 1)
                        normalise(t, i, 0)
                        take_scores(t, i + 1, 0)
                        normalise(t, i, 1)
                    take_scores(t, H // 2 - 1, 1)
                    normalise(t, H // 2 - 1, 0)
                    normalise(t, H // 2 - 1, 1)
                    dve.wait_ge(out_done, t + 1)
                    nc.vector.tensor_tensor(x[:, t, :], x[:, t, :], score_bank[3][:, 0:D], ALU.add).then_inc(x_done, 1)


def prepare_b(nc, arg, xT, bank, stash, values):
    with Phase(nc, "pb") as phase:
        sb, sem = phase.sb, phase.sem
        w_dkv = sb("w_dkv", [P, KC, KVB])
        w_q = sb("w_q", [P, KC, D])
        w_uk = sb("w_uk", [P, D])
        w_uv = sb("w_uv", [P, D])
        c_kv = sb("c_kv", [P, S])
        part = {name: sb(name, [P, KC, S], F32R) for name in ("q_hi", "q_lo", "k_hi", "k_lo")}
        loaded = sem("loaded")
        done = sem("done")
        stored = sem("stored")
        lo_done = sem("lo_done")
        stashed = sem("stashed")
        ones_done = sem("ones_done")
        RING = 4
        FIRST_Q, FIRST_K, FIRST_V, ALL = NCH, NCH + KC * NCH, NCH + 2 * KC * NCH, NCH + 2 * KC * NCH + NT // 2
        with nc.Block() as block:
            @block.sync
            def _(sp):
                sp.dma_start(w_dkv[:], arg["b_dkv_T"].rearrange("(c p) n -> p c n", p=P)).then_inc(loaded, 16)
                sp.dma_start(w_q[:], arg["b_q_T"].rearrange("(c p) n -> p c n", p=P)).then_inc(loaded, 16)
                sp.dma_start(w_uk[:], arg["b_uk_T"]).then_inc(loaded, 16)
                sp.dma_start(w_uv[:], arg["b_uv_T"]).then_inc(loaded, 16)
                for n in range(2 * KC):
                    name, m = "qk"[n // KC], n % KC
                    sp.wait_ge(lo_done, NCH * (n + 1))
                    for which in ("_hi", "_lo"):
                        sp.dma_start(stash[name + which][m * P:(m + 1) * P, :], part[name + which][:, m, :].bitcast(F32)).then_inc(stashed, 16)
                sp.wait_ge(stashed, 2 * 2 * KC * 16)

            @block.gpsimd
            def _(pool):
                nc.gpsimd.memset(values[:, :, :, DHB:], 1.0).then_inc(ones_done, 1)

            @block.tensor
            def _(pe):
                pe.wait_ge(loaded, 4 * 16)
                for n in range(ALL):
                    if n >= RING:
                        pe.wait_ge(stored, n - RING + 1)
                    if FIRST_Q <= n - RING < FIRST_V:
                        pe.wait_ge(lo_done, n - RING - FIRST_Q + 1)
                    out = bank[n % RING]
                    if n < FIRST_Q:
                        for k in range(KC):
                            last = nc.tensor.matmul(out[:], w_dkv[:, k, :], xT[:, k, n * CH:(n + 1) * CH],
                                                    start=k == 0, stop=k == KC - 1)
                    elif n < FIRST_K:
                        m, c = divmod(n - FIRST_Q, NCH)
                        for k in range(KC):
                            last = nc.tensor.matmul(out[:], w_q[:, k, m * P:(m + 1) * P], xT[:, k, c * CH:(c + 1) * CH],
                                                    start=k == 0, stop=k == KC - 1)
                    elif n < FIRST_V:
                        m, c = divmod(n - FIRST_K, NCH)
                        pe.wait_ge(stored, NCH)
                        last = nc.tensor.matmul(out[:], w_uk[:, m * P:(m + 1) * P], c_kv[:, c * CH:(c + 1) * CH],
                                                start=True, stop=True)
                    else:
                        for j in range(2):
                            t = 2 * (n - FIRST_V) + j
                            last = nc.tensor.matmul(out[:, j * D:(j + 1) * D], c_kv[:, t * P:(t + 1) * P], w_uv[:],
                                                    start=True, stop=True)
                    last.then_inc(done, 1)

            @block.scalar
            def _(act):
                for n in range(ALL):
                    act.wait_ge(done, n + 1)
                    have = bank[n % RING][:]
                    if n < FIRST_Q:
                        into, scale = c_kv[:, n * CH:(n + 1) * CH], 1.0
                    elif n < FIRST_V:
                        m, c = divmod((n - FIRST_Q) % (KC * NCH), NCH)
                        name, scale = ("q_hi", SCALE_B) if n < FIRST_K else ("k_hi", 1.0)
                        into = part[name][:, m, c * CH:(c + 1) * CH]
                    else:
                        t = 2 * (n - FIRST_V)
                        into, scale = values[:, :, t:t + 2, 0:DHB].rearrange("p h t d -> p t h d"), 1.0
                        have = have.rearrange("p (t h d) -> p t h d", t=2, d=DHB)
                    nc.scalar.activation(into, have, ACT.Copy, scale=scale).then_inc(stored, 1)

            @block.vector
            def _(dve):
                for n in range(FIRST_Q, FIRST_V):
                    m, c = divmod((n - FIRST_Q) % (KC * NCH), NCH)
                    name, scale = ("q", SCALE_B) if n < FIRST_K else ("k", 1.0)
                    dve.wait_ge(stored, n + 1)
                    cols = slice(c * CH, (c + 1) * CH)
                    nc.vector.scalar_tensor_tensor(out=part[name + "_lo"][:, m, cols], in0=bank[n % RING][:], scalar=scale,
                                                   in1=part[name + "_hi"][:, m, cols].bitcast(F32),
                                                   op0=ALU.mult, op1=ALU.subtract).then_inc(lo_done, 1)


def attention_b(nc, arg, x, xT, bank2, bank, const, stash, max_rows, values):
    NB = 4
    with Phase(nc, "ab") as phase:
        sb, sem = phase.sb, phase.sem
        q_stack = [sb(f"q_stack{p}", [P, S], F32R) for p in range(NB)]
        k_stack = [sb(f"k_stack{p}", [P, S], F32R) for p in range(NB)]
        after_wide = sb("after_wide", [P, 2, P])
        after = sb("after", [P, 2, P], BF16)
        ident16 = sb("ident16", [P, P], BF16)
        alibi = xT[:, 0, :]
        w_out = sb("w_out", [P, KC, D])
        part_max = [sb(f"part_max{p}", [P, 2, NT]) for p in range(2)]
        row_max = [sb(f"row_max{p}", [P, NT]) for p in range(2)]
        neg_max = [sb(f"neg_max{p}", [NT, P], F32R) for p in range(2)]
        prob = [sb(f"prob{n}", [P, CH]) for n in range(4)]
        v_stack = [sb(f"v_stack{p}", [P, NT, DHB + 1]) for p in range(NB)]
        o_rows = [sb(f"o_rows{p}", [P, CH]) for p in range(2)]
        o_sums = sb("o_sums", [P, NT, HB, DHB + 1])
        inv = [sb(f"inv{p}", [P, HB, 1]) for p in range(2)]
        o = [sb(f"o{p}", [P, D]) for p in range(2)]
        o_t = [sb(f"o_t{p}", [P, KC, P]) for p in range(2)]
        consts_in = sem("consts_in")
        stacks_set = sem("stacks_set")
        after_set = sem("after_set")
        staged = [sem(f"staged{p}") for p in range(NB)]
        s_ready = sem("s_ready")
        s_used = sem("s_used")
        max_ready = sem("max_ready")
        max_out = sem("max_out")
        max_in = sem("max_in")
        t_ready = sem("t_ready")
        t_taken = sem("t_taken")
        pv_done = sem("pv_done")
        kept = sem("kept")
        act_go = sem("act_go")
        buffers_set = sem("buffers_set")
        inv_done = sem("inv_done")
        o_done = sem("o_done")
        o_turned = sem("o_turned")
        o_t_done = sem("o_t_done")
        out_done = sem("out_done")
        x_done = sem("x_done")

        s_bank, t_bank, o_bank = bank2, bank[4:6], bank[6:8]
        S_UNITS = [(t, 2 * CH * n, min(2 * CH, (t + 1) * P - 2 * CH * n))
                   for t in reversed(range(NT)) for n in range((t + 8) // 8)]
        T_UNITS = [(c, kb, max(c * CH, kb * P), (c + 1) * CH - max(c * CH, kb * P))
                   for c in range(NCH) for kb in range(4 * (c + 1))]
        NSU, NTU = len(S_UNITS), len(T_UNITS)
        AHEAD = 6
        ENDS = [sum(4 * (k + 1) for k in range(c + 1)) for c in range(NCH)]
        SLOTS = NTU + 1 + NCH

        def order(h):
            todo = [n % NSU for n in range(AHEAD, AHEAD + NSU) if h + 1 + n // NSU < HB]
            columns = sum(S_UNITS[n][2] for n in todo)
            steps, sent, turn_at = [], 0, None
            for n in range(NTU + 2):
                if n < NTU:
                    steps.append(("t", n))
                while len(todo) > (2 if h + 2 < HB else 0) and sent < columns * (n + 1) / (NTU + 2):
                    one = todo.pop(0)
                    sent += S_UNITS[one][2]
                    steps.append(("s", one))
                    if one == NSU - 1:
                        turn_at = n + 3
                if n == turn_at:
                    steps.append(("turn",))
                if n >= 2:
                    steps.append(("weigh", n - 2))
                if n - 4 in ENDS[:-1]:
                    steps.append(("flip", ENDS.index(n - 4)))
            if turn_at is not None and turn_at >= NTU + 2:
                steps.append(("turn",))
            return steps + [("s", n) for n in todo] + [("flip", NCH - 1)]

        def slots(steps):
            return {what: n for n, what in enumerate(w for w in steps if w[0] in ("t", "turn", "flip"))}

        USUAL = order(0)
        TURN = slots(USUAL)[("turn",)]

        with nc.Block() as block:
            @block.sync
            def _(sp):
                sp.dma_start(after_wide[:], arg["b_after"]).then_inc(consts_in, 16)
                sp.dma_start(w_out[:], arg["b_o_T"].rearrange("(c p) n -> p c n", p=P)).then_inc(consts_in, 16)

                def stage(h, b):
                    rows = slice(h * DHB, (h + 1) * DHB) if isinstance(h, int) else bass.ds(h * DHB, DHB)
                    for stack, first, name in ((q_stack, 0, "q_hi"), (q_stack, R_LO, "q_lo"), (q_stack, R_HI2, "q_hi"),
                                               (k_stack, 0, "k_hi"), (k_stack, R_LO, "k_hi"), (k_stack, R_HI2, "k_lo")):
                        sp.dma_start(stack[b][first:first + DHB, :].bitcast(F32), stash[name][rows, :]).then_inc(staged[b], 16)
                    sp.dma_start(v_stack[b][:], values[:, h if isinstance(h, int) else bass.ds(h, 1), :, :]).then_inc(staged[b], 16)

                def send_max(h, slot, b):
                    sp.wait_ge(t_taken, slot + 1 + 2)
                    sp.dma_start(max_rows, neg_max[b % 2][:].bitcast(F32)).then_inc(max_out, 16)
                    sp.wait_ge(max_out, h * 16 + 16)
                    sp.dma_start(q_stack[b][R_MAX:R_MAX + 1, :].bitcast(F32),
                                 max_rows.rearrange("t q -> (t q)").unsqueeze(0)).then_inc(max_in, 16)
                    sp.wait_ge(max_in, h * 16 + 16)

                sp.dma_start(alibi[R_HI2:R_MAX, :], arg["b_alibi"].partition_broadcast(R_MAX - R_HI2)).then_inc(consts_in, 16)
                sp.wait_ge(stacks_set, 5 * NB)
                for h in range(NB):
                    stage(h, h)
                send_max(0, 0, 0)
                with sp.Fori(0, HB // NB - 1) as i:
                    for b in range(NB):
                        h = i * NB + b
                        send_max(h + 1, h * SLOTS + 1 + TURN, (b + 1) % NB)
                        sp.wait_ge(pv_done, (h + 1) * NTU + 4)
                        stage(h + NB, b)
                for h in range(HB - NB, HB - 1):
                    send_max(h + 1, h * SLOTS + 1 + slots(order(h))[("turn",)], (h + 1) % NB)

            @block.tensor
            def _(pe):
                pe.sem_inc(pv_done, 4)

                def s_piece(h, b, n, turn):
                    t, k0, w = S_UNITS[n]
                    if n == 0:
                        pe.wait_ge(staged[b], turn * 7 * 16 + 7 * 16)
                    pe.wait_ge(s_used, h * NSU + n + 1)
                    for c in range(0, w, CH):
                        cw = min(CH, w - c)
                        diag = k0 + c + cw == (t + 1) * P
                        if diag:
                            nc.tensor.matmul(s_bank[n % 2][:, c + cw - P:c + cw], ident16[:], after[:, 0, :],
                                             start=True, stop=False, skip_group_check=True)
                        last = nc.tensor.matmul(s_bank[n % 2][:, c:c + cw], q_stack[b][0:R_MAX, t * P:(t + 1) * P],
                                                k_stack[b][0:R_MAX, k0 + c:k0 + c + cw], start=not diag, stop=True,
                                                skip_group_check=True)
                    last.then_inc(s_ready, 1)

                def turn_max(h, b, slot, bank_of):
                    pe.wait_ge(max_ready, h + 1)
                    pe.wait_ge(t_taken, slot + 1)
                    nc.tensor.transpose(bank_of[0:NT, 0:P], row_max[b % 2][:], const["ident"][:]).then_inc(t_ready, 1)

                def t_piece(h, b, n, slot, bank_of):
                    c, kb, q0, w = T_UNITS[n]
                    if n == 0:
                        pe.wait_ge(max_in, h * 16 + 16)
                    pe.wait_ge(t_taken, slot + 1)
                    diag = kb >= 4 * c
                    if diag:
                        nc.tensor.matmul(bank_of[:, 0:P], ident16[:], after[:, 1, :], start=True, stop=False,
                                         skip_group_check=True)
                    last = nc.tensor.matmul(bank_of[:, 0:w], k_stack[b][0:R_MAX + 1, kb * P:(kb + 1) * P],
                                            q_stack[b][0:R_MAX + 1, q0:q0 + w], start=not diag, stop=True,
                                            skip_group_check=True)
                    last.then_inc(t_ready, 1)

                def weigh(h, b, n, slot):
                    c, kb, q0, w = T_UNITS[n]
                    pe.wait_ge(t_taken, slot + 1 + 2)
                    if kb == 0:
                        pe.wait_ge(kept, h * NCH + c + 1)
                    at = q0 - c * CH
                    parts = [(0, P, True), (P, w, False)] if kb >= 4 * c else [(0, w, False)]
                    for first, end, stop in parts:
                        if first < end:
                            last = nc.tensor.matmul(o_bank[c % 2][0:DHB + 1, at + first:at + end], v_stack[b][:, kb, :],
                                                    prob[n % 4][:, first:end], start=kb == 0 and first == 0, stop=stop,
                                                    skip_group_check=True)
                    last.then_inc(pv_done, 1)

                def flip(h, c, slot, bank_of):
                    pe.wait_ge(kept, h * NCH + c + 3)
                    pe.wait_ge(t_taken, slot + 1)
                    for j in range(CH // P):
                        last = nc.tensor.transpose(bank_of[:, j * P:(j + 1) * P], o_rows[c % 2][:, j * P:(j + 1) * P],
                                                   const["ident"][:])
                    last.then_inc(t_ready, 1)

                def step(h, b, turn, steps):
                    place = slots(steps)
                    later = 1
                    for what in steps:
                        slot = h * SLOTS + 1 + place.get(what, 0)
                        if what[0] == "s":
                            if what[1] == 0:
                                later = 2
                            s_piece(h + later, (b + later) % NB, what[1], turn + (b + later) // NB)
                        elif what[0] == "t":
                            t_piece(h, b, what[1], slot, t_bank[(1 + b + place[what]) % 2])
                        elif what[0] == "turn":
                            turn_max(h + 1, b + 1, slot, t_bank[(1 + b + place[what]) % 2])
                        elif what[0] == "flip":
                            flip(h, what[1], slot, t_bank[(1 + b + place[what]) % 2])
                        else:
                            weigh(h, b, what[1], h * SLOTS + 1 + place[("t", what[1])])

                def out_tile(t):
                    pe.wait_ge(o_t_done, t + 1)
                    for c in range(KC):
                        last = nc.tensor.matmul(o_bank[t % 2][:, 0:D], o_t[t % 2][:, c, :], w_out[:, c, :],
                                                start=c == 0, stop=c == KC - 1)
                    last.then_inc(out_done, 1)

                pe.wait_ge(after_set, 2)
                for n in range(NSU):
                    s_piece(0, 0, n, 0)
                turn_max(0, 0, 0, t_bank[0])
                for n in range(AHEAD):
                    s_piece(1, 1, n, 0)
                with pe.Fori(0, HB // NB - 1) as i:
                    for b in range(NB):
                        step(i * NB + b, b, i, USUAL)
                for h in range(HB - NB, HB):
                    step(h, h % NB, h // NB, order(h))
                pe.wait_ge(t_taken, HB * SLOTS + 2)
                for t in range(NT):
                    p = t % 2
                    pe.wait_ge(o_done, t + 1)
                    if t >= 2:
                        pe.wait_ge(x_done, t - 1)
                    for c in range(KC):
                        last = nc.tensor.transpose(t_bank[p][:, c * P:(c + 1) * P], o[p][:, c * P:(c + 1) * P],
                                                   const["ident"][:])
                    last.then_inc(o_turned, 1)
                    if t:
                        out_tile(t - 1)
                out_tile(NT - 1)

            @block.scalar
            def _(act):
                act.sem_inc(t_taken, 2)
                act.sem_inc(kept, 2)
                act.wait_ge(consts_in, 3 * 16)
                act.wait_ge(buffers_set, 4)
                for b in range(NB):
                    nc.scalar.activation(k_stack[b][R_HI2:R_MAX, :], alibi[R_HI2:R_MAX, :], ACT.Copy).then_inc(stacks_set, 1)

                def negate(b, slot, bank_of):
                    act.wait_ge(t_ready, slot + 1)
                    nc.scalar.activation(neg_max[b % 2][:], bank_of[0:NT, 0:P], ACT.Copy, scale=-1.0).then_inc(t_taken, 1)

                def step(h, b, steps):
                    place = slots(steps)
                    for what in steps:
                        slot, bank_of = h * SLOTS + 1 + place.get(what, 0), t_bank[(1 + b + place.get(what, 0)) % 2]
                        if what[0] == "turn":
                            negate(b + 1, slot, bank_of)
                        elif what[0] == "flip":
                            act.wait_ge(t_ready, slot + 1)
                            act.sem_inc(act_go, 1)
                            nc.scalar.activation(o_sums[:, 4 * what[1]:4 * what[1] + 4, h if isinstance(h, int) else bass.ds(h, 1), :],
                                                 bank_of[:].rearrange("p (j d) -> p j d", d=P)[:, :, 0:DHB + 1],
                                                 ACT.Copy).then_inc(t_taken, 1)
                        elif what[0] == "weigh":
                            if what[1] + 1 in ENDS:
                                c = ENDS.index(what[1] + 1)
                                act.wait_ge(pv_done, h * NTU + ENDS[c] + 4)
                                nc.scalar.activation(o_rows[c % 2][0:DHB + 1, :], o_bank[c % 2][0:DHB + 1, :], ACT.Copy).then_inc(kept, 1)
                        elif what[0] == "t":
                            n = what[1]
                            w = T_UNITS[n][3]
                            act.wait_ge(t_ready, slot + 1)
                            act.wait_ge(pv_done, h * NTU + n + 1)
                            nc.scalar.activation(prob[n % 4][:, 0:w], bank_of[:, 0:w], ACT.Exp).then_inc(t_taken, 1)

                negate(0, 0, t_bank[0])
                with act.Fori(0, HB // NB - 1) as i:
                    for b in range(NB):
                        step(i * NB + b, b, USUAL)
                for h in range(HB - NB, HB):
                    step(h, h % NB, order(h))
                for t in range(NT):
                    act.wait_ge(o_turned, t + 1)
                    if t >= 2:
                        act.wait_ge(out_done, t - 1)
                    nc.scalar.activation(o_t[t % 2][:], t_bank[t % 2][:, 0:D].rearrange("p (c n) -> p c n", c=KC),
                                         ACT.Copy).then_inc(o_t_done, 1)

            @block.vector
            def _(dve):
                for b in range(NB):
                    nc.vector.memset(q_stack[b][0:R_HI2, :].bitcast(F32), 0.0).then_inc(stacks_set, 1)
                    nc.vector.memset(q_stack[b][R_HI2:, :].bitcast(F32), 1.0).then_inc(stacks_set, 1)
                    nc.vector.memset(k_stack[b][0:R_HI2, :].bitcast(F32), 0.0).then_inc(stacks_set, 1)
                    nc.vector.memset(k_stack[b][R_MAX:, :].bitcast(F32), 1.0).then_inc(stacks_set, 1)
                dve.wait_ge(consts_in, 3 * 16)
                nc.vector.tensor_copy(after[:], after_wide[:]).then_inc(after_set, 1)
                nc.vector.tensor_copy(ident16[:], const["ident"][:]).then_inc(after_set, 1)
                for p in range(2):
                    nc.vector.memset(part_max[p][:], -BIG).then_inc(buffers_set, 1)
                    nc.vector.memset(o_rows[p][:], 0.0).then_inc(buffers_set, 1)
                dve.wait_ge(buffers_set, 4)
                dve.sem_inc(s_used, 2)

                def maxima(h, b, first, last):
                    for n in range(first, last):
                        t, k0, w = S_UNITS[n]
                        dve.wait_ge(s_ready, h * NSU + n + 1)
                        nc.vector.tensor_reduce(part_max[b % 2][:, k0 // (2 * CH), t:t + 1], s_bank[n % 2][:, 0:w],
                                                AX.X, ALU.max).then_inc(s_used, 1)
                    if last == NSU:
                        dve.wait_ge(s_used, h * NSU + NSU + 2)
                        nc.vector.tensor_tensor(row_max[b % 2][:], part_max[b % 2][:, 0, :], part_max[b % 2][:, 1, :],
                                                ALU.max).then_inc(max_ready, 1)

                def step(h, b, steps):
                    later = 1
                    for what in steps:
                        if what[0] == "s":
                            if what[1] == 0:
                                later = 2
                            maxima(h + later, b + later, what[1], what[1] + 1)

                maxima(0, 0, 0, NSU)
                maxima(1, 1, 0, AHEAD)
                with dve.Fori(0, HB // NB - 1) as i:
                    for b in range(NB):
                        step(i * NB + b, b, USUAL)
                for h in range(HB - NB, HB):
                    step(h, h % NB, order(h))
                dve.wait_ge(t_taken, HB * SLOTS + 1 + 2 - 1)
                for t in range(NT + 2):
                    p = t % 2
                    if t < NT:
                        nc.vector.reciprocal(inv[p][:], o_sums[:, t, :, DHB:]).then_inc(inv_done, 1)
                    if t >= 2:
                        dve.wait_ge(out_done, t - 1)
                        nc.vector.tensor_tensor(x[:, t - 2, :], x[:, t - 2, :], o_bank[p][:, 0:D], ALU.add).then_inc(x_done, 1)
                    if t < NT:
                        dve.wait_ge(inv_done, t + 1)
                        nc.vector.tensor_tensor(o[p][:].rearrange("p (h d) -> p h d", d=DHB), o_sums[:, t, :, 0:DHB],
                                                inv[p][:].to_broadcast([P, HB, DHB]), ALU.mult).then_inc(o_done, 1)


def experts(nc, tag, arg, x, xT, bank, w13, w2, load, store=None):
    with Phase(nc, tag) as phase:
        sb, sem = phase.sb, phase.sem

        gate_w = sb("gate_w", [P, KC, E])
        prior = sb("prior", [P, E])
        gates = sb("gates", [P, NT, EE])
        gate_in = sem("gate_in")
        gates_done = sem("gates_done")
        loaded = sem("loaded")

        with Phase(nc, tag + "g") as inner:
            sbi, semi = inner.sb, inner.sem

            top = sbi("top", [P, NT])
            prob = sbi("prob", [P, NT, E])
            biased = sbi("biased", [P, NT, E])
            better = sbi("better", [P, E, NT, E])
            rank = sbi("rank", [P, NT, E])
            logits_done = semi("logits_done")
            dve_step = semi("dve_step")
            shifted = semi("shifted")
            exp_done = semi("exp_done")
            with nc.Block() as block:
                @block.sync
                def _(sp):
                    sp.dma_start(gate_w[:], arg["gate_w"].rearrange("(c p) e -> p c e", p=P)).then_inc(gate_in, 16)
                    sp.dma_start(prior[:], arg["expert_bias"].partition_broadcast(P)).then_inc(gate_in, 16)
                    if load:
                        for c in range(KC):
                            rows = slice(c * P, (c + 1) * P)
                            for n, (routed, shared) in enumerate((("w1", "sw1"), ("w3", "sw3"))):
                                cols = slice(n * HID, (n + 1) * HID)
                                sp.dma_start(w13[:, c, 0:E, cols],
                                             arg[routed][:, rows, :].rearrange("e p f -> p e f")).then_inc(loaded, 16)
                                sp.dma_start(w13[:, c, E, cols], arg[shared][rows, :]).then_inc(loaded, 16)
                        for c in range(2):
                            rows = slice(c * HH, (c + 1) * HH)
                            sp.dma_start(w2[:, c, 0:E, :],
                                         arg["w2"][:, rows, :].rearrange("e p f -> p e f")).then_inc(loaded, 16)
                            sp.dma_start(w2[:, c, E, :], arg["sw2"][rows, :]).then_inc(loaded, 16)
                        sp.wait_ge(loaded, 12 * 16)

                @block.tensor
                def _(pe):
                    pe.wait_ge(gate_in, 2 * 16)
                    for t in range(NT):
                        for k in range(KC):
                            last = nc.tensor.matmul(bank[7][:, t * E:(t + 1) * E], xT[:, k, t * P:(t + 1) * P],
                                                    gate_w[:, k, :], start=k == 0, stop=k == KC - 1)
                    last.then_inc(logits_done, 1)

                @block.scalar
                def _(act):
                    act.wait_ge(shifted, 1)
                    nc.scalar.activation(prob[:], prob[:], ACT.Exp).then_inc(exp_done, 1)

                @block.vector
                def _(dve):
                    chain = Chain(dve, dve_step)
                    logits = bank[7][:, 0:NT * E].rearrange("p (t e) -> p t e", e=E)
                    wide = [P, NT, E]
                    chain.step(nc.vector.memset(gates[:, :, E], 1.0))
                    dve.wait_ge(logits_done, 1)
                    chain.step(nc.vector.tensor_reduce(top[:], logits, AX.X, ALU.max))
                    chain.wait()
                    nc.vector.tensor_tensor(prob[:], logits, top[:].unsqueeze(2).to_broadcast(wide),
                                            ALU.subtract).then_inc(shifted, 1)
                    dve.wait_ge(exp_done, 1)
                    chain.step(nc.vector.tensor_reduce(top[:], prob[:], AX.X, ALU.add))
                    chain.wait()
                    chain.step(nc.vector.reciprocal(top[:], top[:]))
                    chain.wait()
                    chain.step(nc.vector.tensor_tensor(prob[:], prob[:], top[:].unsqueeze(2).to_broadcast(wide), ALU.mult))
                    chain.wait()
                    chain.step(nc.vector.tensor_tensor(biased[:], prob[:], prior[:].unsqueeze(1).to_broadcast(wide), ALU.add))
                    chain.wait()
                    for e in range(E):
                        one = biased[:, :, e:e + 1]
                        n = e + 1
                        chain.step(nc.vector.tensor_tensor(better[:, e, :, 0:n], one.to_broadcast([P, NT, n]),
                                                           biased[:, :, 0:n], ALU.is_gt))
                        if n < E:
                            chain.step(nc.vector.tensor_tensor(better[:, e, :, n:E], one.to_broadcast([P, NT, E - n]),
                                                               biased[:, :, n:E], ALU.is_ge))
                    chain.wait()
                    chain.step(nc.vector.tensor_reduce(rank[:], better[:].rearrange("p e t f -> p t f e"), AX.X, ALU.add))
                    chain.wait()
                    nc.vector.scalar_tensor_tensor(out=gates[:, :, 0:E], in0=rank[:], scalar=float(TOPK), in1=prob[:],
                                                   op0=ALU.is_lt, op1=ALU.mult).then_inc(gates_done, 1)

        xs = [sb(f"xs{p}", [P, KC, P]) for p in range(2)]
        silu = [sb(f"silu{p}", [P, HID]) for p in range(2)]
        h = [sb(f"h{p}", [P, HID]) for p in range(2)]
        h_t = [sb(f"h_t{p}", [HH, 2, P]) for p in range(2)]
        staged = sem("staged")
        pool_go = sem("pool_go")
        up_done = sem("up_done")
        silu_done = sem("silu_done")
        h_done = sem("h_done")
        turned = sem("turned")
        h_t_done = sem("h_t_done")
        down_done = sem("down_done")
        x_done = sem("x_done")
        written = sem("written")
        up_bank, turn_bank, y_bank = bank[0:3], bank[3:5], bank[5:7]
        M = 2 * EE
        with nc.Block() as block:
            @block.gpsimd
            def _(pool):
                with pool.Fori(0, NT // 2) as i:
                    for p in range(2):
                        t = i * 2 + p
                        pool.wait_ge(up_done, (t + 1) * EE)
                        pool.sem_inc(pool_go, 1)
                        nc.gpsimd.tensor_copy(xs[p][:], xT[:, :, bass.ds(t * P, P)]).then_inc(staged, 1)

            @block.tensor
            def _(pe):
                pe.sem_inc(up_done, M)
                pe.sem_inc(turned, 2)
                with pe.Fori(0, NT // 2) as i:
                    for m in range(M + 2):
                        if m < M:
                            p, e = m // EE, m % EE
                            n = i * M + m
                            if e == 0:
                                pe.wait_ge(staged, i * 2 + p + 1)
                            pe.wait_ge(h_done, n + 1)
                            for k in range(KC):
                                last = nc.tensor.matmul(up_bank[m % 3][:, 0:2 * HID], xs[p][:, k, :], w13[:, k, e, :],
                                                        start=k == 0, stop=k == KC - 1)
                            last.then_inc(up_done, 1)
                        if 1 <= m <= M:
                            n = i * M + m - 1
                            j = (m - 1) % 2
                            pe.wait_ge(h_done, n + 4)
                            pe.wait_ge(h_t_done, n + 1)
                            for c in range(2):
                                last = nc.tensor.transpose(turn_bank[j][0:HH, c * P:(c + 1) * P],
                                                           h[j][:, c * HH:(c + 1) * HH], arg["ident_sb"][:])
                            last.then_inc(turned, 1)
                        if m >= 2:
                            p, e = (m - 2) // EE, (m - 2) % EE
                            n = i * M + m - 2
                            j = m % 2
                            pe.wait_ge(h_t_done, n + 3)
                            if e == 0:
                                pe.wait_ge(x_done, i * 2 + p + 1)
                            for c in range(2):
                                last = nc.tensor.matmul(y_bank[p][:, 0:D], h_t[j][:, c, :], w2[:, c, e, :],
                                                        start=e == 0 and c == 0, stop=e == EE - 1 and c == 1)
                            last.then_inc(down_done, 1)

            @block.scalar
            def _(act):
                act.sem_inc(h_t_done, 2)
                with act.Fori(0, NT // 2) as i:
                    for m in range(M + 1):
                        if m < M:
                            p, e = m // EE, m % EE
                            n = i * M + m
                            act.wait_ge(up_done, n + 1 + M)
                            act.wait_ge(h_done, n + 2)
                            nc.scalar.activation(silu[m % 2][:], up_bank[m % 3][:, 0:HID], ACT.Silu,
                                                 scale=gates[:, i * 2 + p, e:e + 1]).then_inc(silu_done, 1)
                        if m:
                            n = i * M + m - 1
                            j = (m - 1) % 2
                            act.wait_ge(turned, n + 3)
                            act.wait_ge(down_done, n + 1)
                            nc.scalar.activation(h_t[j][:], turn_bank[j][0:HH, 0:2 * P].rearrange("p (c n) -> p c n", c=2),
                                                 ACT.Copy).then_inc(h_t_done, 1)

            @block.vector
            def _(dve):
                dve.sem_inc(h_done, 3)
                dve.sem_inc(down_done, 2)
                dve.sem_inc(x_done, 2)

                def add(i, p):
                    t = i * 2 + p
                    dve.wait_ge(down_done, t * EE + EE + 2)
                    nc.vector.tensor_tensor(x[:, t, :], x[:, t, :], y_bank[p][:, 0:D], ALU.add).then_inc(x_done, 1)

                with dve.Fori(0, NT // 2) as i:
                    for m in range(M):
                        p, e = m // EE, m % EE
                        n = i * M + m
                        dve.wait_ge(silu_done, n + 1)
                        dve.wait_ge(turned, n + 1)
                        nc.vector.scalar_tensor_tensor(out=h[m % 2][:], in0=up_bank[m % 3][:, HID:2 * HID],
                                                       scalar=gates[:, i * 2 + p, e:e + 1], in1=silu[m % 2][:],
                                                       op0=ALU.mult, op1=ALU.mult).then_inc(h_done, 1)
                        if m == EE + 3:
                            add(i, 0)
                    add(i, 1)

            @block.sync
            def _(sp):
                if store is not None:
                    with sp.Fori(0, NT) as t:
                        sp.wait_ge(x_done, t + 3)
                        sp.dma_start(store[bass.ds(t * P, P), :], x[:, t, :]).then_inc(written, 16)
                    sp.wait_ge(written, 16 * NT)


def program(nc, arg, out):
    with ExitStack() as ctx:
        def sb(name, shape, dt=F32, scope=None):
            return (scope or ctx).enter_context(nc.sbuf_tensor(name, shape, dt))

        psum = ctx.enter_context(nc.psum_tensor("psum", [P, 8 * CH], F32))
        bank = [psum[:, n * CH:(n + 1) * CH] for n in range(8)]
        pair = [psum[:, n * 2 * CH:(n + 1) * 2 * CH] for n in range(2)]
        x = sb("x", [P, NT, D])
        xT = sb("xT", [P, KC, S])
        const = {"ident": sb("ident", [P, P]), "causal": sb("causal", [P, P], BF16), "mean": sb("mean", [P, P])}
        causal_wide = sb("causal_wide", [P, P])
        arg["ident_sb"] = const["ident"]
        x_in = ctx.enter_context(nc.semaphore("x_in"))
        with nc.Block() as block:
            @block.sync
            def _(sp):
                sp.dma_start(x[:], arg["hidden"].rearrange("(t p) d -> p t d", p=P)).then_inc(x_in, 16)
                sp.dma_start(const["ident"][:], arg["ident"]).then_inc(x_in, 16)
                sp.dma_start(causal_wide[:], arg["causal"]).then_inc(x_in, 16)
                sp.wait_ge(x_in, 3 * 16)

            @block.vector
            def _(dve):
                nc.vector.memset(const["mean"][:], 1.0 / S)
                dve.wait_ge(x_in, 3 * 16)
                nc.vector.tensor_copy(const["causal"][:], causal_wide[:])

        layernorm(nc, "ln1", x, xT, bank, const["ident"])
        with ExitStack() as a:
            bias = sb("bias", [P, TRI[NT]], BF16, a)
            empty = sb("empty", [P, NT], F32, a)
            filled = sb("filled", [P, NT], F32, a)
            index_mask(nc, arg, x, xT, bank, const, bias, empty, filled)
            keys = sb("keys", [P, NT, P], F32, a)
            k_hi = sb("ka_hi", [P, S], F32R, a)
            k_lo = sb("ka_lo", [P, S], F32R, a)
            w_all = sb("w_all", [P, KC, HA, P], F32, a)
            w_out = sb("wa_out", [P, HA // 2, D], F32, a)
            mean_c = sb("mean_c", [P, RANK], F32, a)
            rope = sb("rope", [P, 2, NT, HALF], F32, a)
            prepare_a(nc, arg, x, xT, bank, const, keys, k_hi, k_lo, w_all, w_out, mean_c, rope)
            attention(nc, "aa", x, bank, const, k_hi, k_lo, RANK,
                      lambda j, h: keys[:, j, 0:RANK],
                      lambda t, c, w: bias[:, TRI[t] + c:TRI[t] + c + w],
                      w_out, latent={"xT": xT, "w": w_all, "rope": rope, "empty": empty, "filled": filled,
                                     "mean_c": mean_c})
        w13 = sb("w13", [P, KC, EE, 2 * HID])
        w2 = sb("w2", [HH, 2, EE, D])
        layernorm(nc, "ln2", x, xT, bank, const["ident"])
        experts(nc, "f1", arg, x, xT, bank, w13, w2, load=True)
        layernorm(nc, "ln3", x, xT, bank, const["ident"])
        stash = {name: nc.dram_tensor(f"stash_{name}", (D, S), F32, kind="Internal").ap()
                 for name in ("q_hi", "q_lo", "k_hi", "k_lo")}
        with ExitStack() as b:
            values = sb("values", [P, HB, NT, DHB + 1], F32, b)
            prepare_b(nc, arg, xT, bank, stash, values)
            max_rows = nc.dram_tensor("max_rows", (NT, P), F32, kind="Internal").ap()
            attention_b(nc, arg, x, xT, pair, bank, const, stash, max_rows, values)
        layernorm(nc, "ln4", x, xT, bank, const["ident"])
        experts(nc, "f2", arg, x, xT, bank, w13, w2, load=False, store=out)


def kernel(**inputs):
    import numpy as np
    import concourse.bacc as bacc
    from concourse.bass_utils import run_bass_kernel_spmd

    a = {k: np.asarray(v) for k, v in inputs.items()}
    A, B, M = "L0_attn_a_", "L0_attn_b_", "L0_ffn_"
    wq = a[A + "Wq"].reshape(D, HA, DN + DR)
    w_ukv = a[A + "W_ukv"].reshape(RANK, HA, DN + DV)
    lay = {
        "hidden": a[A + "hidden_states"].reshape(S, D),
        "Wq_idx": a[A + "Wq_idx"], "Wk_idx": a[A + "Wk_idx"],
        "bq_idx": a[A + "bq_idx"].reshape(HI, DI).T, "bk_idx": a[A + "bk_idx"].reshape(HI, DI).T,
        "idx_w": a[A + "idx_w"], "w_ctrl": a[A + "w_ctrl"].reshape(KC, P).T, "b_ctrl": a[A + "b_ctrl"].reshape(1),
        "Wq": a[A + "Wq"], "Wq_nope_T": wq[:, :, :DN].transpose(2, 1, 0),
        "W_uk_T": w_ukv[:, :, :DN].transpose(2, 1, 0), "W_uv_T": w_ukv[:, :, DN:].transpose(2, 1, 0),
        "Wo": a[A + "Wo"].reshape(HA, DV, D).transpose(1, 0, 2),
        "W_dkv": a[A + "W_dkv"], "kv_norm_w": a[A + "kv_norm_w"],
        "b_dkv_T": a[B + "w_dkv"].T, "b_q_T": a[B + "w_q"].T, "b_uk_T": a[B + "w_uk"].T,
        "b_uv_T": a[B + "w_uv"].T, "b_o_T": a[B + "w_o"].T,
        "gate_w": a[M + "gate_w"], "expert_bias": a[M + "expert_bias"],
        "w1": a[M + "w1"], "w2": a[M + "w2"], "w3": a[M + "w3"],
        "sw1": a[M + "sw1"], "sw2": a[M + "sw2"], "sw3": a[M + "sw3"],
    }
    inv_freq = (1.0 / 10000.0 ** (np.arange(0, DR, 2, dtype=np.float32) / DR)).astype(np.float32)
    angle = (np.arange(S, dtype=np.float32)[:, None] * inv_freq[None, :]).astype(np.float32)
    table = {"cos": np.cos(angle).astype(np.float32), "sin": np.sin(angle).astype(np.float32)}
    for name, value in table.items():
        tiles = value.reshape(NT, P, HALF).transpose(1, 0, 2)
        lay[name + "_k"] = tiles
        lay[name + "_q"] = (tiles * np.float32(SCALE_A)).astype(np.float32)
    row, col = np.arange(P)[:, None], np.arange(P)[None, :]
    lay["ident"] = np.eye(P, dtype=np.float32)
    lay["causal"] = np.where(col <= row, 0.0, NEG).astype(np.float32)
    lay["b_after"] = np.stack([np.where(col > row, HIDE, 0.0), np.where(row > col, HIDE, 0.0)], axis=1).astype(np.float32)
    lay["b_alibi"] = np.float32(SLOPE / (R_MAX - R_ALIBI)) * np.arange(S, dtype=np.float32)

    nc = bacc.Bacc("TRN2", target_bir_lowering=False, num_devices=1)
    arrays, arg = {}, {}
    for name, value in lay.items():
        value = np.ascontiguousarray(value)
        arrays[f"in_{name}"] = value
        arg[name] = nc.dram_tensor(f"in_{name}", value.shape, mybir.dt.from_np(value.dtype), kind="ExternalInput").ap()
    out = nc.dram_tensor("out", (S, D), F32, kind="ExternalOutput").ap()
    program(nc, arg, out)
    result = run_bass_kernel_spmd(nc, [arrays], core_ids=[0])
    return result.results[0]["out"].reshape(1, S, D)
```

```python
from contextlib import ExitStack

import concourse.bass as bass
from concourse import mybir

F32 = mybir.dt.float32
F32R = mybir.dt.float32r
BF16 = mybir.dt.bfloat16
U32 = mybir.dt.uint32
I32 = mybir.dt.int32
ALU = mybir.AluOpType
ACT = mybir.ActivationFunctionType
AX = mybir.AxisListType

P = 128
S = 2048
D = 256
NT = S // P
KC = D // P
CH = 512
NCH = S // CH
LN_EPS = 1e-5
NEG = -1.0e9

HA, DN, DR, DV, RANK = 16, 128, 64, 128, 64
HALF = DR // 2
HI, DI = 4, 64
RMS_EPS = 1e-6
GH = 4
LAG, FLIP_AT, SCORES_BY, Y_AT, PROJECT_AT = 3, 0.4, 0.75, (0.1, 0.3), 1 + 3e-6
SCALE_A = 1.0 / float(DN + DR) ** 0.5
HB = 16
DHB = D // HB
SLOPE = 0.0625
KVB = 128
SCALE_B = float(DHB) ** -0.5
R_LO, R_HI2, R_ALIBI, R_MAX = 32, 64, 80, 96
HIDE = -1.0e30
E, HID, TOPK = 8, 224, 2
EE = E + 1
HH = HID // 2

GT = 8
TOP = 8
PROBES = 7
PROBE_STEPS = GT // 2 + 1 + 2 + 4 + 8
NEAR, EDGE = 0.4, 0.002
HALVINGS = 64
HALVING_STEPS = 2 + GT + 2 + 2
BIG = 3.0e38
ROUND = 12582912.0

TRI = [t * (t + 1) // 2 * P for t in range(NT + 1)]


class Chain:

    def __init__(self, eng, sem):
        self.eng, self.sem, self.n = eng, sem, 0

    def step(self, ins):
        ins.then_inc(self.sem, 1)
        self.n += 1

    def wait(self, back=0):
        self.eng.wait_ge(self.sem, self.n - back if back else self.n)


class Phase(ExitStack):

    def __init__(self, nc, tag):
        super().__init__()
        self.nc, self.tag, self.used = nc, tag, []

    def sb(self, name, shape, dt=F32):
        return self.enter_context(self.nc.sbuf_tensor(f"{self.tag}_{name}", shape, dt))

    def sem(self, name):
        self.used.append(self.enter_context(self.nc.semaphore(f"{self.tag}_{name}")))
        return self.used[-1]

    def __exit__(self, kind, *rest):
        if kind is None:
            with self.nc.Block() as block:
                @block.gpsimd
                def _(pool):
                    for one in self.used:
                        pool.sem_clear(one)
        return super().__exit__(kind, *rest)


def layernorm(nc, tag, x, xT, bank, ident):
    with Phase(nc, tag) as phase:
        sb, sem = phase.sb, phase.sem

        stats = sb("stats", [P, NT, 6])
        mean = sb("mean", [P, NT])
        half = sb("half", [P, NT])
        var = sb("var", [P, NT])
        std = sb("std", [P, NT])
        rstd = sb("rstd", [P, NT])
        xn = [sb(f"xn{p}", [P, D]) for p in range(2)]
        stats_done = sem("stats_done")
        dve_step = sem("dve_step")
        var_ready = sem("var_ready")
        std_ready = sem("std_ready")
        xn_ready = sem("xn_ready")
        turned = sem("turned")
        stored = sem("stored")

        with nc.Block() as block:
            @block.vector
            def _(dve):
                with dve.Fori(0, NT) as t:
                    nc.vector.bn_stats(stats[:, t, :], x[:, t, :]).then_inc(stats_done, 1)
                dve.wait_ge(stats_done, NT)
                chain = Chain(dve, dve_step)
                chain.step(nc.vector.tensor_tensor(mean[:], stats[:, :, 1], stats[:, :, 4], ALU.add))
                chain.step(nc.vector.tensor_tensor(half[:], stats[:, :, 1], stats[:, :, 4], ALU.subtract))
                chain.step(nc.vector.tensor_tensor(var[:], stats[:, :, 2], stats[:, :, 5], ALU.add))
                chain.wait()
                chain.step(nc.vector.tensor_scalar(mean[:], mean[:], 0.5, None, ALU.mult))
                chain.step(nc.vector.tensor_scalar(half[:], half[:], 0.5, None, ALU.mult))
                chain.step(nc.vector.tensor_scalar(var[:], var[:], 1.0 / D, LN_EPS, ALU.mult, ALU.add))
                chain.wait()
                chain.step(nc.vector.tensor_tensor(half[:], half[:], half[:], ALU.mult))
                chain.wait()
                nc.vector.tensor_tensor(var[:], var[:], half[:], ALU.add).then_inc(var_ready, 1)
                dve.wait_ge(std_ready, 1)
                chain.step(nc.vector.reciprocal(rstd[:], std[:]))
                chain.wait()
                with dve.Fori(0, NT // 2) as i:
                    for p in range(2):
                        t = i * 2 + p
                        dve.wait_ge(turned, t + 1)
                        nc.vector.tensor_scalar(xn[p][:], x[:, t, :], mean[:, bass.ds(t, 1)], rstd[:, bass.ds(t, 1)],
                                                ALU.subtract, ALU.mult).then_inc(xn_ready, 1)

            @block.scalar
            def _(act):
                act.wait_ge(var_ready, 1)
                nc.scalar.activation(std[:], var[:], ACT.Sqrt).then_inc(std_ready, 1)
                act.sem_inc(stored, 2)
                with act.Fori(0, NT // 2) as i:
                    for p in range(2):
                        t = i * 2 + p
                        act.wait_ge(turned, t + 3)
                        nc.scalar.activation(xT[:, :, bass.ds(t * P, P)],
                                             bank[p][:, 0:D].rearrange("p (c n) -> p c n", c=KC),
                                             ACT.Copy).then_inc(stored, 1)

            @block.tensor
            def _(pe):
                pe.sem_inc(turned, 2)
                with pe.Fori(0, NT // 2) as i:
                    for p in range(2):
                        t = i * 2 + p
                        pe.wait_ge(xn_ready, t + 1)
                        pe.wait_ge(stored, t + 1)
                        for c in range(KC):
                            last = nc.tensor.transpose(bank[p][:, c * P:(c + 1) * P], xn[p][:, c * P:(c + 1) * P],
                                                       ident[:])
                        last.then_inc(turned, 1)


def index_mask(nc, arg, x, xT, bank, const, bias, empty, filled):
    with Phase(nc, "ix") as phase:
        sb, sem = phase.sb, phase.sem

        k_stack = sb("k_stack", [P, HI, S], F32R)
        k_lo = sb("k_lo", [P, HI // 2, S], F32R)
        q_stack = sb("q_stack", [P, HI, GT * P], F32R)
        kth = sb("kth", [P, 1])
        weight = sb("weight", [P, HI])
        w_q = sb("w_q", [P, KC, HI, 2, DI])
        b_q = sb("b_q", [P, HI])

        def high(h):
            return slice(h % 2 * DI, h % 2 * DI + DI)

        def low(h):
            return high(h + 1)

        with Phase(nc, "ixp") as inner:
            sbi, semi = inner.sb, inner.sem

            w_k = sbi("w_k", [P, KC, HI, 2, DI])
            b_k = sbi("b_k", [P, HI])
            ctrl = sbi("ctrl", [P, KC])
            ctrl_wide = sbi("ctrl_wide", [P, KC, P])
            bctrl = sbi("bctrl", [P, 1])
            pooled = sbi("pooled", [P, KC])
            z = sbi("z", [P, 1])
            ez = sbi("ez", [P, 1])
            loaded = semi("loaded")
            projected = semi("projected")
            high_done = semi("high_done")
            low_done = semi("low_done")
            pooled_ready = semi("pooled_ready")
            z_ready = semi("z_ready")
            zs_ready = semi("zs_ready")
            ez_ready = semi("ez_ready")
            dve_step = semi("dve_step")
            LOADS = 8 + 4 + 3
            with nc.Block() as block:
                @block.sync
                def _(sp):
                    for w, b, name in ((w_k, b_k, "k"), (w_q, b_q, "q")):
                        for half in range(2):
                            for c in range(KC):
                                sp.dma_start(w[:, c, :, half, :], arg[f"W{name}_idx"][c * P:(c + 1) * P, :].rearrange(
                                    "p (h d) -> p h d", h=HI)).then_inc(loaded, 16)
                    for half in range(2):
                        rows = slice(half * DI, half * DI + DI)
                        sp.dma_start(b_k[rows, :], arg["bk_idx"]).then_inc(loaded, 16)
                        sp.dma_start(b_q[rows, :], arg["bq_idx"]).then_inc(loaded, 16)
                    sp.dma_start(ctrl[:], arg["w_ctrl"]).then_inc(loaded, 16)
                    sp.dma_start(bctrl[:], arg["b_ctrl"].partition_broadcast(P)).then_inc(loaded, 16)
                    sp.dma_start(weight[:], arg["idx_w"].partition_broadcast(P)).then_inc(loaded, 16)
                    sp.wait_ge(loaded, LOADS * 16)

                @block.tensor
                def _(pe):
                    pe.wait_ge(loaded, LOADS * 16)
                    for n in range(HI * NCH):
                        h, c = divmod(n, NCH)
                        if n >= 4:
                            pe.wait_ge(low_done, n - 3)
                        for k in range(KC):
                            last = nc.tensor.matmul(bank[n % 4][:], w_k[:, k, h, :, :].rearrange("p a d -> p (a d)"),
                                                    xT[:, k, c * CH:(c + 1) * CH], start=k == 0, stop=k == KC - 1)
                        last.then_inc(projected, 1)
                    pe.wait_ge(pooled_ready, 1)
                    for k in range(KC):
                        last = nc.tensor.matmul(bank[4][:, 0:1], ctrl_wide[:, k, :], pooled[:, k:k + 1],
                                                start=k == 0, stop=k == KC - 1)
                    last.then_inc(z_ready, 1)

                @block.scalar
                def _(act):
                    act.wait_ge(loaded, LOADS * 16)
                    for n in range(HI * NCH):
                        h, c = divmod(n, NCH)
                        act.wait_ge(projected, n + 1)
                        nc.scalar.activation(k_stack[:, h, c * CH:(c + 1) * CH], bank[n % 4][:], ACT.Identity,
                                             bias=b_k[:, h:h + 1]).then_inc(high_done, 1)
                    act.wait_ge(zs_ready, 1)
                    nc.scalar.activation(ez[:], z[:], ACT.Exp, scale=-1.0).then_inc(ez_ready, 1)

                @block.vector
                def _(dve):
                    chain = Chain(dve, dve_step)
                    dve.wait_ge(loaded, LOADS * 16)
                    for k in range(KC):
                        chain.step(nc.vector.tensor_copy(ctrl_wide[:, k, :], ctrl[:, k:k + 1].to_broadcast([P, P])))
                    chain.wait()
                    nc.vector.tensor_reduce(pooled[:], xT[:], AX.X, ALU.add).then_inc(pooled_ready, 1)
                    for n in range(HI * NCH):
                        h, c = divmod(n, NCH)
                        rows, cols = high(h), slice(c * CH, (c + 1) * CH)
                        dve.wait_ge(high_done, n + 1)
                        nc.vector.scalar_tensor_tensor(out=k_lo[rows, h // 2, cols], in0=bank[n % 4][rows, :],
                                                       scalar=b_k[rows, h:h + 1], in1=k_stack[rows, h, cols].bitcast(F32),
                                                       op0=ALU.add, op1=ALU.subtract).then_inc(low_done, 1)
                    dve.wait_ge(z_ready, 1)
                    nc.vector.scalar_tensor_tensor(out=z[:], in0=bank[4][:, 0:1], scalar=1.0 / S, in1=bctrl[:],
                                                   op0=ALU.mult, op1=ALU.add).then_inc(zs_ready, 1)
                    dve.wait_ge(ez_ready, 1)
                    chain.step(nc.vector.tensor_scalar(ez[:], ez[:], 1.0, None, ALU.add))
                    chain.wait()
                    chain.step(nc.vector.reciprocal(ez[:], ez[:]))
                    chain.wait()
                    chain.step(nc.vector.tensor_scalar(ez[:], ez[:], float(S), None, ALU.mult))
                    chain.wait()
                    chain.step(nc.vector.tensor_scalar(ez[:], ez[:], ROUND, None, ALU.add))
                    chain.wait()
                    chain.step(nc.vector.tensor_scalar(ez[:], ez[:], ROUND, None, ALU.subtract))
                    chain.wait()
                    chain.step(nc.vector.tensor_scalar(kth[:], ez[:], 1.0, float(S), ALU.max, ALU.min))
                    chain.wait()

        scores = sb("scores", [P, GT, S])
        qs = [sb(f"qs{p}", [P, HI, P], F32R) for p in range(2)]
        spare = x[:].rearrange("p t d -> p (t d)")
        relu = spare[:, 0:2 * (HI - 1) * CH].rearrange("p (a h n) -> p a h n", a=2, h=HI - 1)
        masked = spare[:, 0:S]
        junk_act = spare[:, S:S + S // 2].bitcast(BF16)
        row = {name: sb(name, [P, GT]) for name in (
            "low", "high", "lo", "hi", "above", "at_least", "at_lo", "at_hi", "tiny", "zeros", "count", "signs", "nonzero",
            "part", "step", "mid", "neg_mid", "outside", "rank", "bad", "more", "thr")}
        flag = {name: sb(name, [P, GT], U32) for name in ("pos", "neg", "at_zero", "enough", "short")}
        aim = sb("aim", [P, 1])
        shift = sb("shift", [P, GT])
        places = sb("places", [P, TOP])
        best = sb("best", [P, GT, TOP])
        pick = sb("pick", [P, GT, TOP])
        bad_row = sb("bad_row", [P, 1])
        unsolved = sb("unsolved", [P, 1], I32)
        top = sb("top", [P, NT])
        for g in range(NT // GT):
            index_scores(nc, f"ixs{g}", g, xT, bank, w_q, b_q, q_stack, k_stack, k_lo, qs, relu, weight, scores, high, low)
            index_threshold(nc, f"ixt{g}", g, bank, const, scores, kth, masked, junk_act, row, flag, aim, shift,
                            places, best, pick, bad_row, unsolved, top, bias, empty, filled)


def index_scores(nc, tag, g, xT, bank, w_q, b_q, q_stack, k_stack, k_lo, qs, relu, weight, scores, high, low):
    with Phase(nc, tag) as phase:
        sem = phase.sem

        projected = sem("projected")
        high_done = sem("high_done")
        low_done = sem("low_done")
        staged = sem("staged")
        pool_go = sem("pool_go")
        dotted = sem("dotted")
        first_used = sem("first_used")
        relu_done = sem("relu_done")
        summed = sem("summed")
        QC = GT * P // CH
        with nc.Block() as block:
            @block.gpsimd
            def _(pool):
                pool.wait_ge(low_done, HI * QC)
                with pool.Fori(0, GT // 2) as i:
                    for p in range(2):
                        t = i * 2 + p
                        pool.wait_ge(dotted, (t + 1) * NCH * HI)
                        pool.sem_inc(pool_go, 1)
                        nc.gpsimd.tensor_copy(qs[p][:], q_stack[:, :, bass.ds(t * P, P)].bitcast(F32)).then_inc(staged, 1)

            @block.tensor
            def _(pe):
                pe.sem_inc(dotted, NCH * HI * 2)
                for n in range(HI * QC):
                    h, c = divmod(n, QC)
                    for k in range(KC):
                        last = nc.tensor.matmul(bank[n][:], w_q[:, k, h, :, :].rearrange("p a d -> p (a d)"),
                                                xT[:, k, g * GT * P + c * CH:g * GT * P + (c + 1) * CH],
                                                start=k == 0, stop=k == KC - 1)
                    last.then_inc(projected, 1)
                with pe.Fori(0, GT // 2) as i:
                    for p in range(2):
                        t = i * 2 + p
                        pe.wait_ge(staged, t + 1)
                        for c in range(NCH):
                            n = t * NCH + c
                            cols = slice(c * CH, (c + 1) * CH)
                            pe.wait_ge(first_used, n + 1)
                            pe.wait_ge(relu_done, n * (HI - 1) + 1 + HI - 2)
                            for h in range(HI):
                                out = bank[c % 2 * HI + h]
                                nc.tensor.matmul(out[:], qs[p][:, h, :], k_stack[:, h, cols], start=True, stop=False)
                                nc.tensor.matmul(out[:], qs[p][high(h), h, :], k_lo[high(h), h // 2, cols],
                                                 start=False, stop=True).then_inc(dotted, 1)

            @block.scalar
            def _(act):
                for n in range(HI * QC):
                    h, c = divmod(n, QC)
                    act.wait_ge(projected, n + 1)
                    nc.scalar.activation(q_stack[:, h, c * CH:(c + 1) * CH], bank[n][:], ACT.Identity,
                                         bias=b_q[:, h:h + 1]).then_inc(high_done, 1)
                act.sem_inc(relu_done, 2 * (HI - 1))
                with act.Fori(0, GT) as t:
                    for c in range(NCH):
                        n = t * NCH + c
                        act.wait_ge(summed, n * HI + HI)
                        for h in range(1, HI):
                            act.wait_ge(dotted, n * HI + h + 1 + NCH * HI * 2)
                            nc.scalar.activation(relu[:, c % 2, h - 1, :], bank[c % 2 * HI + h][:],
                                                 ACT.Relu).then_inc(relu_done, 1)

            @block.vector
            def _(dve):
                for n in range(HI * QC):
                    h, c = divmod(n, QC)
                    rows, cols = low(h), slice(c * CH, (c + 1) * CH)
                    dve.wait_ge(high_done, n + 1)
                    nc.vector.scalar_tensor_tensor(out=q_stack[rows, h, cols], in0=bank[n][rows, :],
                                                   scalar=b_q[rows, h:h + 1], in1=q_stack[rows, h, cols].bitcast(F32),
                                                   op0=ALU.add, op1=ALU.subtract).then_inc(low_done, 1)
                dve.sem_inc(first_used, 2)
                dve.sem_inc(summed, 2 * HI)
                with dve.Fori(0, GT) as t:
                    for c in range(NCH):
                        n = t * NCH + c
                        into = scores[:, t, c * CH:(c + 1) * CH]
                        dve.wait_ge(dotted, n * HI + 1 + NCH * HI * 2)
                        nc.vector.tensor_scalar(into, bank[c % 2 * HI][:], 0.0, weight[:, 0:1],
                                                ALU.max, ALU.mult).then_inc(first_used, 1)
                        dve.wait_ge(first_used, n + 3)
                        for h in range(1, HI):
                            dve.wait_ge(relu_done, n * (HI - 1) + h + 2 * (HI - 1))
                            if h > 1:
                                dve.wait_ge(summed, n * HI + h - 1 + 2 * HI)
                            last = nc.vector.scalar_tensor_tensor(
                                out=into, in0=relu[:, c % 2, h - 1, :], scalar=weight[:, h:h + 1], in1=into,
                                op0=ALU.mult, op1=ALU.add)
                            last.then_inc(summed, 1 if h < HI - 1 else 2)


def index_threshold(nc, tag, g, bank, const, scores, kth, masked, junk_act, row, flag, aim, shift, places, best, pick,
                    bad_row, unsolved, top, bias, empty, filled):
    own, other = slice(0, GT // 2), slice(GT // 2, GT)
    junk = [bias[:, TRI[g * GT] + p * S:TRI[g * GT] + (p + 1) * S] for p in range(2)]
    with Phase(nc, tag) as phase:
        sem = phase.sem

        dve_step = sem("dve_step")
        zero_step = sem("zero_step")
        mid_ready = sem("mid_ready")
        go = sem("go")
        sign_done = sem("sign_done")
        bad_ready = sem("bad_ready")
        summed = sem("summed")
        halved = sem("halved")
        with nc.Block() as block:
            @block.scalar
            def _(act):
                for j in range(GT):
                    if j:
                        act.wait_ge(zero_step, 2 * j)
                    nc.scalar.activation(junk_act, scores[:, j, :], ACT.Sign,
                                         accum_out=row["signs"][:, j:j + 1]).then_inc(zero_step, 1)
                    act.wait_ge(zero_step, 2 * j + 1)
                    nc.scalar.activation(junk_act, junk_act, ACT.Abs,
                                         accum_out=row["nonzero"][:, j:j + 1]).then_inc(zero_step, 1)
                act.wait_ge(zero_step, 2 * GT)
                with act.Fori(0, PROBES) as r:
                    act.wait_ge(mid_ready, r + 1)
                    for j in range(GT // 2, GT):
                        if j > GT // 2:
                            act.wait_ge(sign_done, r * (GT // 2) + j - GT // 2)
                        nc.scalar.activation(junk_act, scores[:, j, :], ACT.Sign, bias=row["neg_mid"][:, j:j + 1],
                                             accum_out=row["signs"][:, j:j + 1]).then_inc(sign_done, 1)

            @block.tensor
            def _(pe):
                pe.wait_ge(bad_ready, 1)
                nc.tensor.matmul(bank[7][:, 0:1], const["mean"][:], bad_row[:], start=True, stop=True).then_inc(summed, 1)

            @block.vector
            def _(dve):
                chain = Chain(dve, dve_step)
                step, wait = chain.step, chain.wait
                scalar, tensor, fill, copy = nc.vector.tensor_scalar, nc.vector.tensor_tensor, nc.vector.memset, nc.vector.tensor_copy
                at = {name: t[:] for name, t in {**row, **flag}.items()}

                def choose(into, where, value):
                    dve.sem_inc(go, 1)
                    step(nc.vector.copy_predicated(at[into], at[where], at[value]))

                def probe(first):
                    wait()
                    step(scalar(at["part"], at["at_lo"], aim[:, 0:1], None, ALU.subtract))
                    step(tensor(at["step"], at["at_lo"], at["at_hi"], ALU.subtract))
                    wait()
                    step(nc.vector.reciprocal(at["step"], at["step"]))
                    wait()
                    step(tensor(at["part"], at["part"], at["step"], ALU.mult))
                    wait()
                    if first:
                        step(scalar(at["part"], at["part"], NEAR, None, ALU.mult))
                        wait()
                        step(tensor(at["part"], at["part"], shift[:], ALU.add))
                        wait()
                    step(scalar(at["part"], at["part"], EDGE, 1.0 - EDGE, ALU.max, ALU.min))
                    step(tensor(at["step"], at["hi"], at["lo"], ALU.subtract))
                    wait()
                    step(tensor(at["step"], at["step"], at["part"], ALU.mult))
                    wait()
                    step(tensor(at["mid"], at["step"], at["lo"], ALU.add))
                    wait()
                    scalar(at["neg_mid"], at["mid"], -1.0, None, ALU.mult).then_inc(mid_ready, 1)

                step(nc.vector.tensor_reduce(at["low"], scores[:], AX.X, ALU.min))
                step(nc.vector.tensor_reduce(at["high"], scores[:], AX.X, ALU.max))
                step(fill(at["tiny"], 1.2e-38))
                step(fill(at["zeros"], 0.0))
                step(fill(at["at_lo"], float(S)))
                step(fill(at["at_hi"], 0.0))
                step(scalar(aim[:], kth[:], (TOP + 1) / 2.0, None, ALU.subtract))
                for n in range(TOP):
                    step(fill(places[:, n:n + 1], n + 1.0))
                wait()
                step(tensor(at["step"], at["high"], at["low"], ALU.subtract))
                wait()
                step(nc.vector.scalar_tensor_tensor(out=at["high"], in0=at["step"], scalar=2.0 ** -10, in1=at["high"],
                                                    op0=ALU.mult, op1=ALU.add))
                wait()
                step(scalar(at["high"], at["high"], 1e-30, None, ALU.add))
                dve.wait_ge(zero_step, 2 * GT)
                step(tensor(at["above"], at["nonzero"], at["signs"], ALU.add))
                step(tensor(at["at_least"], at["signs"], at["nonzero"], ALU.subtract))
                wait()
                step(scalar(at["above"], at["above"], 0.5, None, ALU.mult))
                step(scalar(at["at_least"], at["at_least"], 0.5, float(S), ALU.mult, ALU.add))
                step(copy(at["lo"], at["low"]))
                step(copy(at["hi"], at["high"]))
                wait()
                step(scalar(at["pos"], at["above"], kth[:, 0:1], None, ALU.is_ge))
                step(scalar(at["neg"], at["at_least"], kth[:, 0:1], None, ALU.is_lt))
                step(scalar(at["outside"], at["above"], kth[:, 0:1], None, ALU.is_ge))
                step(scalar(shift[:], at["at_least"], kth[:, 0:1], None, ALU.is_lt))
                wait()
                choose("lo", "pos", "tiny")
                choose("at_lo", "pos", "above")
                choose("hi", "neg", "zeros")
                choose("at_hi", "neg", "at_least")
                step(tensor(at["outside"], at["outside"], shift[:], ALU.add))
                wait()
                step(scalar(shift[:], shift[:], 1.0 - NEAR, None, ALU.mult))
                step(scalar(at["at_zero"], at["outside"], 0.5, None, ALU.is_lt))
                probe(first=True)
                before = chain.n
                with dve.Fori(0, PROBES) as r:
                    chain.n = r * PROBE_STEPS + before
                    dve.wait_ge(mid_ready, r + 1)
                    for j in range(GT // 2):
                        chain.wait(back=1 if j else 0)
                        step(scalar(junk[j % 2], scores[:, j, :], row["mid"][:, j:j + 1], 0.0, ALU.is_ge, ALU.add,
                                    accum_out=row["count"][:, j:j + 1]))
                    dve.wait_ge(sign_done, r * (GT // 2) + GT // 2)
                    step(scalar(row["count"][:, other], row["signs"][:, other], 0.5, S / 2.0, ALU.mult, ALU.add))
                    wait()
                    step(scalar(at["enough"], at["count"], kth[:, 0:1], None, ALU.is_ge))
                    step(scalar(at["short"], at["count"], kth[:, 0:1], None, ALU.is_lt))
                    wait()
                    choose("lo", "enough", "mid")
                    choose("at_lo", "enough", "count")
                    choose("hi", "short", "mid")
                    choose("at_hi", "short", "count")
                    probe(first=False)
                chain.n = before + PROBES * PROBE_STEPS
                wait()
                for j in range(GT):
                    if j < GT // 2:
                        step(scalar(junk[j % 2], scores[:, j, :], row["hi"][:, j:j + 1], None, ALU.is_ge))
                    else:
                        step(scalar(junk[j % 2], scores[:, j, :], row["hi"][:, j:j + 1], 0.0, ALU.is_ge, ALU.add,
                                    accum_out=row["at_hi"][:, j:j + 1]))
                    wait()
                    step(nc.vector.scalar_tensor_tensor(out=masked, in0=junk[j % 2], scalar=-BIG, in1=scores[:, j, :],
                                                        op0=ALU.mult, op1=ALU.add))
                    wait()
                    step(nc.vector.max(best[:, j, :], masked))
                wait()
                step(scalar(at["rank"], at["at_hi"], -1.0, kth[:, 0:1], ALU.mult, ALU.add))
                wait()
                wide = [P, GT, TOP]
                step(tensor(pick[:], places[:].unsqueeze(1).to_broadcast(wide), row["rank"][:].unsqueeze(2).to_broadcast(wide),
                            ALU.is_equal))
                step(scalar(at["bad"], at["rank"], TOP + 0.5, None, ALU.is_gt))
                step(scalar(at["more"], at["rank"], 0.5, None, ALU.is_lt))
                wait()
                step(tensor(pick[:], pick[:], best[:], ALU.mult))
                step(tensor(at["bad"], at["bad"], at["more"], ALU.add))
                wait()
                step(nc.vector.tensor_reduce(at["thr"], pick[:], AX.X, ALU.add))
                step(tensor(at["bad"], at["bad"], at["outside"], ALU.mult))
                wait()
                nc.vector.tensor_reduce(bad_row[:], at["bad"], AX.X, ALU.max).then_inc(bad_ready, 1)
                choose("thr", "at_zero", "zeros")
                dve.wait_ge(summed, 1)
                step(scalar(unsolved[:], bank[7][:, 0:1], 0.0, None, ALU.is_gt))
                wait()
                some = dve.value_load(unsolved[0:1, 0:1], min_val=0, max_val=1)
                with dve.If(some > 0):
                    halve = Chain(dve, halved)
                    halve.step(copy(at["lo"], at["low"]))
                    halve.step(copy(at["hi"], at["high"]))
                    start = halve.n
                    with dve.Fori(0, HALVINGS) as r:
                        halve.n = r * HALVING_STEPS + start
                        halve.wait()
                        halve.step(tensor(at["mid"], at["lo"], at["hi"], ALU.add))
                        halve.wait()
                        halve.step(scalar(at["mid"], at["mid"], 0.5, None, ALU.mult))
                        for j in range(GT):
                            halve.wait()
                            halve.step(scalar(junk[0], scores[:, j, :], row["mid"][:, j:j + 1], 0.0, ALU.is_ge, ALU.add,
                                              accum_out=row["count"][:, j:j + 1]))
                        halve.wait()
                        halve.step(scalar(at["enough"], at["count"], kth[:, 0:1], None, ALU.is_ge))
                        halve.step(scalar(at["short"], at["count"], kth[:, 0:1], None, ALU.is_lt))
                        halve.wait()
                        for into, where in (("lo", "enough"), ("hi", "short")):
                            dve.sem_inc(go, 1)
                            halve.step(nc.vector.copy_predicated(at[into], at[where], at["mid"]))
                    halve.n = start + HALVINGS * HALVING_STEPS
                    halve.wait()
                    halve.step(copy(at["thr"], at["lo"]))
                    halve.wait()
                for j in range(GT):
                    t = g * GT + j
                    step(scalar(bias[:, TRI[t]:TRI[t + 1]], scores[:, j, 0:(t + 1) * P], row["thr"][:, j:j + 1], NEG,
                                ALU.is_lt, ALU.mult))
                wait()
                for j in range(GT):
                    t = g * GT + j
                    diag = bias[:, TRI[t + 1] - P:TRI[t + 1]]
                    step(tensor(diag, diag, const["causal"][:], ALU.min))
                wait()
                for j in range(GT):
                    t = g * GT + j
                    step(nc.vector.tensor_reduce(top[:, t:t + 1], bias[:, TRI[t]:TRI[t + 1]], AX.X, ALU.max))
                wait()
                rows = slice(g * GT, (g + 1) * GT)
                step(scalar(empty[:, rows], top[:, rows], 0.5 * NEG, None, ALU.is_lt))
                step(scalar(filled[:, rows], top[:, rows], 0.5 * NEG, None, ALU.is_ge))


def prepare_a(nc, arg, x, xT, bank, const, k_hi, k_lo, c_stack, w_all, w_out, nowhere, rope, xT_rows):
    with Phase(nc, "pa") as phase:
        sb, sem = phase.sb, phase.sem

        wq_n = sb("wq_n", [P, HA, D])
        w_uk = sb("w_uk", [P, HA, RANK])
        w_uv = sb("w_uv", [P, HA, 2, RANK])
        keys = sb("keys", [P, NT, P])
        mean_c = sb("mean_c", [RANK, P])
        wo = sb("wo", [P, HA, D])
        w_dkv = sb("w_dkv", [P, KC, RANK + DR])
        norm_w = sb("norm_w", [P, RANK])
        cos = sb("cos", [P, NT, HALF])
        sin = sb("sin", [P, NT, HALF])
        raw = sb("raw", [P, NT, P])
        sq = sb("sq", [P, NT, RANK])
        ss = sb("ss", [P, NT])
        rms = sb("rms", [P, NT])
        tmp = [sb(f"tmp{n}", [P, NT, HALF]) for n in range(4)]
        weights_in = sem("weights_in")
        x_in = sem("x_in")
        dkv_in = sem("dkv_in")
        tables_in = sem("tables_in")
        kv_done = sem("kv_done")
        kv_stored = sem("kv_stored")
        absorbed = sem("absorbed")
        absorbed_stored = sem("absorbed_stored")
        dve_step = sem("dve_step")
        ss_ready = sem("ss_ready")
        rms_ready = sem("rms_ready")
        keys_ready = sem("keys_ready")
        turned = sem("turned")
        hi_done = sem("hi_done")
        c_done = sem("c_done")
        lo_done = sem("lo_done")
        mean_done = sem("mean_done")
        mean_stored = sem("mean_stored")
        pool_step = sem("pool_step")

        with nc.Block() as block:
            @block.sync
            def _(sp):
                sp.dma_start(w_dkv[:], arg["W_dkv"].rearrange("(c p) n -> p c n", p=P)).then_inc(dkv_in, 16)
                sp.dma_start(norm_w[:], arg["kv_norm_w"].partition_broadcast(P)).then_inc(tables_in, 16)
                sp.dma_start(cos[:], arg["cos_k"]).then_inc(tables_in, 16)
                sp.dma_start(sin[:], arg["sin_k"]).then_inc(tables_in, 16)
                sp.dma_start(wq_n[:], arg["Wq_nope_T"]).then_inc(weights_in, 16)
                sp.dma_start(w_uk[:], arg["W_uk_T"]).then_inc(weights_in, 16)
                for n in range(2):
                    sp.dma_start(w_uv[:, :, n, :], arg["W_uv_T"]).then_inc(weights_in, 16)
                sp.dma_start(wo[:], arg["Wo"]).then_inc(weights_in, 16)
                for c in range(KC):
                    sp.dma_start(w_all[:, c, :, RANK:], arg["Wq"][c * P:(c + 1) * P, :].rearrange(
                        "p (h d) -> p h d", h=HA)[:, :, DN:]).then_inc(weights_in, 16)
                sp.dma_start(rope[:, 0], arg["cos_q"]).then_inc(weights_in, 16)
                sp.dma_start(rope[:, 1], arg["sin_q"]).then_inc(weights_in, 16)
                sp.dma_start(x[:], arg["hidden"].rearrange("(t p) d -> p t d", p=P)).then_inc(x_in, 16)
                sp.dma_start(xT_rows, xT[:]).then_inc(x_in, 16)
                sp.wait_ge(weights_in, 9 * 16)
                sp.wait_ge(x_in, 2 * 16)

            @block.tensor
            def _(pe):
                pe.wait_ge(dkv_in, 16)
                for t in range(NT):
                    for k in range(KC):
                        last = nc.tensor.matmul(bank[t // 4][:, t % 4 * P:(t % 4 + 1) * P], xT[:, k, t * P:(t + 1) * P],
                                                w_dkv[:, k, :], start=k == 0, stop=k == KC - 1)
                    if t % 4 == 3:
                        last.then_inc(kv_done, 1)
                pe.wait_ge(weights_in, 9 * 16)
                for n in range(HA * KC):
                    h, c = n // KC, n % KC
                    last = nc.tensor.matmul(bank[4 + n // 8][:, n % 8 * RANK:(n % 8 + 1) * RANK],
                                            wq_n[:, h, c * P:(c + 1) * P], w_uk[:, h, :], start=True, stop=True)
                    if n % 8 == 7:
                        last.then_inc(absorbed, 1)
                for n in range(HA // 2):
                    pe.wait_ge(absorbed_stored, n + 1)
                    for j in range(2):
                        last = nc.tensor.matmul(bank[4 + n % 4][:, j * D:(j + 1) * D],
                                                w_uv[:, 2 * n + j, :, :].rearrange("p a r -> p (a r)"), wo[:, 2 * n + j, :],
                                                start=True, stop=True)
                    last.then_inc(absorbed, 1)
                pe.wait_ge(keys_ready, 1)
                for t in range(NT):
                    last = nc.tensor.transpose(bank[t // 4][:, t % 4 * P:(t % 4 + 1) * P], keys[:, t, :], const["ident"][:])
                    if t % 4 == 3:
                        last.then_inc(turned, 1)
                pe.wait_ge(absorbed_stored, 4 + HA // 2)
                for t in range(NT):
                    last = nc.tensor.matmul(bank[4][0:RANK, 0:P], keys[:, t, 0:RANK], const["mean"][:],
                                            start=t == 0, stop=t == NT - 1)
                last.then_inc(mean_done, 1)
                pe.wait_ge(mean_stored, 1)
                for h in range(HA):
                    last = nc.tensor.matmul(bank[5][:, 0:D], mean_c[:], w_out[0:RANK, h, :], start=h == 0, stop=h == HA - 1)
                last.then_inc(mean_done, 1)

            @block.scalar
            def _(act):
                for n in range(4):
                    act.wait_ge(kv_done, n + 1)
                    nc.scalar.activation(raw[:, 4 * n:4 * n + 4, :], bank[n][:].rearrange("p (t n) -> p t n", t=4),
                                         ACT.Copy).then_inc(kv_stored, 1)
                act.wait_ge(ss_ready, 1)
                nc.scalar.activation(rms[:], ss[:], ACT.Sqrt).then_inc(rms_ready, 1)
                for n in range(4):
                    act.wait_ge(absorbed, n + 1)
                    for c in range(KC):
                        last = nc.scalar.activation(
                            w_all[:, c, 4 * n:4 * n + 4, 0:RANK],
                            bank[4 + n][:].rearrange("p (h c r) -> p c h r", c=KC, r=RANK)[:, c], ACT.Copy, scale=SCALE_A)
                    last.then_inc(absorbed_stored, 1)
                for n in range(HA // 2):
                    act.wait_ge(absorbed, 4 + n + 1)
                    nc.scalar.activation(w_out[:, 2 * n:2 * n + 2, :], bank[4 + n % 4].rearrange("p (a n) -> p a n", a=2),
                                         ACT.Copy).then_inc(absorbed_stored, 1)
                act.wait_ge(keys_ready, 1)
                nc.scalar.activation(c_stack[:, :, 0:RANK], keys[:, :, 0:RANK], ACT.Copy).then_inc(c_done, 1)
                for n in range(4):
                    act.wait_ge(turned, n + 1)
                    nc.scalar.activation(k_hi[:, n * CH:(n + 1) * CH], bank[n][:], ACT.Copy).then_inc(hi_done, 1)
                act.wait_ge(mean_done, 1)
                nc.scalar.activation(mean_c[:], bank[4][0:RANK, 0:P], ACT.Copy).then_inc(mean_stored, 1)
                act.wait_ge(mean_done, 2)
                nc.scalar.activation(nowhere[:], bank[5][:, 0:D], ACT.Copy)

            @block.vector
            def _(dve):
                chain = Chain(dve, dve_step)
                dve.wait_ge(kv_stored, 4)
                dve.wait_ge(tables_in, 3 * 16)
                chain.step(nc.vector.tensor_tensor(sq[:], raw[:, :, 0:RANK], raw[:, :, 0:RANK], ALU.mult))
                chain.wait()
                chain.step(nc.vector.tensor_reduce(ss[:], sq[:], AX.X, ALU.add))
                chain.wait()
                nc.vector.tensor_scalar(ss[:], ss[:], 1.0 / RANK, RMS_EPS, ALU.mult, ALU.add).then_inc(ss_ready, 1)
                r1, r2 = raw[:, :, RANK:RANK + HALF], raw[:, :, RANK + HALF:]
                chain.step(nc.vector.tensor_tensor(tmp[0][:], r1, cos[:], ALU.mult))
                chain.step(nc.vector.tensor_tensor(tmp[1][:], r2, sin[:], ALU.mult))
                chain.step(nc.vector.tensor_tensor(tmp[2][:], r2, cos[:], ALU.mult))
                chain.step(nc.vector.tensor_tensor(tmp[3][:], r1, sin[:], ALU.mult))
                chain.wait()
                chain.step(nc.vector.tensor_tensor(keys[:, :, RANK:RANK + HALF], tmp[0][:], tmp[1][:], ALU.subtract))
                chain.step(nc.vector.tensor_tensor(keys[:, :, RANK + HALF:], tmp[2][:], tmp[3][:], ALU.add))
                dve.wait_ge(rms_ready, 1)
                chain.step(nc.vector.reciprocal(rms[:], rms[:]))
                chain.wait()
                chain.step(nc.vector.tensor_tensor(sq[:], raw[:, :, 0:RANK],
                                                   rms[:].unsqueeze(2).to_broadcast([P, NT, RANK]), ALU.mult))
                chain.wait()
                nc.vector.tensor_tensor(keys[:, :, 0:RANK], sq[:],
                                        norm_w[:].unsqueeze(1).to_broadcast([P, NT, RANK]), ALU.mult).then_inc(keys_ready, 1)
                for n in range(4):
                    dve.wait_ge(hi_done, n + 1)
                    part = slice(n * CH, (n + 1) * CH)
                    nc.vector.tensor_tensor(k_lo[:, part], bank[n][:], k_hi[:, part].bitcast(F32),
                                            ALU.subtract).then_inc(lo_done, 1)
                dve.wait_ge(c_done, 1)
                nc.vector.tensor_tensor(c_stack[:, :, RANK:], keys[:, :, 0:RANK], c_stack[:, :, 0:RANK].bitcast(F32),
                                        ALU.subtract).then_inc(lo_done, 1)


def attention_a(nc, arg, x, xT, bank, const, k_hi, k_lo, c_stack, bias, empty, filled, w_all, w_out, nowhere, rope, xT_rows):
    NG = HA // GH
    chunks = [(t + 4) // 4 for t in range(NT)]
    QB = [GH * sum(chunks[:t]) for t in range(NT + 1)]
    TB = [t * (t + 1) // 2 for t in range(NT + 1)]
    QN, TN = QB[NT], TB[NT]
    RING = 4

    with Phase(nc, "aa") as phase:
        sb, sem = phase.sb, phase.sem
        xt = [sb(f"xt{p}", [P, KC, P]) for p in range(2)]
        q_nat = sb("q_nat", [P, GH, P])
        tmp = [sb(f"tmp{n}", [P, GH, HALF]) for n in range(4)]
        q_hi = [sb(f"q_hi{p}", [P, GH * P], F32R) for p in range(2)]
        q_lo = [sb(f"q_lo{p}", [P, GH * P], F32R) for p in range(2)]
        prob = [[sb(f"prob0{h}", [P, S - P])[:] for h in range(GH)],
                [xT[:, h, :] for h in range(KC)] + [sb(f"prob1{h}", [P, S])[:] for h in range(KC, GH)]]
        pt_hi = [sb(f"pt_hi{n}", [P, GH * P], F32R) for n in range(RING)]
        pt_lo = [sb(f"pt_lo{n}", [P, GH * P], F32R) for n in range(RING)]
        out_t = sb("out_t", [P, GH * P])
        chunk_max = [sb(f"chunk_max{p}", [P, GH, NCH]) for p in range(2)]
        neg_max = [sb(f"neg_max{p}", [P, GH]) for p in range(2)]
        total = [sb(f"total{p}", [P, GH]) for p in range(2)]
        inv = [sb(f"inv{p}", [P, GH]) for p in range(2)]

        xt_in = [sem(f"xt_in{p}") for p in range(2)]
        q_proj = sem("q_proj")
        q_nat_ready = sem("q_nat_ready")
        roped = sem("roped")
        q_turned = sem("q_turned")
        q_hi_done = sem("q_hi_done")
        q_lo_done = sem("q_lo_done")
        scores_ready = sem("scores_ready")
        scores_out = sem("scores_out")
        take_go = sem("take_go")
        max_ready = sem("max_ready")
        exp_done = sem("exp_done")
        turned = sem("turned")
        pt_hi_done = sem("pt_hi_done")
        pt_lo_done = sem("pt_lo_done")
        pv_done = sem("pv_done")
        kept = sem("kept")
        total_turned = sem("total_turned")
        inv_done = sem("inv_done")
        y_ready = sem("y_ready")
        x_added = sem("x_added")
        nowhere_added = sem("nowhere_added")
        score_bank, turn_bank, out_bank = bank[0:2], bank[2:2 + RING], bank[6]
        y_bank = q_bank = bank[7]

        def plan(t, left, scored, flipped, queried):
            todo = []
            for j in range(t + 1):
                todo.append((j / (t + 1), ("turn", j)))
                todo.append(((j + LAG) / (t + 1) + 2e-6, ("weigh", j)))
            if left:
                todo += [(Y_AT[pair], ("y", pair)) for pair in range(GH // 2)]
            if scored:
                n = GH * chunks[(t + 1) % NT]
                for k in range(n):
                    todo.append(((k + 0.5) / n * SCORES_BY, ("score", *divmod(k, chunks[(t + 1) % NT]))))
            if flipped:
                todo.append((FLIP_AT, ("flip",)))
            if queried:
                todo.append((PROJECT_AT, ("project",)))
            return [what for _, what in sorted(todo, key=lambda one: one[0])]

        def behind(steps, lags):
            mine = [(n + lags[what[0]], n, what) for n, what in enumerate(steps) if what[0] in lags]
            return [what for _, _, what in sorted(mine)]

        def walk(eng, before, step, finish):
            def passes(i, last):
                for t in range(NT):
                    ahead = [(i + (t + n) // NT, (t + n) % NT) for n in (1, 2, 3)]
                    there = [not last or t + n < NT for n in (1, 2, 3)]
                    step(i, t, ahead, plan(t, t > 0, *there))
                finish(i)
            before()
            with eng.Fori(0, NG - 1) as i:
                passes(i, False)
            passes(NG - 1, True)

        with nc.Block() as block:
            @block.sync
            def _(sp):
                def load(i, t):
                    g = i * NT + t
                    sp.wait_ge(q_proj, g + 1)
                    sp.dma_start(xt[t % 2][:], xT_rows[:, :, t * P:(t + 1) * P]).then_inc(xt_in[t % 2], 16)

                with sp.Fori(0, NG) as i:
                    for t in range(NT):
                        load(i, t)

            @block.gpsimd
            def _(pool):
                def rotate(i, t):
                    g = i * NT + t
                    cos = rope[:, 0, t, :].unsqueeze(1).to_broadcast([P, GH, HALF])
                    sin = rope[:, 1, t, :].unsqueeze(1).to_broadcast([P, GH, HALF])
                    r1, r2 = q_nat[:, :, RANK:RANK + HALF], q_nat[:, :, RANK + HALF:]
                    pool.wait_ge(q_nat_ready, g + 1)
                    pool.wait_ge(roped, g * 6 + 1)
                    for n, (r, table) in enumerate(((r1, cos), (r2, sin), (r2, cos), (r1, sin))):
                        nc.gpsimd.tensor_tensor(tmp[n][:], r, table, ALU.mult).then_inc(roped, 1)
                    pool.wait_ge(roped, g * 6 + 4 + 1)
                    nc.gpsimd.tensor_tensor(r1, tmp[0][:], tmp[1][:], ALU.subtract).then_inc(roped, 1)
                    nc.gpsimd.tensor_tensor(r2, tmp[2][:], tmp[3][:], ALU.add).then_inc(roped, 1)

                pool.sem_inc(roped, 1)
                with pool.Fori(0, NG) as i:
                    for t in range(NT):
                        rotate(i, t)

            @block.tensor
            def _(pe):
                def project(i, t):
                    g = i * NT + t
                    pe.wait_ge(xt_in[t % 2], (i * (NT // 2) + t // 2) * 16 + 16)
                    pe.wait_ge(q_lo_done, g + 1)
                    heads = w_all[:].rearrange("p c h d -> p c (h d)")
                    first = i * GH * P
                    for k in range(KC):
                        cols = slice(first, first + GH * P) if isinstance(i, int) else bass.ds(first, GH * P)
                        last = nc.tensor.matmul(q_bank[:], xt[t % 2][:, k, :], heads[:, k, cols],
                                                start=k == 0, stop=k == KC - 1)
                    last.then_inc(q_proj, 1)

                def flip(i, t):
                    g = i * NT + t
                    pe.wait_ge(roped, g * 6 + 6 + 1)
                    pe.wait_ge(x_added, (g - 2) * GH + 4 * GH)
                    for h in range(GH):
                        last = nc.tensor.transpose(q_bank[:, h * P:(h + 1) * P], q_nat[:, h, :], const["ident"][:])
                    last.then_inc(q_turned, 1)

                def score(i, t, h, c):
                    g, n = i * NT + t, i * QN + QB[t] + h * chunks[t] + c
                    w = min(CH, (t + 1) * P - c * CH)
                    if h == 0 and c == 0:
                        pe.wait_ge(q_lo_done, g + 1 + 1)
                    pe.wait_ge(scores_out, n + 1)
                    out = score_bank[(QB[t] + h * chunks[t] + c) % 2]
                    cols, head = slice(c * CH, c * CH + w), slice(h * P, (h + 1) * P)
                    nc.tensor.matmul(out[:, 0:w], q_hi[t % 2][:, head], k_hi[:, cols], start=True, stop=False)
                    nc.tensor.matmul(out[:, 0:w], q_hi[t % 2][:, head], k_lo[:, cols], start=False, stop=False)
                    nc.tensor.matmul(out[:, 0:w], q_lo[t % 2][:, head], k_hi[:, cols], start=False,
                                     stop=True).then_inc(scores_ready, 1)

                def turn(i, t, j):
                    g, n = i * NT + t, i * TN + TB[t] + j
                    if j == 0:
                        pe.wait_ge(exp_done, g * GH + GH)
                    pe.wait_ge(pt_lo_done, n + 1)
                    for h in range(GH):
                        last = nc.tensor.transpose(turn_bank[(TB[t] + j) % RING][:, h * P:(h + 1) * P],
                                                   prob[t % 2][h][:, j * P:(j + 1) * P], const["ident"][:])
                    last.then_inc(turned, 1)

                def weigh(i, t, j):
                    g, n = i * NT + t, i * TN + TB[t] + j
                    out, ring = out_bank, (TB[t] + j) % RING
                    pe.wait_ge(pt_lo_done, n + 1 + RING)
                    if j == 0:
                        pe.wait_ge(kept, g + 1)
                    nc.tensor.matmul(out[:], c_stack[:, j, :], pt_hi[ring][:], start=j == 0, stop=j == t,
                                     skip_group_check=True)
                    nc.tensor.matmul(out[0:RANK, :], c_stack[:, j, 0:RANK], pt_lo[ring][:], start=False, stop=j == t,
                                     skip_group_check=True).then_inc(pv_done, 1)

                def leave(i, t, pair):
                    g = i * NT + t
                    pe.wait_ge(kept, g + 1 + 1)
                    if pair == 0:
                        pe.wait_ge(q_nat_ready, min(g + 4, NG * NT) if isinstance(g, int) else g + 4)
                    pe.wait_ge(x_added, g * GH + 2 * pair + 4 * GH)
                    for h in range(2 * pair, 2 * pair + 2):
                        head = i * GH + h
                        last = nc.tensor.matmul(y_bank[:, h % 2 * D:(h % 2 + 1) * D], out_t[:, h * P:(h + 1) * P],
                                                w_out[:, head if isinstance(head, int) else bass.ds(head, 1), :],
                                                start=True, stop=True)
                    last.then_inc(y_ready, 1)

                def before():
                    pe.sem_inc(q_proj, 2)
                    pe.sem_inc(turned, TN)
                    pe.sem_inc(pv_done, RING)
                    pe.sem_inc(y_ready, GH // 2)
                    pe.sem_inc(scores_ready, QN)
                    for t in range(2):
                        project(0, t)
                        flip(0, t)
                    project(0, 2)
                    for h in range(GH):
                        score(0, 0, h, 0)

                def step(i, t, ahead, steps):
                    for what in steps:
                        if what[0] == "project":
                            project(*ahead[2])
                        elif what[0] == "flip":
                            flip(*ahead[1])
                        elif what[0] == "score":
                            score(*ahead[0], *what[1:])
                        elif what[0] == "turn":
                            turn(i, t, what[1])
                        elif what[0] == "weigh":
                            weigh(i, t, what[1])
                        else:
                            leave(i, t - 1, what[1])

                def finish(i):
                    for pair in range(GH // 2):
                        leave(i, NT - 1, pair)

                walk(pe, before, step, finish)

            @block.scalar
            def _(act):
                def store_queries(i, t):
                    g = i * NT + t
                    act.wait_ge(q_proj, g + 1 + 2)
                    act.wait_ge(q_turned, g + 1)
                    nc.scalar.activation(q_nat[:], q_bank.rearrange("p (h d) -> p h d", h=GH),
                                         ACT.Copy).then_inc(q_nat_ready, 1)

                def split_queries(i, t):
                    g = i * NT + t
                    act.wait_ge(q_turned, g + 1 + 1)
                    act.wait_ge(scores_ready, i * QN + (QB[t - 1] if t else QB[NT - 1] - QN) + QN)
                    nc.scalar.activation(q_hi[t % 2][:], q_bank, ACT.Copy).then_inc(q_hi_done, 1)

                def exponentials(i, t, h):
                    g, L = i * NT + t, (t + 1) * P
                    act.wait_ge(max_ready, g * GH + h + 1)
                    if h == 0:
                        act.wait_ge(inv_done, g + 1)
                    nc.scalar.activation(prob[t % 2][h][:, 0:L], prob[t % 2][h][:, 0:L], ACT.Exp,
                                         bias=neg_max[t % 2][:, h:h + 1],
                                         accum_out=total[t % 2][:, h:h + 1]).then_inc(exp_done, 1)

                def split_turned(i, t, j):
                    n = i * TN + TB[t] + j
                    act.wait_ge(turned, n + 1 + TN)
                    act.wait_ge(pv_done, n + 1)
                    nc.scalar.activation(pt_hi[(TB[t] + j) % RING][:], turn_bank[(TB[t] + j) % RING], ACT.Copy).then_inc(pt_hi_done, 1)

                def keep(i, t):
                    g = i * NT + t
                    act.wait_ge(pv_done, i * TN + TB[t + 1] + RING)
                    act.wait_ge(y_ready, (g + 1) * (GH // 2))
                    nc.scalar.activation(out_t[:], out_bank, ACT.Copy).then_inc(kept, 1)

                def before():
                    act.sem_inc(q_turned, 1)
                    act.sem_inc(kept, 1)
                    for t in range(2):
                        store_queries(0, t)
                        split_queries(0, t)
                    store_queries(0, 2)
                    for h in range(GH):
                        exponentials(0, 0, h)

                def step(i, t, ahead, steps):
                    for what in behind(steps, {"project": 0, "flip": 0, "score": 4, "turn": 0}):
                        if what[0] == "project":
                            store_queries(*ahead[2])
                        elif what[0] == "flip":
                            split_queries(*ahead[1])
                        elif what[0] == "turn":
                            split_turned(i, t, what[1])
                        elif what[2] == chunks[ahead[0][1]] - 1:
                            exponentials(*ahead[0], what[1])
                    keep(i, t)

                walk(act, before, step, lambda i: None)

            @block.vector
            def _(dve):
                def split_queries(i, t):
                    dve.wait_ge(q_hi_done, i * NT + t + 1)
                    nc.vector.tensor_tensor(q_lo[t % 2][:], q_bank, q_hi[t % 2][:].bitcast(F32),
                                            ALU.subtract).then_inc(q_lo_done, 1)

                def take(i, t, h, c):
                    g, n = i * NT + t, i * QN + QB[t] + h * chunks[t] + c
                    w = min(CH, (t + 1) * P - c * CH)
                    if h == 0 and c == 0:
                        dve.wait_ge(turned, i * TN + (TB[t - 1] if t else TB[NT - 1] - TN) + TN)
                    dve.wait_ge(scores_ready, n + 1 + QN)
                    dve.sem_inc(take_go, 1)
                    nc.vector.tensor_tensor_reduce(prob[t % 2][h][:, c * CH:c * CH + w],
                                                   score_bank[(QB[t] + h * chunks[t] + c) % 2][:, 0:w],
                                                   bias[:, TRI[t] + c * CH:TRI[t] + c * CH + w], 1.0, -BIG, ALU.add, ALU.max,
                                                   chunk_max[t % 2][:, h, c:c + 1]).then_inc(scores_out, 1)
                    if c == chunks[t] - 1:
                        dve.wait_ge(scores_out, n + 1 + 2)
                        nc.vector.tensor_reduce(neg_max[t % 2][:, h:h + 1], chunk_max[t % 2][:, h, 0:c + 1], AX.X, ALU.max,
                                                negate=True).then_inc(max_ready, 1)

                def split_turned(i, t, j):
                    n = i * TN + TB[t] + j
                    ring = (TB[t] + j) % RING
                    dve.wait_ge(pt_hi_done, n + 1)
                    nc.vector.tensor_tensor(pt_lo[ring][:], turn_bank[(TB[t] + j) % RING], pt_hi[ring][:].bitcast(F32),
                                            ALU.subtract).then_inc(pt_lo_done, 1)

                def invert(i, t):
                    g = i * NT + t
                    dve.wait_ge(exp_done, g * GH + GH)
                    dve.wait_ge(x_added, (g - 1) * GH + 4 * GH)
                    nc.vector.reciprocal(inv[t % 2][:], total[t % 2][:]).then_inc(total_turned, 1)
                    dve.wait_ge(total_turned, g + 1)
                    nc.vector.tensor_scalar(inv[t % 2][:], inv[t % 2][:], filled[:, t:t + 1], None,
                                            ALU.mult).then_inc(inv_done, 1)

                def add(i, t, pair):
                    g = i * NT + t
                    dve.wait_ge(y_ready, (g + 1) * (GH // 2) + pair + 1)
                    dve.wait_ge(inv_done, g + 1 + 2)
                    for h in range(2 * pair, 2 * pair + 2):
                        dve.wait_ge(x_added, g * GH + h + 4 * GH)
                        nc.vector.scalar_tensor_tensor(out=x[:, t, :], in0=y_bank[:, h % 2 * D:(h % 2 + 1) * D],
                                                       scalar=inv[t % 2][:, h:h + 1], in1=x[:, t, :],
                                                       op0=ALU.mult, op1=ALU.add).then_inc(x_added, 1)

                def before():
                    dve.sem_inc(q_lo_done, 1)
                    dve.sem_inc(scores_out, 2)
                    dve.sem_inc(pt_lo_done, RING)
                    dve.sem_inc(inv_done, 2)
                    dve.sem_inc(x_added, 4 * GH)
                    for t in range(NT):
                        nc.vector.scalar_tensor_tensor(out=x[:, t, :], in0=nowhere[:], scalar=empty[:, t:t + 1], in1=x[:, t, :],
                                                       op0=ALU.mult, op1=ALU.add).then_inc(nowhere_added, 1)
                    dve.wait_ge(nowhere_added, NT)
                    for t in range(2):
                        split_queries(0, t)
                    for h in range(GH):
                        take(0, 0, h, 0)

                def step(i, t, ahead, steps):
                    invert(i, t)
                    for what in behind(steps, {"flip": 1, "score": 0, "turn": 3, "y": 1}):
                        if what[0] == "flip":
                            split_queries(*ahead[1])
                        elif what[0] == "score":
                            take(*ahead[0], *what[1:])
                        elif what[0] == "turn":
                            split_turned(i, t, what[1])
                        else:
                            add(i, t - 1, what[1])

                def finish(i):
                    for pair in range(GH // 2):
                        add(i, NT - 1, pair)

                walk(dve, before, step, finish)


def prepare_b(nc, arg, xT, bank, stash, values):
    with Phase(nc, "pb") as phase:
        sb, sem = phase.sb, phase.sem
        w_dkv = sb("w_dkv", [P, KC, KVB])
        w_q = sb("w_q", [P, KC, D])
        w_uk = sb("w_uk", [P, D])
        w_uv = sb("w_uv", [P, D])
        c_kv = sb("c_kv", [P, S])
        part = {name: sb(name, [P, KC, S], F32R) for name in ("q_hi", "q_lo", "k_hi", "k_lo")}
        loaded = sem("loaded")
        done = sem("done")
        stored = sem("stored")
        lo_done = sem("lo_done")
        stashed = sem("stashed")
        ones_done = sem("ones_done")
        RING = 4
        FIRST_Q, FIRST_K, FIRST_V, ALL = NCH, NCH + KC * NCH, NCH + 2 * KC * NCH, NCH + 2 * KC * NCH + NT // 2
        with nc.Block() as block:
            @block.sync
            def _(sp):
                sp.dma_start(w_dkv[:], arg["b_dkv_T"].rearrange("(c p) n -> p c n", p=P)).then_inc(loaded, 16)
                sp.dma_start(w_q[:], arg["b_q_T"].rearrange("(c p) n -> p c n", p=P)).then_inc(loaded, 16)
                sp.dma_start(w_uk[:], arg["b_uk_T"]).then_inc(loaded, 16)
                sp.dma_start(w_uv[:], arg["b_uv_T"]).then_inc(loaded, 16)
                for n in range(2 * KC):
                    name, m = "qk"[n // KC], n % KC
                    sp.wait_ge(lo_done, NCH * (n + 1))
                    for which in ("_hi", "_lo"):
                        sp.dma_start(stash[name + which][m * P:(m + 1) * P, :], part[name + which][:, m, :].bitcast(F32)).then_inc(stashed, 16)
                sp.wait_ge(stashed, 2 * 2 * KC * 16)

            @block.gpsimd
            def _(pool):
                nc.gpsimd.memset(values[:, :, :, DHB:], 1.0).then_inc(ones_done, 1)

            @block.tensor
            def _(pe):
                pe.wait_ge(loaded, 4 * 16)
                for n in range(ALL):
                    if n >= RING:
                        pe.wait_ge(stored, n - RING + 1)
                    if FIRST_Q <= n - RING < FIRST_V:
                        pe.wait_ge(lo_done, n - RING - FIRST_Q + 1)
                    out = bank[n % RING]
                    if n < FIRST_Q:
                        for k in range(KC):
                            last = nc.tensor.matmul(out[:], w_dkv[:, k, :], xT[:, k, n * CH:(n + 1) * CH],
                                                    start=k == 0, stop=k == KC - 1)
                    elif n < FIRST_K:
                        m, c = divmod(n - FIRST_Q, NCH)
                        for k in range(KC):
                            last = nc.tensor.matmul(out[:], w_q[:, k, m * P:(m + 1) * P], xT[:, k, c * CH:(c + 1) * CH],
                                                    start=k == 0, stop=k == KC - 1)
                    elif n < FIRST_V:
                        m, c = divmod(n - FIRST_K, NCH)
                        pe.wait_ge(stored, NCH)
                        last = nc.tensor.matmul(out[:], w_uk[:, m * P:(m + 1) * P], c_kv[:, c * CH:(c + 1) * CH],
                                                start=True, stop=True)
                    else:
                        for j in range(2):
                            t = 2 * (n - FIRST_V) + j
                            last = nc.tensor.matmul(out[:, j * D:(j + 1) * D], c_kv[:, t * P:(t + 1) * P], w_uv[:],
                                                    start=True, stop=True)
                    last.then_inc(done, 1)

            @block.scalar
            def _(act):
                for n in range(ALL):
                    act.wait_ge(done, n + 1)
                    have = bank[n % RING][:]
                    if n < FIRST_Q:
                        into, scale = c_kv[:, n * CH:(n + 1) * CH], 1.0
                    elif n < FIRST_V:
                        m, c = divmod((n - FIRST_Q) % (KC * NCH), NCH)
                        name, scale = ("q_hi", SCALE_B) if n < FIRST_K else ("k_hi", 1.0)
                        into = part[name][:, m, c * CH:(c + 1) * CH]
                    else:
                        t = 2 * (n - FIRST_V)
                        into, scale = values[:, :, t:t + 2, 0:DHB].rearrange("p h t d -> p t h d"), 1.0
                        have = have.rearrange("p (t h d) -> p t h d", t=2, d=DHB)
                    nc.scalar.activation(into, have, ACT.Copy, scale=scale).then_inc(stored, 1)

            @block.vector
            def _(dve):
                for n in range(FIRST_Q, FIRST_V):
                    m, c = divmod((n - FIRST_Q) % (KC * NCH), NCH)
                    name, scale = ("q", SCALE_B) if n < FIRST_K else ("k", 1.0)
                    dve.wait_ge(stored, n + 1)
                    cols = slice(c * CH, (c + 1) * CH)
                    nc.vector.scalar_tensor_tensor(out=part[name + "_lo"][:, m, cols], in0=bank[n % RING][:], scalar=scale,
                                                   in1=part[name + "_hi"][:, m, cols].bitcast(F32),
                                                   op0=ALU.mult, op1=ALU.subtract).then_inc(lo_done, 1)


def attention_b(nc, arg, x, xT, bank2, bank, const, stash, max_rows, values):
    NB = 4
    with Phase(nc, "ab") as phase:
        sb, sem = phase.sb, phase.sem
        q_stack = [sb(f"q_stack{p}", [P, S], F32R) for p in range(NB)]
        k_stack = [sb(f"k_stack{p}", [P, S], F32R) for p in range(NB)]
        after_wide = sb("after_wide", [P, 2, P])
        after = sb("after", [P, 2, P], BF16)
        ident16 = sb("ident16", [P, P], BF16)
        alibi = xT[:, 0, :]
        w_out = sb("w_out", [P, KC, D])
        part_max = [sb(f"part_max{p}", [P, 2, NT]) for p in range(2)]
        row_max = [sb(f"row_max{p}", [P, NT]) for p in range(2)]
        neg_max = [sb(f"neg_max{p}", [NT, P], F32R) for p in range(2)]
        prob = [sb(f"prob{n}", [P, CH]) for n in range(4)]
        v_stack = [sb(f"v_stack{p}", [P, NT, DHB + 1]) for p in range(NB)]
        o_rows = [sb(f"o_rows{p}", [P, CH]) for p in range(2)]
        o_sums = sb("o_sums", [P, NT, HB, DHB + 1])
        inv = [sb(f"inv{p}", [P, HB, 1]) for p in range(2)]
        o = [sb(f"o{p}", [P, D]) for p in range(2)]
        o_t = [sb(f"o_t{p}", [P, KC, P]) for p in range(2)]
        consts_in = sem("consts_in")
        stacks_set = sem("stacks_set")
        after_set = sem("after_set")
        staged = [sem(f"staged{p}") for p in range(NB)]
        s_ready = sem("s_ready")
        s_used = sem("s_used")
        max_ready = sem("max_ready")
        max_out = sem("max_out")
        max_in = sem("max_in")
        t_ready = sem("t_ready")
        t_taken = sem("t_taken")
        pv_done = sem("pv_done")
        kept = sem("kept")
        act_go = sem("act_go")
        buffers_set = sem("buffers_set")
        inv_done = sem("inv_done")
        o_done = sem("o_done")
        o_turned = sem("o_turned")
        o_t_done = sem("o_t_done")
        out_done = sem("out_done")
        x_done = sem("x_done")

        s_bank, t_bank, o_bank = bank2, bank[4:6], bank[6:8]
        S_UNITS = [(t, 2 * CH * n, min(2 * CH, (t + 1) * P - 2 * CH * n))
                   for t in reversed(range(NT)) for n in range((t + 8) // 8)]
        T_UNITS = [(c, kb, max(c * CH, kb * P), (c + 1) * CH - max(c * CH, kb * P))
                   for c in range(NCH) for kb in range(4 * (c + 1))]
        NSU, NTU = len(S_UNITS), len(T_UNITS)
        AHEAD = 6
        ENDS = [sum(4 * (k + 1) for k in range(c + 1)) for c in range(NCH)]
        SLOTS = NTU + 1 + NCH

        def order(h):
            todo = [n % NSU for n in range(AHEAD, AHEAD + NSU) if h + 1 + n // NSU < HB]
            columns = sum(S_UNITS[n][2] for n in todo)
            steps, sent, turn_at = [], 0, None
            for n in range(NTU + 2):
                if n < NTU:
                    steps.append(("t", n))
                while len(todo) > (2 if h + 2 < HB else 0) and sent < columns * (n + 1) / (NTU + 2):
                    one = todo.pop(0)
                    sent += S_UNITS[one][2]
                    steps.append(("s", one))
                    if one == NSU - 1:
                        turn_at = n + 3
                if n == turn_at:
                    steps.append(("turn",))
                if n >= 2:
                    steps.append(("weigh", n - 2))
                if n - 4 in ENDS[:-1]:
                    steps.append(("flip", ENDS.index(n - 4)))
            if turn_at is not None and turn_at >= NTU + 2:
                steps.append(("turn",))
            return steps + [("s", n) for n in todo] + [("flip", NCH - 1)]

        def slots(steps):
            return {what: n for n, what in enumerate(w for w in steps if w[0] in ("t", "turn", "flip"))}

        USUAL = order(0)
        TURN = slots(USUAL)[("turn",)]

        with nc.Block() as block:
            @block.sync
            def _(sp):
                sp.dma_start(after_wide[:], arg["b_after"]).then_inc(consts_in, 16)
                sp.dma_start(w_out[:], arg["b_o_T"].rearrange("(c p) n -> p c n", p=P)).then_inc(consts_in, 16)

                def stage(h, b):
                    rows = slice(h * DHB, (h + 1) * DHB) if isinstance(h, int) else bass.ds(h * DHB, DHB)
                    for stack, first, name in ((q_stack, 0, "q_hi"), (q_stack, R_LO, "q_lo"), (q_stack, R_HI2, "q_hi"),
                                               (k_stack, 0, "k_hi"), (k_stack, R_LO, "k_hi"), (k_stack, R_HI2, "k_lo")):
                        sp.dma_start(stack[b][first:first + DHB, :].bitcast(F32), stash[name][rows, :]).then_inc(staged[b], 16)
                    sp.dma_start(v_stack[b][:], values[:, h if isinstance(h, int) else bass.ds(h, 1), :, :]).then_inc(staged[b], 16)

                def send_max(h, slot, b):
                    sp.wait_ge(t_taken, slot + 1 + 2)
                    sp.dma_start(max_rows, neg_max[b % 2][:].bitcast(F32)).then_inc(max_out, 16)
                    sp.wait_ge(max_out, h * 16 + 16)
                    sp.dma_start(q_stack[b][R_MAX:R_MAX + 1, :].bitcast(F32),
                                 max_rows.rearrange("t q -> (t q)").unsqueeze(0)).then_inc(max_in, 16)
                    sp.wait_ge(max_in, h * 16 + 16)

                sp.dma_start(alibi[R_HI2:R_MAX, :], arg["b_alibi"].partition_broadcast(R_MAX - R_HI2)).then_inc(consts_in, 16)
                sp.wait_ge(stacks_set, 5 * NB)
                for h in range(NB):
                    stage(h, h)
                send_max(0, 0, 0)
                with sp.Fori(0, HB // NB - 1) as i:
                    for b in range(NB):
                        h = i * NB + b
                        send_max(h + 1, h * SLOTS + 1 + TURN, (b + 1) % NB)
                        sp.wait_ge(pv_done, (h + 1) * NTU + 4)
                        stage(h + NB, b)
                for h in range(HB - NB, HB - 1):
                    send_max(h + 1, h * SLOTS + 1 + slots(order(h))[("turn",)], (h + 1) % NB)

            @block.tensor
            def _(pe):
                pe.sem_inc(pv_done, 4)

                def s_piece(h, b, n, turn):
                    t, k0, w = S_UNITS[n]
                    if n == 0:
                        pe.wait_ge(staged[b], turn * 7 * 16 + 7 * 16)
                    pe.wait_ge(s_used, h * NSU + n + 1)
                    for c in range(0, w, CH):
                        cw = min(CH, w - c)
                        diag = k0 + c + cw == (t + 1) * P
                        if diag:
                            nc.tensor.matmul(s_bank[n % 2][:, c + cw - P:c + cw], ident16[:], after[:, 0, :],
                                             start=True, stop=False, skip_group_check=True)
                        last = nc.tensor.matmul(s_bank[n % 2][:, c:c + cw], q_stack[b][0:R_MAX, t * P:(t + 1) * P],
                                                k_stack[b][0:R_MAX, k0 + c:k0 + c + cw], start=not diag, stop=True,
                                                skip_group_check=True)
                    last.then_inc(s_ready, 1)

                def turn_max(h, b, slot, bank_of):
                    pe.wait_ge(max_ready, h + 1)
                    pe.wait_ge(t_taken, slot + 1)
                    nc.tensor.transpose(bank_of[0:NT, 0:P], row_max[b % 2][:], const["ident"][:]).then_inc(t_ready, 1)

                def t_piece(h, b, n, slot, bank_of):
                    c, kb, q0, w = T_UNITS[n]
                    if n == 0:
                        pe.wait_ge(max_in, h * 16 + 16)
                    pe.wait_ge(t_taken, slot + 1)
                    diag = kb >= 4 * c
                    if diag:
                        nc.tensor.matmul(bank_of[:, 0:P], ident16[:], after[:, 1, :], start=True, stop=False,
                                         skip_group_check=True)
                    last = nc.tensor.matmul(bank_of[:, 0:w], k_stack[b][0:R_MAX + 1, kb * P:(kb + 1) * P],
                                            q_stack[b][0:R_MAX + 1, q0:q0 + w], start=not diag, stop=True,
                                            skip_group_check=True)
                    last.then_inc(t_ready, 1)

                def weigh(h, b, n, slot):
                    c, kb, q0, w = T_UNITS[n]
                    pe.wait_ge(t_taken, slot + 1 + 2)
                    if kb == 0:
                        pe.wait_ge(kept, h * NCH + c + 1)
                    at = q0 - c * CH
                    parts = [(0, P, True), (P, w, False)] if kb >= 4 * c else [(0, w, False)]
                    for first, end, stop in parts:
                        if first < end:
                            last = nc.tensor.matmul(o_bank[c % 2][0:DHB + 1, at + first:at + end], v_stack[b][:, kb, :],
                                                    prob[n % 4][:, first:end], start=kb == 0 and first == 0, stop=stop,
                                                    skip_group_check=True)
                    last.then_inc(pv_done, 1)

                def flip(h, c, slot, bank_of):
                    pe.wait_ge(kept, h * NCH + c + 3)
                    pe.wait_ge(t_taken, slot + 1)
                    for j in range(CH // P):
                        last = nc.tensor.transpose(bank_of[:, j * P:(j + 1) * P], o_rows[c % 2][:, j * P:(j + 1) * P],
                                                   const["ident"][:])
                    last.then_inc(t_ready, 1)

                def step(h, b, turn, steps):
                    place = slots(steps)
                    later = 1
                    for what in steps:
                        slot = h * SLOTS + 1 + place.get(what, 0)
                        if what[0] == "s":
                            if what[1] == 0:
                                later = 2
                            s_piece(h + later, (b + later) % NB, what[1], turn + (b + later) // NB)
                        elif what[0] == "t":
                            t_piece(h, b, what[1], slot, t_bank[(1 + b + place[what]) % 2])
                        elif what[0] == "turn":
                            turn_max(h + 1, b + 1, slot, t_bank[(1 + b + place[what]) % 2])
                        elif what[0] == "flip":
                            flip(h, what[1], slot, t_bank[(1 + b + place[what]) % 2])
                        else:
                            weigh(h, b, what[1], h * SLOTS + 1 + place[("t", what[1])])

                def out_tile(t):
                    pe.wait_ge(o_t_done, t + 1)
                    for c in range(KC):
                        last = nc.tensor.matmul(o_bank[t % 2][:, 0:D], o_t[t % 2][:, c, :], w_out[:, c, :],
                                                start=c == 0, stop=c == KC - 1)
                    last.then_inc(out_done, 1)

                pe.wait_ge(after_set, 2)
                for n in range(NSU):
                    s_piece(0, 0, n, 0)
                turn_max(0, 0, 0, t_bank[0])
                for n in range(AHEAD):
                    s_piece(1, 1, n, 0)
                with pe.Fori(0, HB // NB - 1) as i:
                    for b in range(NB):
                        step(i * NB + b, b, i, USUAL)
                for h in range(HB - NB, HB):
                    step(h, h % NB, h // NB, order(h))
                pe.wait_ge(t_taken, HB * SLOTS + 2)
                for t in range(NT):
                    p = t % 2
                    pe.wait_ge(o_done, t + 1)
                    if t >= 2:
                        pe.wait_ge(x_done, t - 1)
                    for c in range(KC):
                        last = nc.tensor.transpose(t_bank[p][:, c * P:(c + 1) * P], o[p][:, c * P:(c + 1) * P],
                                                   const["ident"][:])
                    last.then_inc(o_turned, 1)
                    if t:
                        out_tile(t - 1)
                out_tile(NT - 1)

            @block.scalar
            def _(act):
                act.sem_inc(t_taken, 2)
                act.sem_inc(kept, 2)
                act.wait_ge(consts_in, 3 * 16)
                act.wait_ge(buffers_set, 4)
                for b in range(NB):
                    nc.scalar.activation(k_stack[b][R_HI2:R_MAX, :], alibi[R_HI2:R_MAX, :], ACT.Copy).then_inc(stacks_set, 1)

                def negate(b, slot, bank_of):
                    act.wait_ge(t_ready, slot + 1)
                    nc.scalar.activation(neg_max[b % 2][:], bank_of[0:NT, 0:P], ACT.Copy, scale=-1.0).then_inc(t_taken, 1)

                def step(h, b, steps):
                    place = slots(steps)
                    for what in steps:
                        slot, bank_of = h * SLOTS + 1 + place.get(what, 0), t_bank[(1 + b + place.get(what, 0)) % 2]
                        if what[0] == "turn":
                            negate(b + 1, slot, bank_of)
                        elif what[0] == "flip":
                            act.wait_ge(t_ready, slot + 1)
                            act.sem_inc(act_go, 1)
                            nc.scalar.activation(o_sums[:, 4 * what[1]:4 * what[1] + 4, h if isinstance(h, int) else bass.ds(h, 1), :],
                                                 bank_of[:].rearrange("p (j d) -> p j d", d=P)[:, :, 0:DHB + 1],
                                                 ACT.Copy).then_inc(t_taken, 1)
                        elif what[0] == "weigh":
                            if what[1] + 1 in ENDS:
                                c = ENDS.index(what[1] + 1)
                                act.wait_ge(pv_done, h * NTU + ENDS[c] + 4)
                                nc.scalar.activation(o_rows[c % 2][0:DHB + 1, :], o_bank[c % 2][0:DHB + 1, :], ACT.Copy).then_inc(kept, 1)
                        elif what[0] == "t":
                            n = what[1]
                            w = T_UNITS[n][3]
                            act.wait_ge(t_ready, slot + 1)
                            act.wait_ge(pv_done, h * NTU + n + 1)
                            nc.scalar.activation(prob[n % 4][:, 0:w], bank_of[:, 0:w], ACT.Exp).then_inc(t_taken, 1)

                negate(0, 0, t_bank[0])
                with act.Fori(0, HB // NB - 1) as i:
                    for b in range(NB):
                        step(i * NB + b, b, USUAL)
                for h in range(HB - NB, HB):
                    step(h, h % NB, order(h))
                for t in range(NT):
                    act.wait_ge(o_turned, t + 1)
                    if t >= 2:
                        act.wait_ge(out_done, t - 1)
                    nc.scalar.activation(o_t[t % 2][:], t_bank[t % 2][:, 0:D].rearrange("p (c n) -> p c n", c=KC),
                                         ACT.Copy).then_inc(o_t_done, 1)

            @block.vector
            def _(dve):
                for b in range(NB):
                    nc.vector.memset(q_stack[b][0:R_HI2, :].bitcast(F32), 0.0).then_inc(stacks_set, 1)
                    nc.vector.memset(q_stack[b][R_HI2:, :].bitcast(F32), 1.0).then_inc(stacks_set, 1)
                    nc.vector.memset(k_stack[b][0:R_HI2, :].bitcast(F32), 0.0).then_inc(stacks_set, 1)
                    nc.vector.memset(k_stack[b][R_MAX:, :].bitcast(F32), 1.0).then_inc(stacks_set, 1)
                dve.wait_ge(consts_in, 3 * 16)
                nc.vector.tensor_copy(after[:], after_wide[:]).then_inc(after_set, 1)
                nc.vector.tensor_copy(ident16[:], const["ident"][:]).then_inc(after_set, 1)
                for p in range(2):
                    nc.vector.memset(part_max[p][:], -BIG).then_inc(buffers_set, 1)
                    nc.vector.memset(o_rows[p][:], 0.0).then_inc(buffers_set, 1)
                dve.wait_ge(buffers_set, 4)
                dve.sem_inc(s_used, 2)

                def maxima(h, b, first, last):
                    for n in range(first, last):
                        t, k0, w = S_UNITS[n]
                        dve.wait_ge(s_ready, h * NSU + n + 1)
                        nc.vector.tensor_reduce(part_max[b % 2][:, k0 // (2 * CH), t:t + 1], s_bank[n % 2][:, 0:w],
                                                AX.X, ALU.max).then_inc(s_used, 1)
                    if last == NSU:
                        dve.wait_ge(s_used, h * NSU + NSU + 2)
                        nc.vector.tensor_tensor(row_max[b % 2][:], part_max[b % 2][:, 0, :], part_max[b % 2][:, 1, :],
                                                ALU.max).then_inc(max_ready, 1)

                def step(h, b, steps):
                    later = 1
                    for what in steps:
                        if what[0] == "s":
                            if what[1] == 0:
                                later = 2
                            maxima(h + later, b + later, what[1], what[1] + 1)

                maxima(0, 0, 0, NSU)
                maxima(1, 1, 0, AHEAD)
                with dve.Fori(0, HB // NB - 1) as i:
                    for b in range(NB):
                        step(i * NB + b, b, USUAL)
                for h in range(HB - NB, HB):
                    step(h, h % NB, order(h))
                dve.wait_ge(t_taken, HB * SLOTS + 1 + 2 - 1)
                for t in range(NT + 2):
                    p = t % 2
                    if t < NT:
                        nc.vector.reciprocal(inv[p][:], o_sums[:, t, :, DHB:]).then_inc(inv_done, 1)
                    if t >= 2:
                        dve.wait_ge(out_done, t - 1)
                        nc.vector.tensor_tensor(x[:, t - 2, :], x[:, t - 2, :], o_bank[p][:, 0:D], ALU.add).then_inc(x_done, 1)
                    if t < NT:
                        dve.wait_ge(inv_done, t + 1)
                        nc.vector.tensor_tensor(o[p][:].rearrange("p (h d) -> p h d", d=DHB), o_sums[:, t, :, 0:DHB],
                                                inv[p][:].to_broadcast([P, HB, DHB]), ALU.mult).then_inc(o_done, 1)


def experts(nc, tag, arg, x, xT, bank, w13, w2, load, store=None):
    with Phase(nc, tag) as phase:
        sb, sem = phase.sb, phase.sem

        gate_w = sb("gate_w", [P, KC, E])
        prior = sb("prior", [P, E])
        gates = sb("gates", [P, NT, EE])
        gate_in = sem("gate_in")
        gates_done = sem("gates_done")
        loaded = sem("loaded")

        with Phase(nc, tag + "g") as inner:
            sbi, semi = inner.sb, inner.sem

            top = sbi("top", [P, NT])
            prob = sbi("prob", [P, NT, E])
            biased = sbi("biased", [P, NT, E])
            better = sbi("better", [P, E, NT, E])
            rank = sbi("rank", [P, NT, E])
            logits_done = semi("logits_done")
            dve_step = semi("dve_step")
            shifted = semi("shifted")
            exp_done = semi("exp_done")
            with nc.Block() as block:
                @block.sync
                def _(sp):
                    sp.dma_start(gate_w[:], arg["gate_w"].rearrange("(c p) e -> p c e", p=P)).then_inc(gate_in, 16)
                    sp.dma_start(prior[:], arg["expert_bias"].partition_broadcast(P)).then_inc(gate_in, 16)
                    if load:
                        for c in range(KC):
                            rows = slice(c * P, (c + 1) * P)
                            for n, (routed, shared) in enumerate((("w1", "sw1"), ("w3", "sw3"))):
                                cols = slice(n * HID, (n + 1) * HID)
                                sp.dma_start(w13[:, c, 0:E, cols],
                                             arg[routed][:, rows, :].rearrange("e p f -> p e f")).then_inc(loaded, 16)
                                sp.dma_start(w13[:, c, E, cols], arg[shared][rows, :]).then_inc(loaded, 16)
                        for c in range(2):
                            rows = slice(c * HH, (c + 1) * HH)
                            sp.dma_start(w2[:, c, 0:E, :],
                                         arg["w2"][:, rows, :].rearrange("e p f -> p e f")).then_inc(loaded, 16)
                            sp.dma_start(w2[:, c, E, :], arg["sw2"][rows, :]).then_inc(loaded, 16)
                        sp.wait_ge(loaded, 12 * 16)

                @block.tensor
                def _(pe):
                    pe.wait_ge(gate_in, 2 * 16)
                    for t in range(NT):
                        for k in range(KC):
                            last = nc.tensor.matmul(bank[7][:, t * E:(t + 1) * E], xT[:, k, t * P:(t + 1) * P],
                                                    gate_w[:, k, :], start=k == 0, stop=k == KC - 1)
                    last.then_inc(logits_done, 1)

                @block.scalar
                def _(act):
                    act.wait_ge(shifted, 1)
                    nc.scalar.activation(prob[:], prob[:], ACT.Exp).then_inc(exp_done, 1)

                @block.vector
                def _(dve):
                    chain = Chain(dve, dve_step)
                    logits = bank[7][:, 0:NT * E].rearrange("p (t e) -> p t e", e=E)
                    wide = [P, NT, E]
                    chain.step(nc.vector.memset(gates[:, :, E], 1.0))
                    dve.wait_ge(logits_done, 1)
                    chain.step(nc.vector.tensor_reduce(top[:], logits, AX.X, ALU.max))
                    chain.wait()
                    nc.vector.tensor_tensor(prob[:], logits, top[:].unsqueeze(2).to_broadcast(wide),
                                            ALU.subtract).then_inc(shifted, 1)
                    dve.wait_ge(exp_done, 1)
                    chain.step(nc.vector.tensor_reduce(top[:], prob[:], AX.X, ALU.add))
                    chain.wait()
                    chain.step(nc.vector.reciprocal(top[:], top[:]))
                    chain.wait()
                    chain.step(nc.vector.tensor_tensor(prob[:], prob[:], top[:].unsqueeze(2).to_broadcast(wide), ALU.mult))
                    chain.wait()
                    chain.step(nc.vector.tensor_tensor(biased[:], prob[:], prior[:].unsqueeze(1).to_broadcast(wide), ALU.add))
                    chain.wait()
                    for e in range(E):
                        one = biased[:, :, e:e + 1]
                        n = e + 1
                        chain.step(nc.vector.tensor_tensor(better[:, e, :, 0:n], one.to_broadcast([P, NT, n]),
                                                           biased[:, :, 0:n], ALU.is_gt))
                        if n < E:
                            chain.step(nc.vector.tensor_tensor(better[:, e, :, n:E], one.to_broadcast([P, NT, E - n]),
                                                               biased[:, :, n:E], ALU.is_ge))
                    chain.wait()
                    chain.step(nc.vector.tensor_reduce(rank[:], better[:].rearrange("p e t f -> p t f e"), AX.X, ALU.add))
                    chain.wait()
                    nc.vector.scalar_tensor_tensor(out=gates[:, :, 0:E], in0=rank[:], scalar=float(TOPK), in1=prob[:],
                                                   op0=ALU.is_lt, op1=ALU.mult).then_inc(gates_done, 1)

        xs = [sb(f"xs{p}", [P, KC, P]) for p in range(2)]
        silu = [sb(f"silu{p}", [P, HID]) for p in range(2)]
        h = [sb(f"h{p}", [P, HID]) for p in range(2)]
        h_t = [sb(f"h_t{p}", [HH, 2, P]) for p in range(2)]
        staged = sem("staged")
        pool_go = sem("pool_go")
        up_done = sem("up_done")
        silu_done = sem("silu_done")
        h_done = sem("h_done")
        turned = sem("turned")
        h_t_done = sem("h_t_done")
        down_done = sem("down_done")
        x_done = sem("x_done")
        written = sem("written")
        up_bank, turn_bank, y_bank = bank[0:3], bank[3:5], bank[5:7]
        M = 2 * EE
        with nc.Block() as block:
            @block.gpsimd
            def _(pool):
                with pool.Fori(0, NT // 2) as i:
                    for p in range(2):
                        t = i * 2 + p
                        pool.wait_ge(up_done, (t + 1) * EE)
                        pool.sem_inc(pool_go, 1)
                        nc.gpsimd.tensor_copy(xs[p][:], xT[:, :, bass.ds(t * P, P)]).then_inc(staged, 1)

            @block.tensor
            def _(pe):
                pe.sem_inc(up_done, M)
                pe.sem_inc(turned, 2)
                with pe.Fori(0, NT // 2) as i:
                    for m in range(M + 2):
                        if m < M:
                            p, e = m // EE, m % EE
                            n = i * M + m
                            if e == 0:
                                pe.wait_ge(staged, i * 2 + p + 1)
                            pe.wait_ge(h_done, n + 1)
                            for k in range(KC):
                                last = nc.tensor.matmul(up_bank[m % 3][:, 0:2 * HID], xs[p][:, k, :], w13[:, k, e, :],
                                                        start=k == 0, stop=k == KC - 1)
                            last.then_inc(up_done, 1)
                        if 1 <= m <= M:
                            n = i * M + m - 1
                            j = (m - 1) % 2
                            pe.wait_ge(h_done, n + 4)
                            pe.wait_ge(h_t_done, n + 1)
                            for c in range(2):
                                last = nc.tensor.transpose(turn_bank[j][0:HH, c * P:(c + 1) * P],
                                                           h[j][:, c * HH:(c + 1) * HH], arg["ident_sb"][:])
                            last.then_inc(turned, 1)
                        if m >= 2:
                            p, e = (m - 2) // EE, (m - 2) % EE
                            n = i * M + m - 2
                            j = m % 2
                            pe.wait_ge(h_t_done, n + 3)
                            if e == 0:
                                pe.wait_ge(x_done, i * 2 + p + 1)
                            for c in range(2):
                                last = nc.tensor.matmul(y_bank[p][:, 0:D], h_t[j][:, c, :], w2[:, c, e, :],
                                                        start=e == 0 and c == 0, stop=e == EE - 1 and c == 1)
                            last.then_inc(down_done, 1)

            @block.scalar
            def _(act):
                act.sem_inc(h_t_done, 2)
                with act.Fori(0, NT // 2) as i:
                    for m in range(M + 1):
                        if m < M:
                            p, e = m // EE, m % EE
                            n = i * M + m
                            act.wait_ge(up_done, n + 1 + M)
                            act.wait_ge(h_done, n + 2)
                            nc.scalar.activation(silu[m % 2][:], up_bank[m % 3][:, 0:HID], ACT.Silu,
                                                 scale=gates[:, i * 2 + p, e:e + 1]).then_inc(silu_done, 1)
                        if m:
                            n = i * M + m - 1
                            j = (m - 1) % 2
                            act.wait_ge(turned, n + 3)
                            act.wait_ge(down_done, n + 1)
                            nc.scalar.activation(h_t[j][:], turn_bank[j][0:HH, 0:2 * P].rearrange("p (c n) -> p c n", c=2),
                                                 ACT.Copy).then_inc(h_t_done, 1)

            @block.vector
            def _(dve):
                dve.sem_inc(h_done, 3)
                dve.sem_inc(down_done, 2)
                dve.sem_inc(x_done, 2)

                def add(i, p):
                    t = i * 2 + p
                    dve.wait_ge(down_done, t * EE + EE + 2)
                    nc.vector.tensor_tensor(x[:, t, :], x[:, t, :], y_bank[p][:, 0:D], ALU.add).then_inc(x_done, 1)

                with dve.Fori(0, NT // 2) as i:
                    for m in range(M):
                        p, e = m // EE, m % EE
                        n = i * M + m
                        dve.wait_ge(silu_done, n + 1)
                        dve.wait_ge(turned, n + 1)
                        nc.vector.scalar_tensor_tensor(out=h[m % 2][:], in0=up_bank[m % 3][:, HID:2 * HID],
                                                       scalar=gates[:, i * 2 + p, e:e + 1], in1=silu[m % 2][:],
                                                       op0=ALU.mult, op1=ALU.mult).then_inc(h_done, 1)
                        if m == EE + 3:
                            add(i, 0)
                    add(i, 1)

            @block.sync
            def _(sp):
                if store is not None:
                    with sp.Fori(0, NT) as t:
                        sp.wait_ge(x_done, t + 3)
                        sp.dma_start(store[bass.ds(t * P, P), :], x[:, t, :]).then_inc(written, 16)
                    sp.wait_ge(written, 16 * NT)


def program(nc, arg, out):
    with ExitStack() as ctx:
        def sb(name, shape, dt=F32, scope=None):
            return (scope or ctx).enter_context(nc.sbuf_tensor(name, shape, dt))

        psum = ctx.enter_context(nc.psum_tensor("psum", [P, 8 * CH], F32))
        bank = [psum[:, n * CH:(n + 1) * CH] for n in range(8)]
        pair = [psum[:, n * 2 * CH:(n + 1) * 2 * CH] for n in range(2)]
        x = sb("x", [P, NT, D])
        xT = sb("xT", [P, KC, S])
        const = {"ident": sb("ident", [P, P]), "causal": sb("causal", [P, P], BF16), "mean": sb("mean", [P, P])}
        causal_wide = sb("causal_wide", [P, P])
        arg["ident_sb"] = const["ident"]
        x_in = ctx.enter_context(nc.semaphore("x_in"))
        with nc.Block() as block:
            @block.sync
            def _(sp):
                sp.dma_start(x[:], arg["hidden"].rearrange("(t p) d -> p t d", p=P)).then_inc(x_in, 16)
                sp.dma_start(const["ident"][:], arg["ident"]).then_inc(x_in, 16)
                sp.dma_start(causal_wide[:], arg["causal"]).then_inc(x_in, 16)
                sp.wait_ge(x_in, 3 * 16)

            @block.vector
            def _(dve):
                nc.vector.memset(const["mean"][:], 1.0 / S)
                dve.wait_ge(x_in, 3 * 16)
                nc.vector.tensor_copy(const["causal"][:], causal_wide[:])

        layernorm(nc, "ln1", x, xT, bank, const["ident"])
        with ExitStack() as a:
            bias = sb("bias", [P, TRI[NT]], BF16, a)
            empty = sb("empty", [P, NT], F32, a)
            filled = sb("filled", [P, NT], F32, a)
            index_mask(nc, arg, x, xT, bank, const, bias, empty, filled)
            k_hi = sb("ka_hi", [P, S], F32R, a)
            k_lo = sb("ka_lo", [P, S], F32R, a)
            c_stack = sb("c_stack", [P, NT, 2 * RANK], F32R, a)
            w_all = sb("w_all", [P, KC, HA, P], F32, a)
            w_out = sb("wa_out", [P, HA, D], F32, a)
            nowhere = sb("nowhere", [P, D], F32, a)
            rope = sb("rope", [P, 2, NT, HALF], F32, a)
            xT_rows = nc.dram_tensor("xT_rows", (P, KC, S), F32, kind="Internal").ap()
            prepare_a(nc, arg, x, xT, bank, const, k_hi, k_lo, c_stack, w_all, w_out, nowhere, rope, xT_rows)
            attention_a(nc, arg, x, xT, bank, const, k_hi, k_lo, c_stack, bias, empty, filled, w_all, w_out, nowhere, rope,
                        xT_rows)
        w13 = sb("w13", [P, KC, EE, 2 * HID])
        w2 = sb("w2", [HH, 2, EE, D])
        layernorm(nc, "ln2", x, xT, bank, const["ident"])
        experts(nc, "f1", arg, x, xT, bank, w13, w2, load=True)
        layernorm(nc, "ln3", x, xT, bank, const["ident"])
        stash = {name: nc.dram_tensor(f"stash_{name}", (D, S), F32, kind="Internal").ap()
                 for name in ("q_hi", "q_lo", "k_hi", "k_lo")}
        with ExitStack() as b:
            values = sb("values", [P, HB, NT, DHB + 1], F32, b)
            prepare_b(nc, arg, xT, bank, stash, values)
            max_rows = nc.dram_tensor("max_rows", (NT, P), F32, kind="Internal").ap()
            attention_b(nc, arg, x, xT, pair, bank, const, stash, max_rows, values)
        layernorm(nc, "ln4", x, xT, bank, const["ident"])
        experts(nc, "f2", arg, x, xT, bank, w13, w2, load=False, store=out)


def kernel(**inputs):
    import numpy as np
    import concourse.bacc as bacc
    from concourse.bass_utils import run_bass_kernel_spmd

    a = {k: np.asarray(v) for k, v in inputs.items()}
    A, B, M = "L0_attn_a_", "L0_attn_b_", "L0_ffn_"
    wq = a[A + "Wq"].reshape(D, HA, DN + DR)
    w_ukv = a[A + "W_ukv"].reshape(RANK, HA, DN + DV)
    lay = {
        "hidden": a[A + "hidden_states"].reshape(S, D),
        "Wq_idx": a[A + "Wq_idx"], "Wk_idx": a[A + "Wk_idx"],
        "bq_idx": a[A + "bq_idx"].reshape(HI, DI).T, "bk_idx": a[A + "bk_idx"].reshape(HI, DI).T,
        "idx_w": a[A + "idx_w"], "w_ctrl": a[A + "w_ctrl"].reshape(KC, P).T, "b_ctrl": a[A + "b_ctrl"].reshape(1),
        "Wq": a[A + "Wq"], "Wq_nope_T": wq[:, :, :DN].transpose(2, 1, 0),
        "W_uk_T": w_ukv[:, :, :DN].transpose(2, 1, 0), "W_uv_T": w_ukv[:, :, DN:].transpose(2, 1, 0),
        "Wo": a[A + "Wo"].reshape(HA, DV, D).transpose(1, 0, 2),
        "W_dkv": a[A + "W_dkv"], "kv_norm_w": a[A + "kv_norm_w"],
        "b_dkv_T": a[B + "w_dkv"].T, "b_q_T": a[B + "w_q"].T, "b_uk_T": a[B + "w_uk"].T,
        "b_uv_T": a[B + "w_uv"].T, "b_o_T": a[B + "w_o"].T,
        "gate_w": a[M + "gate_w"], "expert_bias": a[M + "expert_bias"],
        "w1": a[M + "w1"], "w2": a[M + "w2"], "w3": a[M + "w3"],
        "sw1": a[M + "sw1"], "sw2": a[M + "sw2"], "sw3": a[M + "sw3"],
    }
    inv_freq = (1.0 / 10000.0 ** (np.arange(0, DR, 2, dtype=np.float32) / DR)).astype(np.float32)
    angle = (np.arange(S, dtype=np.float32)[:, None] * inv_freq[None, :]).astype(np.float32)
    table = {"cos": np.cos(angle).astype(np.float32), "sin": np.sin(angle).astype(np.float32)}
    for name, value in table.items():
        tiles = value.reshape(NT, P, HALF).transpose(1, 0, 2)
        lay[name + "_k"] = tiles
        lay[name + "_q"] = (tiles * np.float32(SCALE_A)).astype(np.float32)
    row, col = np.arange(P)[:, None], np.arange(P)[None, :]
    lay["ident"] = np.eye(P, dtype=np.float32)
    lay["causal"] = np.where(col <= row, 0.0, NEG).astype(np.float32)
    lay["b_after"] = np.stack([np.where(col > row, HIDE, 0.0), np.where(row > col, HIDE, 0.0)], axis=1).astype(np.float32)
    lay["b_alibi"] = np.float32(SLOPE / (R_MAX - R_ALIBI)) * np.arange(S, dtype=np.float32)

    nc = bacc.Bacc("TRN2", target_bir_lowering=False, num_devices=1)
    arrays, arg = {}, {}
    for name, value in lay.items():
        value = np.ascontiguousarray(value)
        arrays[f"in_{name}"] = value
        arg[name] = nc.dram_tensor(f"in_{name}", value.shape, mybir.dt.from_np(value.dtype), kind="ExternalInput").ap()
    out = nc.dram_tensor("out", (S, D), F32, kind="ExternalOutput").ap()
    program(nc, arg, out)
    result = run_bass_kernel_spmd(nc, [arrays], core_ids=[0])
    return result.results[0]["out"].reshape(1, S, D)
```

```python
from contextlib import ExitStack

import concourse.bass as bass
from concourse import mybir

F32 = mybir.dt.float32
F32R = mybir.dt.float32r
BF16 = mybir.dt.bfloat16
U32 = mybir.dt.uint32
I32 = mybir.dt.int32
ALU = mybir.AluOpType
ACT = mybir.ActivationFunctionType
AX = mybir.AxisListType

P = 128
S = 2048
D = 256
NT = S // P
KC = D // P
CH = 512
NCH = S // CH
LN_EPS = 1e-5
NEG = -1.0e9

HA, DN, DR, DV, RANK = 16, 128, 64, 128, 64
HALF = DR // 2
HI, DI = 4, 64
RMS_EPS = 1e-6
GH = 4
LAG, FLIP_AT, SCORES_BY, Y_AT, PROJECT_AT = 3, 0.4, 0.75, (0.1, 0.3), 1 + 3e-6
SCALE_A = 1.0 / float(DN + DR) ** 0.5
HB = 16
DHB = D // HB
SLOPE = 0.0625
KVB = 128
SCALE_B = float(DHB) ** -0.5
R_LO, R_HI2, R_ALIBI, R_MAX = 16, 32, 48, 49
HIDE = -1.0e30
E, HID, TOPK = 8, 224, 2
EE = E + 1
HH = HID // 2
SLOTS = TOPK * S // P + E

GT = 8
TOP = 8
PROBES = 6
PROBE_STEPS = GT // 2 + 1 + 2 + 4 + 8
NEAR, EDGE = 0.4, 0.002
HALVINGS = 64
HALVING_STEPS = 2 + GT + 2 + 2
BIG = 3.0e38
ROUND = 12582912.0

TRI = [t * (t + 1) // 2 * P for t in range(NT + 1)]


class Chain:

    def __init__(self, eng, sem):
        self.eng, self.sem, self.n = eng, sem, 0

    def step(self, ins):
        ins.then_inc(self.sem, 1)
        self.n += 1

    def wait(self, back=0):
        self.eng.wait_ge(self.sem, self.n - back if back else self.n)


class Phase(ExitStack):

    def __init__(self, nc, tag):
        super().__init__()
        self.nc, self.tag, self.used = nc, tag, []

    def sb(self, name, shape, dt=F32):
        return self.enter_context(self.nc.sbuf_tensor(f"{self.tag}_{name}", shape, dt))

    def sem(self, name):
        self.used.append(self.enter_context(self.nc.semaphore(f"{self.tag}_{name}")))
        return self.used[-1]

    def __exit__(self, kind, *rest):
        if kind is None:
            with self.nc.Block() as block:
                @block.gpsimd
                def _(pool):
                    for one in self.used:
                        pool.sem_clear(one)
        return super().__exit__(kind, *rest)


def layernorm(nc, tag, x, xT, bank, ident, mean, rstd):
    DEEP = 4
    with Phase(nc, tag) as phase:
        sb, sem = phase.sb, phase.sem

        stats = sb("stats", [P, NT, 6])
        half = sb("half", [P, NT])
        var = sb("var", [P, NT])
        std = sb("std", [P, NT])
        xn = [sb(f"xn{p}", [P, D]) for p in range(DEEP)]
        stats_done = sem("stats_done")
        dve_step = sem("dve_step")
        var_ready = sem("var_ready")
        std_ready = sem("std_ready")
        xn_ready = sem("xn_ready")
        turned = sem("turned")
        stored = sem("stored")

        with nc.Block() as block:
            @block.vector
            def _(dve):
                with dve.Fori(0, NT // DEEP) as i:
                    for p in range(DEEP):
                        at = bass.ds(i * DEEP + p, 1)
                        nc.vector.bn_stats(stats[:, at, :], x[:, at, :]).then_inc(stats_done, 1)
                dve.wait_ge(stats_done, NT)
                chain = Chain(dve, dve_step)
                chain.step(nc.vector.tensor_tensor(mean[:], stats[:, :, 1], stats[:, :, 4], ALU.add))
                chain.step(nc.vector.tensor_tensor(half[:], stats[:, :, 1], stats[:, :, 4], ALU.subtract))
                chain.step(nc.vector.tensor_tensor(var[:], stats[:, :, 2], stats[:, :, 5], ALU.add))
                chain.wait()
                chain.step(nc.vector.tensor_scalar(mean[:], mean[:], 0.5, None, ALU.mult))
                chain.step(nc.vector.tensor_scalar(half[:], half[:], 0.5, None, ALU.mult))
                chain.step(nc.vector.tensor_scalar(var[:], var[:], 1.0 / D, LN_EPS, ALU.mult, ALU.add))
                chain.wait()
                chain.step(nc.vector.tensor_tensor(half[:], half[:], half[:], ALU.mult))
                chain.wait()
                nc.vector.tensor_tensor(var[:], var[:], half[:], ALU.add).then_inc(var_ready, 1)
                dve.wait_ge(std_ready, 1)
                chain.step(nc.vector.reciprocal(rstd[:], std[:]))
                chain.wait()
                with dve.Fori(0, NT // DEEP) as i:
                    for p in range(DEEP):
                        t = i * DEEP + p
                        dve.wait_ge(turned, t + 1)
                        nc.vector.tensor_scalar(xn[p][:], x[:, t, :], mean[:, bass.ds(t, 1)], rstd[:, bass.ds(t, 1)],
                                                ALU.subtract, ALU.mult).then_inc(xn_ready, 1)

            @block.scalar
            def _(act):
                act.wait_ge(var_ready, 1)
                nc.scalar.activation(std[:], var[:], ACT.Sqrt).then_inc(std_ready, 1)
                act.sem_inc(stored, DEEP)
                with act.Fori(0, NT // DEEP) as i:
                    for p in range(DEEP):
                        t = i * DEEP + p
                        act.wait_ge(turned, t + 1 + DEEP)
                        nc.scalar.activation(xT[:, :, bass.ds(t * P, P)],
                                             bank[p][:, 0:D].rearrange("p (c n) -> p c n", c=KC),
                                             ACT.Copy).then_inc(stored, 1)

            @block.tensor
            def _(pe):
                pe.sem_inc(turned, DEEP)
                with pe.Fori(0, NT // DEEP) as i:
                    for p in range(DEEP):
                        t = i * DEEP + p
                        pe.wait_ge(xn_ready, t + 1)
                        pe.wait_ge(stored, t + 1)
                        for c in range(KC):
                            last = nc.tensor.transpose(bank[p][:, c * P:(c + 1) * P], xn[p][:, c * P:(c + 1) * P],
                                                       ident[:])
                        last.then_inc(turned, 1)


def index_mask(nc, arg, x, xT, bank, const, bias, empty, filled, sent):
    with Phase(nc, "ix") as phase:
        sb, sem = phase.sb, phase.sem

        k_stack = sb("k_stack", [P, HI, S], F32R)
        k_lo = sb("k_lo", [P, HI // 2, S], F32R)
        q_stack = sb("q_stack", [P, HI, GT * P], F32R)
        kth = sb("kth", [P, 1])
        weight = sb("weight", [P, HI])
        w_q = sb("w_q", [P, KC, HI, 2, DI])
        b_q = sb("b_q", [P, HI])

        def high(h):
            return slice(h % 2 * DI, h % 2 * DI + DI)

        def low(h):
            return high(h + 1)

        with Phase(nc, "ixp") as inner:
            sbi, semi = inner.sb, inner.sem

            w_k = sbi("w_k", [P, KC, HI, 2, DI])
            b_k = sbi("b_k", [P, HI])
            ctrl = sbi("ctrl", [P, KC])
            ctrl_wide = sbi("ctrl_wide", [P, KC, P])
            bctrl = sbi("bctrl", [P, 1])
            zeros = sbi("zeros", [P, SLOTS // 4, D])
            pooled = sbi("pooled", [P, KC])
            z = sbi("z", [P, 1])
            ez = sbi("ez", [P, 1])
            loaded = semi("loaded")
            projected = semi("projected")
            high_done = semi("high_done")
            low_done = semi("low_done")
            pooled_ready = semi("pooled_ready")
            z_ready = semi("z_ready")
            zs_ready = semi("zs_ready")
            ez_ready = semi("ez_ready")
            dve_step = semi("dve_step")
            zeros_set = semi("zeros_set")
            zeros_out = semi("zeros_out")
            LOADS = 8 + 4 + 3
            with nc.Block() as block:
                @block.sync
                def _(sp):
                    for w, b, name in ((w_k, b_k, "k"), (w_q, b_q, "q")):
                        for half in range(2):
                            for c in range(KC):
                                sp.dma_start(w[:, c, :, half, :], arg[f"W{name}_idx"][c * P:(c + 1) * P, :].rearrange(
                                    "p (h d) -> p h d", h=HI)).then_inc(loaded, 16)
                    for half in range(2):
                        rows = slice(half * DI, half * DI + DI)
                        sp.dma_start(b_k[rows, :], arg["bk_idx"]).then_inc(loaded, 16)
                        sp.dma_start(b_q[rows, :], arg["bq_idx"]).then_inc(loaded, 16)
                    sp.dma_start(ctrl[:], arg["w_ctrl"]).then_inc(loaded, 16)
                    sp.dma_start(bctrl[:], arg["b_ctrl"].partition_broadcast(P)).then_inc(loaded, 16)
                    sp.dma_start(weight[:], arg["idx_w"].partition_broadcast(P)).then_inc(loaded, 16)
                    sp.wait_ge(zeros_set, 1)
                    for n in range(4):
                        sp.dma_start(sent[n * SLOTS // 4 * P:(n + 1) * SLOTS // 4 * P, :].rearrange("(n p) d -> p n d", p=P),
                                     zeros[:]).then_inc(zeros_out, 16)
                    sp.wait_ge(zeros_out, 4 * 16)
                    sp.wait_ge(loaded, LOADS * 16)

                @block.gpsimd
                def _(pool):
                    nc.gpsimd.memset(zeros[:], 0.0).then_inc(zeros_set, 1)

                @block.tensor
                def _(pe):
                    pe.wait_ge(loaded, LOADS * 16)
                    for n in range(HI * NCH):
                        h, c = divmod(n, NCH)
                        if n >= 4:
                            pe.wait_ge(low_done, n - 3)
                        for k in range(KC):
                            last = nc.tensor.matmul(bank[n % 4][:], w_k[:, k, h, :, :].rearrange("p a d -> p (a d)"),
                                                    xT[:, k, c * CH:(c + 1) * CH], start=k == 0, stop=k == KC - 1)
                        last.then_inc(projected, 1)
                    pe.wait_ge(pooled_ready, 1)
                    for k in range(KC):
                        last = nc.tensor.matmul(bank[4][:, 0:1], ctrl_wide[:, k, :], pooled[:, k:k + 1],
                                                start=k == 0, stop=k == KC - 1)
                    last.then_inc(z_ready, 1)

                @block.scalar
                def _(act):
                    act.wait_ge(loaded, LOADS * 16)
                    for n in range(HI * NCH):
                        h, c = divmod(n, NCH)
                        act.wait_ge(projected, n + 1)
                        nc.scalar.activation(k_stack[:, h, c * CH:(c + 1) * CH], bank[n % 4][:], ACT.Identity,
                                             bias=b_k[:, h:h + 1]).then_inc(high_done, 1)
                    act.wait_ge(zs_ready, 1)
                    nc.scalar.activation(ez[:], z[:], ACT.Exp, scale=-1.0).then_inc(ez_ready, 1)

                @block.vector
                def _(dve):
                    chain = Chain(dve, dve_step)
                    dve.wait_ge(loaded, LOADS * 16)
                    for k in range(KC):
                        chain.step(nc.vector.tensor_copy(ctrl_wide[:, k, :], ctrl[:, k:k + 1].to_broadcast([P, P])))
                    chain.wait()
                    nc.vector.tensor_reduce(pooled[:], xT[:], AX.X, ALU.add).then_inc(pooled_ready, 1)
                    for n in range(HI * NCH):
                        h, c = divmod(n, NCH)
                        rows, cols = high(h), slice(c * CH, (c + 1) * CH)
                        dve.wait_ge(high_done, n + 1)
                        nc.vector.scalar_tensor_tensor(out=k_lo[rows, h // 2, cols], in0=bank[n % 4][rows, :],
                                                       scalar=b_k[rows, h:h + 1], in1=k_stack[rows, h, cols].bitcast(F32),
                                                       op0=ALU.add, op1=ALU.subtract).then_inc(low_done, 1)
                    dve.wait_ge(z_ready, 1)
                    nc.vector.scalar_tensor_tensor(out=z[:], in0=bank[4][:, 0:1], scalar=1.0 / S, in1=bctrl[:],
                                                   op0=ALU.mult, op1=ALU.add).then_inc(zs_ready, 1)
                    dve.wait_ge(ez_ready, 1)
                    chain.step(nc.vector.tensor_scalar(ez[:], ez[:], 1.0, None, ALU.add))
                    chain.wait()
                    chain.step(nc.vector.reciprocal(ez[:], ez[:]))
                    chain.wait()
                    chain.step(nc.vector.tensor_scalar(ez[:], ez[:], float(S), None, ALU.mult))
                    chain.wait()
                    chain.step(nc.vector.tensor_scalar(ez[:], ez[:], ROUND, None, ALU.add))
                    chain.wait()
                    chain.step(nc.vector.tensor_scalar(ez[:], ez[:], ROUND, None, ALU.subtract))
                    chain.wait()
                    chain.step(nc.vector.tensor_scalar(kth[:], ez[:], 1.0, float(S), ALU.max, ALU.min))
                    chain.wait()

        scores = sb("scores", [P, GT, S])
        qs = [sb(f"qs{p}", [P, HI, P], F32R) for p in range(2)]
        spare = x[:].rearrange("p t d -> p (t d)")
        relu = spare[:, 0:2 * (HI - 1) * CH].rearrange("p (a h n) -> p a h n", a=2, h=HI - 1)
        masked = spare[:, 0:S]
        junk_act = spare[:, S:S + S // 2].bitcast(BF16)
        row = {name: sb(name, [P, GT]) for name in (
            "low", "high", "lo", "hi", "above", "at_least", "at_lo", "at_hi", "tiny", "zeros", "count", "signs", "nonzero",
            "part", "step", "mid", "neg_mid", "outside", "rank", "bad", "more", "thr")}
        flag = {name: sb(name, [P, GT], U32) for name in ("pos", "neg", "at_zero", "enough", "short")}
        aim = sb("aim", [P, 1])
        shift = sb("shift", [P, GT])
        places = sb("places", [P, TOP])
        best = sb("best", [P, GT, TOP])
        pick = sb("pick", [P, GT, TOP])
        bad_row = sb("bad_row", [P, 1])
        unsolved = sb("unsolved", [P, 1], I32)
        top = sb("top", [P, NT])
        for g in range(NT // GT):
            index_scores(nc, f"ixs{g}", g, xT, bank, w_q, b_q, q_stack, k_stack, k_lo, qs, relu, weight, scores, high, low)
            index_threshold(nc, f"ixt{g}", g, bank, const, scores, kth, masked, junk_act, row, flag, aim, shift,
                            places, best, pick, bad_row, unsolved, top, bias, empty, filled)


def index_scores(nc, tag, g, xT, bank, w_q, b_q, q_stack, k_stack, k_lo, qs, relu, weight, scores, high, low):
    with Phase(nc, tag) as phase:
        sem = phase.sem

        projected = sem("projected")
        high_done = sem("high_done")
        low_done = sem("low_done")
        staged = sem("staged")
        dotted = sem("dotted")
        first_used = sem("first_used")
        relu_done = sem("relu_done")
        summed = sem("summed")
        weighed = sem("weighed")
        joined = sem("joined")
        LAST = HI - 1
        QC = GT * P // CH
        with nc.Block() as block:
            @block.gpsimd
            def _(pool):
                pool.wait_ge(low_done, HI * QC)

                def stage(t, p):
                    pool.wait_ge(dotted, (t + 1) * NCH * HI)
                    nc.gpsimd.tensor_copy(qs[p][:], q_stack[:, :, slice(t * P, t * P + P) if isinstance(t, int) else
                                                            bass.ds(t * P, P)].bitcast(F32)).then_inc(staged, 1)

                def join(t):
                    for c in range(NCH):
                        n = t * NCH + c
                        into = scores[:, t, c * CH:(c + 1) * CH]
                        term = relu[:, c % 2, LAST - 1, :]
                        pool.wait_ge(weighed, n + 1)
                        pool.wait_ge(summed, n * (HI - 2) + HI - 2 + 2 * (HI - 2))
                        nc.gpsimd.tensor_tensor(into, into, term, ALU.add).then_inc(joined, 1)

                pool.sem_inc(joined, 2)
                for t in range(2):
                    stage(t, t)
                with pool.Fori(0, GT // 2 - 1) as i:
                    for p in range(2):
                        join(i * 2 + p)
                        stage(i * 2 + p + 2, p)
                for t in range(GT - 2, GT):
                    join(t)

            @block.tensor
            def _(pe):
                pe.sem_inc(dotted, NCH * HI * 2)
                for n in range(HI * QC):
                    h, c = divmod(n, QC)
                    for k in range(KC):
                        last = nc.tensor.matmul(bank[n][:], w_q[:, k, h, :, :].rearrange("p a d -> p (a d)"),
                                                xT[:, k, g * GT * P + c * CH:g * GT * P + (c + 1) * CH],
                                                start=k == 0, stop=k == KC - 1)
                    last.then_inc(projected, 1)
                with pe.Fori(0, GT // 2) as i:
                    for p in range(2):
                        t = i * 2 + p
                        pe.wait_ge(staged, t + 1)
                        for c in range(NCH):
                            n = t * NCH + c
                            cols = slice(c * CH, (c + 1) * CH)
                            pe.wait_ge(first_used, n + 1)
                            pe.wait_ge(relu_done, n * (HI - 1) + 1 + HI - 2)
                            for h in range(HI):
                                out = bank[c % 2 * HI + h]
                                nc.tensor.matmul(out[:], qs[p][:, h, :], k_stack[:, h, cols], start=True, stop=False)
                                nc.tensor.matmul(out[:], qs[p][high(h), h, :], k_lo[high(h), h // 2, cols],
                                                 start=False, stop=True).then_inc(dotted, 1)

            @block.scalar
            def _(act):
                for n in range(HI * QC):
                    h, c = divmod(n, QC)
                    act.wait_ge(projected, n + 1)
                    nc.scalar.activation(q_stack[:, h, c * CH:(c + 1) * CH], bank[n][:], ACT.Identity,
                                         bias=b_q[:, h:h + 1]).then_inc(high_done, 1)
                act.sem_inc(relu_done, 2 * (HI - 1))
                with act.Fori(0, GT) as t:
                    for c in range(NCH):
                        n = t * NCH + c
                        act.wait_ge(summed, n * (HI - 2) + HI - 2)
                        act.wait_ge(joined, n + 1)
                        for h in range(1, HI):
                            act.wait_ge(dotted, n * HI + h + 1 + NCH * HI * 2)
                            nc.scalar.activation(relu[:, c % 2, h - 1, :], bank[c % 2 * HI + h][:],
                                                 ACT.Relu).then_inc(relu_done, 1)
                        act.wait_ge(relu_done, (n + 1) * (HI - 1) + 2 * (HI - 1))
                        nc.scalar.activation(relu[:, c % 2, LAST - 1, :], relu[:, c % 2, LAST - 1, :], ACT.Copy,
                                             scale=weight[:, LAST:HI]).then_inc(weighed, 1)

            @block.vector
            def _(dve):
                for n in range(HI * QC):
                    h, c = divmod(n, QC)
                    rows, cols = low(h), slice(c * CH, (c + 1) * CH)
                    dve.wait_ge(high_done, n + 1)
                    nc.vector.scalar_tensor_tensor(out=q_stack[rows, h, cols], in0=bank[n][rows, :],
                                                   scalar=b_q[rows, h:h + 1], in1=q_stack[rows, h, cols].bitcast(F32),
                                                   op0=ALU.add, op1=ALU.subtract).then_inc(low_done, 1)
                dve.sem_inc(first_used, 2)
                dve.sem_inc(summed, 2 * (HI - 2))
                with dve.Fori(0, GT) as t:
                    for c in range(NCH):
                        n = t * NCH + c
                        into = scores[:, t, c * CH:(c + 1) * CH]
                        dve.wait_ge(dotted, n * HI + 1 + NCH * HI * 2)
                        nc.vector.tensor_scalar(into, bank[c % 2 * HI][:], 0.0, weight[:, 0:1],
                                                ALU.max, ALU.mult).then_inc(first_used, 1)
                        dve.wait_ge(first_used, n + 3)
                        for h in range(1, LAST):
                            dve.wait_ge(relu_done, n * (HI - 1) + h + 2 * (HI - 1))
                            if h > 1:
                                dve.wait_ge(summed, n * (HI - 2) + h - 1 + 2 * (HI - 2))
                            nc.vector.scalar_tensor_tensor(out=into, in0=relu[:, c % 2, h - 1, :], scalar=weight[:, h:h + 1],
                                                           in1=into, op0=ALU.mult, op1=ALU.add).then_inc(summed, 1)


def index_threshold(nc, tag, g, bank, const, scores, kth, masked, junk_act, row, flag, aim, shift, places, best, pick,
                    bad_row, unsolved, top, bias, empty, filled):
    other = slice(GT // 2, GT)
    junk = [bias[:, TRI[g * GT] + p * S:TRI[g * GT] + (p + 1) * S] for p in range(2)]
    with Phase(nc, tag) as phase:
        sem = phase.sem

        dve_step = sem("dve_step")
        zero_step = sem("zero_step")
        mid_ready = sem("mid_ready")
        go = sem("go")
        sign_done = sem("sign_done")
        bad_ready = sem("bad_ready")
        summed = sem("summed")
        halved = sem("halved")
        with nc.Block() as block:
            @block.scalar
            def _(act):
                for j in range(GT):
                    if j:
                        act.wait_ge(zero_step, 2 * j)
                    nc.scalar.activation(junk_act, scores[:, j, :], ACT.Sign,
                                         accum_out=row["signs"][:, j:j + 1]).then_inc(zero_step, 1)
                    act.wait_ge(zero_step, 2 * j + 1)
                    nc.scalar.activation(junk_act, junk_act, ACT.Abs,
                                         accum_out=row["nonzero"][:, j:j + 1]).then_inc(zero_step, 1)
                act.wait_ge(zero_step, 2 * GT)
                with act.Fori(0, PROBES) as r:
                    act.wait_ge(mid_ready, r + 1)
                    for j in range(GT // 2, GT):
                        if j > GT // 2:
                            act.wait_ge(sign_done, r * (GT // 2) + j - GT // 2)
                        nc.scalar.activation(junk_act, scores[:, j, :], ACT.Sign, bias=row["neg_mid"][:, j:j + 1],
                                             accum_out=row["signs"][:, j:j + 1]).then_inc(sign_done, 1)

            @block.tensor
            def _(pe):
                pe.wait_ge(bad_ready, 1)
                nc.tensor.matmul(bank[7][:, 0:1], const["mean"][:], bad_row[:], start=True, stop=True).then_inc(summed, 1)

            @block.vector
            def _(dve):
                chain = Chain(dve, dve_step)
                step, wait = chain.step, chain.wait
                scalar, tensor, fill, copy = nc.vector.tensor_scalar, nc.vector.tensor_tensor, nc.vector.memset, nc.vector.tensor_copy
                at = {name: t[:] for name, t in {**row, **flag}.items()}

                def choose(into, where, value):
                    dve.sem_inc(go, 1)
                    step(nc.vector.copy_predicated(at[into], at[where], at[value]))

                def probe(first):
                    wait()
                    step(scalar(at["part"], at["at_lo"], aim[:, 0:1], None, ALU.subtract))
                    step(tensor(at["step"], at["at_lo"], at["at_hi"], ALU.subtract))
                    wait()
                    step(nc.vector.reciprocal(at["step"], at["step"]))
                    wait()
                    step(tensor(at["part"], at["part"], at["step"], ALU.mult))
                    wait()
                    if first:
                        step(scalar(at["part"], at["part"], NEAR, None, ALU.mult))
                        wait()
                        step(tensor(at["part"], at["part"], shift[:], ALU.add))
                        wait()
                    step(scalar(at["part"], at["part"], EDGE, 1.0 - EDGE, ALU.max, ALU.min))
                    step(tensor(at["step"], at["hi"], at["lo"], ALU.subtract))
                    wait()
                    step(tensor(at["step"], at["step"], at["part"], ALU.mult))
                    wait()
                    step(tensor(at["mid"], at["step"], at["lo"], ALU.add))
                    wait()
                    scalar(at["neg_mid"], at["mid"], -1.0, None, ALU.mult).then_inc(mid_ready, 1)

                step(nc.vector.tensor_reduce(at["low"], scores[:], AX.X, ALU.min))
                step(nc.vector.tensor_reduce(at["high"], scores[:], AX.X, ALU.max))
                step(fill(at["tiny"], 1.2e-38))
                step(fill(at["zeros"], 0.0))
                step(fill(at["at_lo"], float(S)))
                step(fill(at["at_hi"], 0.0))
                step(scalar(aim[:], kth[:], (TOP + 1) / 2.0, None, ALU.subtract))
                for n in range(TOP):
                    step(fill(places[:, n:n + 1], n + 1.0))
                wait()
                step(tensor(at["step"], at["high"], at["low"], ALU.subtract))
                wait()
                step(nc.vector.scalar_tensor_tensor(out=at["high"], in0=at["step"], scalar=2.0 ** -10, in1=at["high"],
                                                    op0=ALU.mult, op1=ALU.add))
                wait()
                step(scalar(at["high"], at["high"], 1e-30, None, ALU.add))
                dve.wait_ge(zero_step, 2 * GT)
                step(tensor(at["above"], at["nonzero"], at["signs"], ALU.add))
                step(tensor(at["at_least"], at["signs"], at["nonzero"], ALU.subtract))
                wait()
                step(scalar(at["above"], at["above"], 0.5, None, ALU.mult))
                step(scalar(at["at_least"], at["at_least"], 0.5, float(S), ALU.mult, ALU.add))
                step(copy(at["lo"], at["low"]))
                step(copy(at["hi"], at["high"]))
                wait()
                step(scalar(at["pos"], at["above"], kth[:, 0:1], None, ALU.is_ge))
                step(scalar(at["neg"], at["at_least"], kth[:, 0:1], None, ALU.is_lt))
                step(scalar(at["outside"], at["above"], kth[:, 0:1], None, ALU.is_ge))
                step(scalar(shift[:], at["at_least"], kth[:, 0:1], None, ALU.is_lt))
                wait()
                choose("lo", "pos", "tiny")
                choose("at_lo", "pos", "above")
                choose("hi", "neg", "zeros")
                choose("at_hi", "neg", "at_least")
                step(tensor(at["outside"], at["outside"], shift[:], ALU.add))
                wait()
                step(scalar(shift[:], shift[:], 1.0 - NEAR, None, ALU.mult))
                step(scalar(at["at_zero"], at["outside"], 0.5, None, ALU.is_lt))
                probe(first=True)
                before = chain.n
                with dve.Fori(0, PROBES) as r:
                    chain.n = r * PROBE_STEPS + before
                    dve.wait_ge(mid_ready, r + 1)
                    for j in range(GT // 2):
                        chain.wait(back=1 if j else 0)
                        step(scalar(junk[j % 2], scores[:, j, :], row["mid"][:, j:j + 1], 0.0, ALU.is_ge, ALU.add,
                                    accum_out=row["count"][:, j:j + 1]))
                    dve.wait_ge(sign_done, r * (GT // 2) + GT // 2)
                    step(scalar(row["count"][:, other], row["signs"][:, other], 0.5, S / 2.0, ALU.mult, ALU.add))
                    wait()
                    step(scalar(at["enough"], at["count"], kth[:, 0:1], None, ALU.is_ge))
                    step(scalar(at["short"], at["count"], kth[:, 0:1], None, ALU.is_lt))
                    wait()
                    choose("lo", "enough", "mid")
                    choose("at_lo", "enough", "count")
                    choose("hi", "short", "mid")
                    choose("at_hi", "short", "count")
                    probe(first=False)
                chain.n = before + PROBES * PROBE_STEPS
                wait()
                for j in range(GT):
                    if j < GT // 2:
                        step(scalar(junk[j % 2], scores[:, j, :], row["hi"][:, j:j + 1], None, ALU.is_ge))
                    else:
                        step(scalar(junk[j % 2], scores[:, j, :], row["hi"][:, j:j + 1], 0.0, ALU.is_ge, ALU.add,
                                    accum_out=row["at_hi"][:, j:j + 1]))
                    wait()
                    step(nc.vector.scalar_tensor_tensor(out=masked, in0=junk[j % 2], scalar=-BIG, in1=scores[:, j, :],
                                                        op0=ALU.mult, op1=ALU.add))
                    wait()
                    step(nc.vector.max(best[:, j, :], masked))
                wait()
                step(scalar(at["rank"], at["at_hi"], -1.0, kth[:, 0:1], ALU.mult, ALU.add))
                wait()
                wide = [P, GT, TOP]
                step(tensor(pick[:], places[:].unsqueeze(1).to_broadcast(wide), row["rank"][:].unsqueeze(2).to_broadcast(wide),
                            ALU.is_equal))
                step(scalar(at["bad"], at["rank"], TOP + 0.5, None, ALU.is_gt))
                step(scalar(at["more"], at["rank"], 0.5, None, ALU.is_lt))
                wait()
                step(tensor(pick[:], pick[:], best[:], ALU.mult))
                step(tensor(at["bad"], at["bad"], at["more"], ALU.add))
                wait()
                step(nc.vector.tensor_reduce(at["thr"], pick[:], AX.X, ALU.add))
                step(tensor(at["bad"], at["bad"], at["outside"], ALU.mult))
                wait()
                nc.vector.tensor_reduce(bad_row[:], at["bad"], AX.X, ALU.max).then_inc(bad_ready, 1)
                choose("thr", "at_zero", "zeros")
                dve.wait_ge(summed, 1)
                step(scalar(unsolved[:], bank[7][:, 0:1], 0.0, None, ALU.is_gt))
                wait()
                some = dve.value_load(unsolved[0:1, 0:1], min_val=0, max_val=1)
                with dve.If(some > 0):
                    halve = Chain(dve, halved)
                    halve.step(copy(at["lo"], at["low"]))
                    halve.step(copy(at["hi"], at["high"]))
                    start = halve.n
                    with dve.Fori(0, HALVINGS) as r:
                        halve.n = r * HALVING_STEPS + start
                        halve.wait()
                        halve.step(tensor(at["mid"], at["lo"], at["hi"], ALU.add))
                        halve.wait()
                        halve.step(scalar(at["mid"], at["mid"], 0.5, None, ALU.mult))
                        for j in range(GT):
                            halve.wait()
                            halve.step(scalar(junk[0], scores[:, j, :], row["mid"][:, j:j + 1], 0.0, ALU.is_ge, ALU.add,
                                              accum_out=row["count"][:, j:j + 1]))
                        halve.wait()
                        halve.step(scalar(at["enough"], at["count"], kth[:, 0:1], None, ALU.is_ge))
                        halve.step(scalar(at["short"], at["count"], kth[:, 0:1], None, ALU.is_lt))
                        halve.wait()
                        for into, where in (("lo", "enough"), ("hi", "short")):
                            dve.sem_inc(go, 1)
                            halve.step(nc.vector.copy_predicated(at[into], at[where], at["mid"]))
                    halve.n = start + HALVINGS * HALVING_STEPS
                    halve.wait()
                    halve.step(copy(at["thr"], at["lo"]))
                    halve.wait()
                for j in range(GT):
                    t = g * GT + j
                    step(scalar(bias[:, TRI[t]:TRI[t + 1]], scores[:, j, 0:(t + 1) * P], row["thr"][:, j:j + 1], NEG,
                                ALU.is_lt, ALU.mult))
                wait()
                for j in range(GT):
                    t = g * GT + j
                    diag = bias[:, TRI[t + 1] - P:TRI[t + 1]]
                    step(tensor(diag, diag, const["causal"][:], ALU.min))
                wait()
                for j in range(GT):
                    t = g * GT + j
                    step(nc.vector.tensor_reduce(top[:, t:t + 1], bias[:, TRI[t]:TRI[t + 1]], AX.X, ALU.max))
                wait()
                rows = slice(g * GT, (g + 1) * GT)
                step(scalar(empty[:, rows], top[:, rows], 0.5 * NEG, None, ALU.is_lt))
                step(scalar(filled[:, rows], top[:, rows], 0.5 * NEG, None, ALU.is_ge))


def prepare_a(nc, arg, x, xT, bank, const, k_hi, k_lo, c_stack, w_all, w_out, nowhere, rope, xT_rows):
    with Phase(nc, "pa") as phase:
        sb, sem = phase.sb, phase.sem

        wq_n = sb("wq_n", [P, HA, D])
        w_uk = sb("w_uk", [P, HA, RANK])
        w_uv = sb("w_uv", [P, HA, 2, RANK])
        keys = sb("keys", [P, NT, P])
        mean_c = sb("mean_c", [RANK, P])
        wo = sb("wo", [P, HA, D])
        w_dkv = sb("w_dkv", [P, KC, RANK + DR])
        norm_w = sb("norm_w", [P, RANK])
        cos = sb("cos", [P, NT, HALF])
        sin = sb("sin", [P, NT, HALF])
        raw = sb("raw", [P, NT, P])
        sq = sb("sq", [P, NT, RANK])
        ss = sb("ss", [P, NT])
        rms = sb("rms", [P, NT])
        tmp = [sb(f"tmp{n}", [P, NT, HALF]) for n in range(4)]
        weights_in = sem("weights_in")
        x_in = sem("x_in")
        dkv_in = sem("dkv_in")
        tables_in = sem("tables_in")
        kv_done = sem("kv_done")
        kv_stored = sem("kv_stored")
        absorbed = sem("absorbed")
        absorbed_stored = sem("absorbed_stored")
        dve_step = sem("dve_step")
        ss_ready = sem("ss_ready")
        rms_ready = sem("rms_ready")
        keys_ready = sem("keys_ready")
        turned = sem("turned")
        hi_done = sem("hi_done")
        c_done = sem("c_done")
        lo_done = sem("lo_done")
        mean_done = sem("mean_done")
        mean_stored = sem("mean_stored")

        with nc.Block() as block:
            @block.sync
            def _(sp):
                sp.dma_start(w_dkv[:], arg["W_dkv"].rearrange("(c p) n -> p c n", p=P)).then_inc(dkv_in, 16)
                sp.dma_start(norm_w[:], arg["kv_norm_w"].partition_broadcast(P)).then_inc(tables_in, 16)
                sp.dma_start(cos[:], arg["cos_k"]).then_inc(tables_in, 16)
                sp.dma_start(sin[:], arg["sin_k"]).then_inc(tables_in, 16)
                sp.dma_start(wq_n[:], arg["Wq_nope_T"]).then_inc(weights_in, 16)
                sp.dma_start(w_uk[:], arg["W_uk_T"]).then_inc(weights_in, 16)
                for n in range(2):
                    sp.dma_start(w_uv[:, :, n, :], arg["W_uv_T"]).then_inc(weights_in, 16)
                sp.dma_start(wo[:], arg["Wo"]).then_inc(weights_in, 16)
                for c in range(KC):
                    sp.dma_start(w_all[:, c, :, RANK:], arg["Wq"][c * P:(c + 1) * P, :].rearrange(
                        "p (h d) -> p h d", h=HA)[:, :, DN:]).then_inc(weights_in, 16)
                sp.dma_start(rope[:, 0], arg["cos_q"]).then_inc(weights_in, 16)
                sp.dma_start(rope[:, 1], arg["sin_q"]).then_inc(weights_in, 16)
                sp.dma_start(x[:], arg["hidden"].rearrange("(t p) d -> p t d", p=P)).then_inc(x_in, 16)
                sp.dma_start(xT_rows, xT[:]).then_inc(x_in, 16)
                sp.wait_ge(weights_in, 9 * 16)
                sp.wait_ge(x_in, 2 * 16)

            @block.tensor
            def _(pe):
                pe.wait_ge(dkv_in, 16)
                for t in range(NT):
                    for k in range(KC):
                        last = nc.tensor.matmul(bank[t // 4][:, t % 4 * P:(t % 4 + 1) * P], xT[:, k, t * P:(t + 1) * P],
                                                w_dkv[:, k, :], start=k == 0, stop=k == KC - 1)
                    if t % 4 == 3:
                        last.then_inc(kv_done, 1)
                pe.wait_ge(weights_in, 9 * 16)
                for n in range(HA * KC):
                    h, c = n // KC, n % KC
                    last = nc.tensor.matmul(bank[4 + n // 8][:, n % 8 * RANK:(n % 8 + 1) * RANK],
                                            wq_n[:, h, c * P:(c + 1) * P], w_uk[:, h, :], start=True, stop=True)
                    if n % 8 == 7:
                        last.then_inc(absorbed, 1)
                for n in range(HA // 2):
                    pe.wait_ge(absorbed_stored, n + 1)
                    for j in range(2):
                        last = nc.tensor.matmul(bank[4 + n % 4][:, j * D:(j + 1) * D],
                                                w_uv[:, 2 * n + j, :, :].rearrange("p a r -> p (a r)"), wo[:, 2 * n + j, :],
                                                start=True, stop=True)
                    last.then_inc(absorbed, 1)
                pe.wait_ge(keys_ready, 1)
                for t in range(NT):
                    last = nc.tensor.transpose(bank[t // 4][:, t % 4 * P:(t % 4 + 1) * P], keys[:, t, :], const["ident"][:])
                    if t % 4 == 3:
                        last.then_inc(turned, 1)
                pe.wait_ge(absorbed_stored, 4 + HA // 2)
                for t in range(NT):
                    last = nc.tensor.matmul(bank[4][0:RANK, 0:P], keys[:, t, 0:RANK], const["mean"][:],
                                            start=t == 0, stop=t == NT - 1)
                last.then_inc(mean_done, 1)
                pe.wait_ge(mean_stored, 1)
                for h in range(HA):
                    last = nc.tensor.matmul(bank[5][:, 0:D], mean_c[:], w_out[0:RANK, h, :], start=h == 0, stop=h == HA - 1)
                last.then_inc(mean_done, 1)

            @block.scalar
            def _(act):
                for n in range(4):
                    act.wait_ge(kv_done, n + 1)
                    nc.scalar.activation(raw[:, 4 * n:4 * n + 4, :], bank[n][:].rearrange("p (t n) -> p t n", t=4),
                                         ACT.Copy).then_inc(kv_stored, 1)
                act.wait_ge(ss_ready, 1)
                nc.scalar.activation(rms[:], ss[:], ACT.Sqrt).then_inc(rms_ready, 1)
                for n in range(4):
                    act.wait_ge(absorbed, n + 1)
                    for c in range(KC):
                        last = nc.scalar.activation(
                            w_all[:, c, 4 * n:4 * n + 4, 0:RANK],
                            bank[4 + n][:].rearrange("p (h c r) -> p c h r", c=KC, r=RANK)[:, c], ACT.Copy, scale=SCALE_A)
                    last.then_inc(absorbed_stored, 1)
                for n in range(HA // 2):
                    act.wait_ge(absorbed, 4 + n + 1)
                    nc.scalar.activation(w_out[:, 2 * n:2 * n + 2, :], bank[4 + n % 4].rearrange("p (a n) -> p a n", a=2),
                                         ACT.Copy).then_inc(absorbed_stored, 1)
                act.wait_ge(keys_ready, 1)
                nc.scalar.activation(c_stack[:, :, 0:RANK], keys[:, :, 0:RANK], ACT.Copy).then_inc(c_done, 1)
                for n in range(4):
                    act.wait_ge(turned, n + 1)
                    nc.scalar.activation(k_hi[:, n * CH:(n + 1) * CH], bank[n][:], ACT.Copy).then_inc(hi_done, 1)
                act.wait_ge(mean_done, 1)
                nc.scalar.activation(mean_c[:], bank[4][0:RANK, 0:P], ACT.Copy).then_inc(mean_stored, 1)
                act.wait_ge(mean_done, 2)
                nc.scalar.activation(nowhere[:], bank[5][:, 0:D], ACT.Copy)

            @block.vector
            def _(dve):
                chain = Chain(dve, dve_step)
                dve.wait_ge(kv_stored, 4)
                dve.wait_ge(tables_in, 3 * 16)
                chain.step(nc.vector.tensor_tensor(sq[:], raw[:, :, 0:RANK], raw[:, :, 0:RANK], ALU.mult))
                chain.wait()
                chain.step(nc.vector.tensor_reduce(ss[:], sq[:], AX.X, ALU.add))
                chain.wait()
                nc.vector.tensor_scalar(ss[:], ss[:], 1.0 / RANK, RMS_EPS, ALU.mult, ALU.add).then_inc(ss_ready, 1)
                r1, r2 = raw[:, :, RANK:RANK + HALF], raw[:, :, RANK + HALF:]
                chain.step(nc.vector.tensor_tensor(tmp[0][:], r1, cos[:], ALU.mult))
                chain.step(nc.vector.tensor_tensor(tmp[1][:], r2, sin[:], ALU.mult))
                chain.step(nc.vector.tensor_tensor(tmp[2][:], r2, cos[:], ALU.mult))
                chain.step(nc.vector.tensor_tensor(tmp[3][:], r1, sin[:], ALU.mult))
                chain.wait()
                chain.step(nc.vector.tensor_tensor(keys[:, :, RANK:RANK + HALF], tmp[0][:], tmp[1][:], ALU.subtract))
                chain.step(nc.vector.tensor_tensor(keys[:, :, RANK + HALF:], tmp[2][:], tmp[3][:], ALU.add))
                dve.wait_ge(rms_ready, 1)
                chain.step(nc.vector.reciprocal(rms[:], rms[:]))
                chain.wait()
                chain.step(nc.vector.tensor_tensor(sq[:], raw[:, :, 0:RANK],
                                                   rms[:].unsqueeze(2).to_broadcast([P, NT, RANK]), ALU.mult))
                chain.wait()
                nc.vector.tensor_tensor(keys[:, :, 0:RANK], sq[:],
                                        norm_w[:].unsqueeze(1).to_broadcast([P, NT, RANK]), ALU.mult).then_inc(keys_ready, 1)
                for n in range(4):
                    dve.wait_ge(hi_done, n + 1)
                    part = slice(n * CH, (n + 1) * CH)
                    nc.vector.tensor_tensor(k_lo[:, part], bank[n][:], k_hi[:, part].bitcast(F32),
                                            ALU.subtract).then_inc(lo_done, 1)
                dve.wait_ge(c_done, 1)
                nc.vector.tensor_tensor(c_stack[:, :, RANK:], keys[:, :, 0:RANK], c_stack[:, :, 0:RANK].bitcast(F32),
                                        ALU.subtract).then_inc(lo_done, 1)


def attention_a(nc, arg, x, xT, bank, const, k_hi, k_lo, c_stack, bias, empty, filled, w_all, w_out, nowhere, rope, xT_rows):
    NG = HA // GH
    chunks = [(t + 4) // 4 for t in range(NT)]
    QB = [GH * sum(chunks[:t]) for t in range(NT + 1)]
    TB = [t * (t + 1) // 2 for t in range(NT + 1)]
    QN, TN = QB[NT], TB[NT]
    RING = 4

    with Phase(nc, "aa") as phase:
        sb, sem = phase.sb, phase.sem
        xt = [sb(f"xt{p}", [P, KC, P]) for p in range(2)]
        q_nat = sb("q_nat", [P, GH, P])
        tmp = [sb(f"tmp{n}", [P, GH, HALF]) for n in range(4)]
        q_hi = [sb(f"q_hi{p}", [P, GH * P], F32R) for p in range(2)]
        q_lo = [sb(f"q_lo{p}", [P, GH * P], F32R) for p in range(2)]
        prob = [[sb(f"prob0{h}", [P, S - P])[:] for h in range(GH)],
                [xT[:, h, :] for h in range(KC)] + [sb(f"prob1{h}", [P, S])[:] for h in range(KC, GH)]]
        pt_hi = [sb(f"pt_hi{n}", [P, GH * P], F32R) for n in range(RING)]
        pt_lo = [sb(f"pt_lo{n}", [P, GH * P], F32R) for n in range(RING)]
        out_t = sb("out_t", [P, GH * P])
        chunk_max = [sb(f"chunk_max{p}", [P, GH, NCH]) for p in range(2)]
        neg_max = [sb(f"neg_max{p}", [P, GH]) for p in range(2)]
        total = [sb(f"total{p}", [P, GH]) for p in range(2)]
        inv = [sb(f"inv{p}", [P, GH]) for p in range(2)]

        xt_in = [sem(f"xt_in{p}") for p in range(2)]
        q_proj = sem("q_proj")
        q_nat_ready = sem("q_nat_ready")
        roped = sem("roped")
        q_turned = sem("q_turned")
        q_hi_done = sem("q_hi_done")
        q_lo_done = sem("q_lo_done")
        scores_ready = sem("scores_ready")
        scores_out = sem("scores_out")
        take_go = sem("take_go")
        max_ready = sem("max_ready")
        exp_done = sem("exp_done")
        turned = sem("turned")
        pt_hi_done = sem("pt_hi_done")
        pt_lo_done = sem("pt_lo_done")
        pv_done = sem("pv_done")
        kept = sem("kept")
        total_turned = sem("total_turned")
        inv_done = sem("inv_done")
        y_ready = sem("y_ready")
        x_added = sem("x_added")
        nowhere_added = sem("nowhere_added")
        score_bank, turn_bank, out_bank = bank[0:2], bank[2:2 + RING], bank[6]
        y_bank = q_bank = bank[7]

        def plan(t, left, scored, flipped, queried):
            todo = []
            for j in range(t + 1):
                todo.append((j / (t + 1), ("turn", j)))
                todo.append(((j + LAG) / (t + 1) + 2e-6, ("weigh", j)))
            if left:
                todo += [(Y_AT[pair], ("y", pair)) for pair in range(GH // 2)]
            if scored:
                n = GH * chunks[(t + 1) % NT]
                for k in range(n):
                    todo.append(((k + 0.5) / n * SCORES_BY, ("score", *divmod(k, chunks[(t + 1) % NT]))))
            if flipped:
                todo.append((FLIP_AT, ("flip",)))
            if queried:
                todo.append((PROJECT_AT, ("project",)))
            return [what for _, what in sorted(todo, key=lambda one: one[0])]

        def behind(steps, lags):
            mine = [(n + lags[what[0]], n, what) for n, what in enumerate(steps) if what[0] in lags]
            return [what for _, _, what in sorted(mine)]

        def walk(eng, before, step, finish):
            def passes(i, last):
                for t in range(NT):
                    ahead = [(i + (t + n) // NT, (t + n) % NT) for n in (1, 2, 3)]
                    there = [not last or t + n < NT for n in (1, 2, 3)]
                    step(i, t, ahead, plan(t, t > 0, *there))
                finish(i)
            before()
            with eng.Fori(0, NG - 1) as i:
                passes(i, False)
            passes(NG - 1, True)

        with nc.Block() as block:
            @block.sync
            def _(sp):
                def load(i, t):
                    g = i * NT + t
                    sp.wait_ge(q_proj, g + 1)
                    sp.dma_start(xt[t % 2][:], xT_rows[:, :, t * P:(t + 1) * P]).then_inc(xt_in[t % 2], 16)

                with sp.Fori(0, NG) as i:
                    for t in range(NT):
                        load(i, t)

            @block.gpsimd
            def _(pool):
                def rotate(i, t):
                    g = i * NT + t
                    cos = rope[:, 0, t, :].unsqueeze(1).to_broadcast([P, GH, HALF])
                    sin = rope[:, 1, t, :].unsqueeze(1).to_broadcast([P, GH, HALF])
                    r1, r2 = q_nat[:, :, RANK:RANK + HALF], q_nat[:, :, RANK + HALF:]
                    pool.wait_ge(q_nat_ready, g + 1)
                    pool.wait_ge(roped, g * 6 + 1)
                    for n, (r, table) in enumerate(((r1, cos), (r2, sin), (r2, cos), (r1, sin))):
                        nc.gpsimd.tensor_tensor(tmp[n][:], r, table, ALU.mult).then_inc(roped, 1)
                    pool.wait_ge(roped, g * 6 + 4 + 1)
                    nc.gpsimd.tensor_tensor(r1, tmp[0][:], tmp[1][:], ALU.subtract).then_inc(roped, 1)
                    nc.gpsimd.tensor_tensor(r2, tmp[2][:], tmp[3][:], ALU.add).then_inc(roped, 1)

                pool.sem_inc(roped, 1)
                with pool.Fori(0, NG) as i:
                    for t in range(NT):
                        rotate(i, t)

            @block.tensor
            def _(pe):
                def project(i, t):
                    g = i * NT + t
                    pe.wait_ge(xt_in[t % 2], (i * (NT // 2) + t // 2) * 16 + 16)
                    pe.wait_ge(q_lo_done, g + 1)
                    heads = w_all[:].rearrange("p c h d -> p c (h d)")
                    first = i * GH * P
                    for k in range(KC):
                        cols = slice(first, first + GH * P) if isinstance(i, int) else bass.ds(first, GH * P)
                        last = nc.tensor.matmul(q_bank[:], xt[t % 2][:, k, :], heads[:, k, cols],
                                                start=k == 0, stop=k == KC - 1)
                    last.then_inc(q_proj, 1)

                def flip(i, t):
                    g = i * NT + t
                    pe.wait_ge(roped, g * 6 + 6 + 1)
                    pe.wait_ge(x_added, (g - 2) * GH + 4 * GH)
                    for h in range(GH):
                        last = nc.tensor.transpose(q_bank[:, h * P:(h + 1) * P], q_nat[:, h, :], const["ident"][:])
                    last.then_inc(q_turned, 1)

                def score(i, t, h, c):
                    g, n = i * NT + t, i * QN + QB[t] + h * chunks[t] + c
                    w = min(CH, (t + 1) * P - c * CH)
                    if h == 0 and c == 0:
                        pe.wait_ge(q_lo_done, g + 1 + 1)
                    pe.wait_ge(scores_out, n + 1)
                    out = score_bank[(QB[t] + h * chunks[t] + c) % 2]
                    cols, head = slice(c * CH, c * CH + w), slice(h * P, (h + 1) * P)
                    nc.tensor.matmul(out[:, 0:w], q_hi[t % 2][:, head], k_hi[:, cols], start=True, stop=False)
                    nc.tensor.matmul(out[:, 0:w], q_hi[t % 2][:, head], k_lo[:, cols], start=False, stop=False)
                    nc.tensor.matmul(out[:, 0:w], q_lo[t % 2][:, head], k_hi[:, cols], start=False,
                                     stop=True).then_inc(scores_ready, 1)

                def turn(i, t, j):
                    g, n = i * NT + t, i * TN + TB[t] + j
                    if j == 0:
                        pe.wait_ge(exp_done, g * GH + GH)
                    pe.wait_ge(pt_lo_done, n + 1)
                    for h in range(GH):
                        last = nc.tensor.transpose(turn_bank[(TB[t] + j) % RING][:, h * P:(h + 1) * P],
                                                   prob[t % 2][h][:, j * P:(j + 1) * P], const["ident"][:])
                    last.then_inc(turned, 1)

                def weigh(i, t, j):
                    g, n = i * NT + t, i * TN + TB[t] + j
                    out, ring = out_bank, (TB[t] + j) % RING
                    pe.wait_ge(pt_lo_done, n + 1 + RING)
                    if j == 0:
                        pe.wait_ge(kept, g + 1)
                    nc.tensor.matmul(out[:], c_stack[:, j, :], pt_hi[ring][:], start=j == 0, stop=j == t,
                                     skip_group_check=True)
                    nc.tensor.matmul(out[0:RANK, :], c_stack[:, j, 0:RANK], pt_lo[ring][:], start=False, stop=j == t,
                                     skip_group_check=True).then_inc(pv_done, 1)

                def leave(i, t, pair):
                    g = i * NT + t
                    pe.wait_ge(kept, g + 1 + 1)
                    if pair == 0:
                        pe.wait_ge(q_nat_ready, min(g + 4, NG * NT) if isinstance(g, int) else g + 4)
                    pe.wait_ge(x_added, g * GH + 2 * pair + 4 * GH)
                    for h in range(2 * pair, 2 * pair + 2):
                        head = i * GH + h
                        last = nc.tensor.matmul(y_bank[:, h % 2 * D:(h % 2 + 1) * D], out_t[:, h * P:(h + 1) * P],
                                                w_out[:, head if isinstance(head, int) else bass.ds(head, 1), :],
                                                start=True, stop=True)
                    last.then_inc(y_ready, 1)

                def before():
                    pe.sem_inc(q_proj, 2)
                    pe.sem_inc(turned, TN)
                    pe.sem_inc(pv_done, RING)
                    pe.sem_inc(y_ready, GH // 2)
                    pe.sem_inc(scores_ready, QN)
                    for t in range(2):
                        project(0, t)
                        flip(0, t)
                    project(0, 2)
                    for h in range(GH):
                        score(0, 0, h, 0)

                def step(i, t, ahead, steps):
                    for what in steps:
                        if what[0] == "project":
                            project(*ahead[2])
                        elif what[0] == "flip":
                            flip(*ahead[1])
                        elif what[0] == "score":
                            score(*ahead[0], *what[1:])
                        elif what[0] == "turn":
                            turn(i, t, what[1])
                        elif what[0] == "weigh":
                            weigh(i, t, what[1])
                        else:
                            leave(i, t - 1, what[1])

                def finish(i):
                    for pair in range(GH // 2):
                        leave(i, NT - 1, pair)

                walk(pe, before, step, finish)

            @block.scalar
            def _(act):
                def store_queries(i, t):
                    g = i * NT + t
                    act.wait_ge(q_proj, g + 1 + 2)
                    act.wait_ge(q_turned, g + 1)
                    nc.scalar.activation(q_nat[:], q_bank.rearrange("p (h d) -> p h d", h=GH),
                                         ACT.Copy).then_inc(q_nat_ready, 1)

                def split_queries(i, t):
                    g = i * NT + t
                    act.wait_ge(q_turned, g + 1 + 1)
                    act.wait_ge(scores_ready, i * QN + (QB[t - 1] if t else QB[NT - 1] - QN) + QN)
                    nc.scalar.activation(q_hi[t % 2][:], q_bank, ACT.Copy).then_inc(q_hi_done, 1)

                def exponentials(i, t, h):
                    g, L = i * NT + t, (t + 1) * P
                    act.wait_ge(max_ready, g * GH + h + 1)
                    if h == 0:
                        act.wait_ge(inv_done, g + 1)
                    nc.scalar.activation(prob[t % 2][h][:, 0:L], prob[t % 2][h][:, 0:L], ACT.Exp,
                                         bias=neg_max[t % 2][:, h:h + 1],
                                         accum_out=total[t % 2][:, h:h + 1]).then_inc(exp_done, 1)

                def split_turned(i, t, j):
                    n = i * TN + TB[t] + j
                    act.wait_ge(turned, n + 1 + TN)
                    act.wait_ge(pv_done, n + 1)
                    nc.scalar.activation(pt_hi[(TB[t] + j) % RING][:], turn_bank[(TB[t] + j) % RING], ACT.Copy).then_inc(pt_hi_done, 1)

                def keep(i, t):
                    g = i * NT + t
                    act.wait_ge(pv_done, i * TN + TB[t + 1] + RING)
                    act.wait_ge(y_ready, (g + 1) * (GH // 2))
                    nc.scalar.activation(out_t[:], out_bank, ACT.Copy).then_inc(kept, 1)

                def before():
                    act.sem_inc(q_turned, 1)
                    act.sem_inc(kept, 1)
                    for t in range(2):
                        store_queries(0, t)
                        split_queries(0, t)
                    store_queries(0, 2)
                    for h in range(GH):
                        exponentials(0, 0, h)

                def step(i, t, ahead, steps):
                    for what in behind(steps, {"project": 0, "flip": 0, "score": 4, "turn": 0}):
                        if what[0] == "project":
                            store_queries(*ahead[2])
                        elif what[0] == "flip":
                            split_queries(*ahead[1])
                        elif what[0] == "turn":
                            split_turned(i, t, what[1])
                        elif what[2] == chunks[ahead[0][1]] - 1:
                            exponentials(*ahead[0], what[1])
                    keep(i, t)

                walk(act, before, step, lambda i: None)

            @block.vector
            def _(dve):
                def split_queries(i, t):
                    dve.wait_ge(q_hi_done, i * NT + t + 1)
                    nc.vector.tensor_tensor(q_lo[t % 2][:], q_bank, q_hi[t % 2][:].bitcast(F32),
                                            ALU.subtract).then_inc(q_lo_done, 1)

                def take(i, t, h, c):
                    g, n = i * NT + t, i * QN + QB[t] + h * chunks[t] + c
                    w = min(CH, (t + 1) * P - c * CH)
                    if h == 0 and c == 0:
                        dve.wait_ge(turned, i * TN + (TB[t - 1] if t else TB[NT - 1] - TN) + TN)
                    dve.wait_ge(scores_ready, n + 1 + QN)
                    dve.sem_inc(take_go, 1)
                    nc.vector.tensor_tensor_reduce(prob[t % 2][h][:, c * CH:c * CH + w],
                                                   score_bank[(QB[t] + h * chunks[t] + c) % 2][:, 0:w],
                                                   bias[:, TRI[t] + c * CH:TRI[t] + c * CH + w], 1.0, -BIG, ALU.add, ALU.max,
                                                   chunk_max[t % 2][:, h, c:c + 1]).then_inc(scores_out, 1)
                    if c == chunks[t] - 1:
                        dve.wait_ge(scores_out, n + 1 + 2)
                        nc.vector.tensor_reduce(neg_max[t % 2][:, h:h + 1], chunk_max[t % 2][:, h, 0:c + 1], AX.X, ALU.max,
                                                negate=True).then_inc(max_ready, 1)

                def split_turned(i, t, j):
                    n = i * TN + TB[t] + j
                    ring = (TB[t] + j) % RING
                    dve.wait_ge(pt_hi_done, n + 1)
                    nc.vector.tensor_tensor(pt_lo[ring][:], turn_bank[(TB[t] + j) % RING], pt_hi[ring][:].bitcast(F32),
                                            ALU.subtract).then_inc(pt_lo_done, 1)

                def invert(i, t):
                    g = i * NT + t
                    dve.wait_ge(exp_done, g * GH + GH)
                    dve.wait_ge(x_added, (g - 1) * GH + 4 * GH)
                    nc.vector.reciprocal(inv[t % 2][:], total[t % 2][:]).then_inc(total_turned, 1)
                    dve.wait_ge(total_turned, g + 1)
                    nc.vector.tensor_scalar(inv[t % 2][:], inv[t % 2][:], filled[:, t:t + 1], None,
                                            ALU.mult).then_inc(inv_done, 1)

                def add(i, t, pair):
                    g = i * NT + t
                    dve.wait_ge(y_ready, (g + 1) * (GH // 2) + pair + 1)
                    dve.wait_ge(inv_done, g + 1 + 2)
                    for h in range(2 * pair, 2 * pair + 2):
                        dve.wait_ge(x_added, g * GH + h + 4 * GH)
                        nc.vector.scalar_tensor_tensor(out=x[:, t, :], in0=y_bank[:, h % 2 * D:(h % 2 + 1) * D],
                                                       scalar=inv[t % 2][:, h:h + 1], in1=x[:, t, :],
                                                       op0=ALU.mult, op1=ALU.add).then_inc(x_added, 1)

                def before():
                    dve.sem_inc(q_lo_done, 1)
                    dve.sem_inc(scores_out, 2)
                    dve.sem_inc(pt_lo_done, RING)
                    dve.sem_inc(inv_done, 2)
                    dve.sem_inc(x_added, 4 * GH)
                    for t in range(NT):
                        nc.vector.scalar_tensor_tensor(out=x[:, t, :], in0=nowhere[:], scalar=empty[:, t:t + 1], in1=x[:, t, :],
                                                       op0=ALU.mult, op1=ALU.add).then_inc(nowhere_added, 1)
                    dve.wait_ge(nowhere_added, NT)
                    for t in range(2):
                        split_queries(0, t)
                    for h in range(GH):
                        take(0, 0, h, 0)

                def step(i, t, ahead, steps):
                    invert(i, t)
                    for what in behind(steps, {"flip": 1, "score": 0, "turn": 3, "y": 1}):
                        if what[0] == "flip":
                            split_queries(*ahead[1])
                        elif what[0] == "score":
                            take(*ahead[0], *what[1:])
                        elif what[0] == "turn":
                            split_turned(i, t, what[1])
                        else:
                            add(i, t - 1, what[1])

                def finish(i):
                    for pair in range(GH // 2):
                        add(i, NT - 1, pair)

                walk(dve, before, step, finish)


def prepare_b(nc, arg, xT, bank, stash, values):
    with Phase(nc, "pb") as phase:
        sb, sem = phase.sb, phase.sem
        w_dkv = sb("w_dkv", [P, KC, KVB])
        w_q = sb("w_q", [P, KC, D])
        w_uk = sb("w_uk", [P, D])
        w_uv = sb("w_uv", [P, D])
        c_kv = sb("c_kv", [P, S])
        part = {name: sb(name, [P, KC, S], F32R) for name in ("q_hi", "q_lo", "k_hi", "k_lo")}
        loaded = sem("loaded")
        done = sem("done")
        stored = sem("stored")
        lo_done = sem("lo_done")
        stashed = sem("stashed")
        ones_done = sem("ones_done")
        RING = 4
        FIRST_Q, FIRST_K, FIRST_V, ALL = NCH, NCH + KC * NCH, NCH + 2 * KC * NCH, NCH + 2 * KC * NCH + NT // 2
        with nc.Block() as block:
            @block.sync
            def _(sp):
                sp.dma_start(w_dkv[:], arg["b_dkv_T"].rearrange("(c p) n -> p c n", p=P)).then_inc(loaded, 16)
                sp.dma_start(w_q[:], arg["b_q_T"].rearrange("(c p) n -> p c n", p=P)).then_inc(loaded, 16)
                sp.dma_start(w_uk[:], arg["b_uk_T"]).then_inc(loaded, 16)
                sp.dma_start(w_uv[:], arg["b_uv_T"]).then_inc(loaded, 16)
                for n in range(2 * KC):
                    name, m = "qk"[n // KC], n % KC
                    sp.wait_ge(lo_done, NCH * (n + 1))
                    for which in ("_hi", "_lo"):
                        sp.dma_start(stash[name + which][m * P:(m + 1) * P, :], part[name + which][:, m, :].bitcast(F32)).then_inc(stashed, 16)
                sp.wait_ge(stashed, 2 * 2 * KC * 16)

            @block.gpsimd
            def _(pool):
                nc.gpsimd.memset(values[:, :, :, DHB:], 1.0).then_inc(ones_done, 1)

            @block.tensor
            def _(pe):
                pe.wait_ge(loaded, 4 * 16)
                for n in range(ALL):
                    if n >= RING:
                        pe.wait_ge(stored, n - RING + 1)
                    if FIRST_Q <= n - RING < FIRST_V:
                        pe.wait_ge(lo_done, n - RING - FIRST_Q + 1)
                    out = bank[n % RING]
                    if n < FIRST_Q:
                        for k in range(KC):
                            last = nc.tensor.matmul(out[:], w_dkv[:, k, :], xT[:, k, n * CH:(n + 1) * CH],
                                                    start=k == 0, stop=k == KC - 1)
                    elif n < FIRST_K:
                        m, c = divmod(n - FIRST_Q, NCH)
                        for k in range(KC):
                            last = nc.tensor.matmul(out[:], w_q[:, k, m * P:(m + 1) * P], xT[:, k, c * CH:(c + 1) * CH],
                                                    start=k == 0, stop=k == KC - 1)
                    elif n < FIRST_V:
                        m, c = divmod(n - FIRST_K, NCH)
                        pe.wait_ge(stored, NCH)
                        last = nc.tensor.matmul(out[:], w_uk[:, m * P:(m + 1) * P], c_kv[:, c * CH:(c + 1) * CH],
                                                start=True, stop=True)
                    else:
                        for j in range(2):
                            t = 2 * (n - FIRST_V) + j
                            last = nc.tensor.matmul(out[:, j * D:(j + 1) * D], c_kv[:, t * P:(t + 1) * P], w_uv[:],
                                                    start=True, stop=True)
                    last.then_inc(done, 1)

            @block.scalar
            def _(act):
                for n in range(ALL):
                    act.wait_ge(done, n + 1)
                    have = bank[n % RING][:]
                    if n < FIRST_Q:
                        into, scale = c_kv[:, n * CH:(n + 1) * CH], 1.0
                    elif n < FIRST_V:
                        m, c = divmod((n - FIRST_Q) % (KC * NCH), NCH)
                        name, scale = ("q_hi", SCALE_B) if n < FIRST_K else ("k_hi", 1.0)
                        into = part[name][:, m, c * CH:(c + 1) * CH]
                    else:
                        t = 2 * (n - FIRST_V)
                        into, scale = values[:, :, t:t + 2, 0:DHB].rearrange("p h t d -> p t h d"), 1.0
                        have = have.rearrange("p (t h d) -> p t h d", t=2, d=DHB)
                    nc.scalar.activation(into, have, ACT.Copy, scale=scale).then_inc(stored, 1)

            @block.vector
            def _(dve):
                for n in range(FIRST_Q, FIRST_V):
                    m, c = divmod((n - FIRST_Q) % (KC * NCH), NCH)
                    name, scale = ("q", SCALE_B) if n < FIRST_K else ("k", 1.0)
                    dve.wait_ge(stored, n + 1)
                    cols = slice(c * CH, (c + 1) * CH)
                    nc.vector.scalar_tensor_tensor(out=part[name + "_lo"][:, m, cols], in0=bank[n % RING][:], scalar=scale,
                                                   in1=part[name + "_hi"][:, m, cols].bitcast(F32),
                                                   op0=ALU.mult, op1=ALU.subtract).then_inc(lo_done, 1)


def attention_b(nc, arg, x, xT, bank2, bank, const, stash, max_rows, values):
    NB = 4
    DEEP, LATE = 4, 5
    with Phase(nc, "ab") as phase:
        sb, sem = phase.sb, phase.sem
        q_stack = [sb(f"q_stack{p}", [P, S], F32R) for p in range(NB)]
        k_stack = [sb(f"k_stack{p}", [P, S], F32R) for p in range(NB)]
        after_wide = sb("after_wide", [P, 2, P])
        after = sb("after", [P, 2, P], BF16)
        ident16 = sb("ident16", [P, P], BF16)
        same = xT
        w_out = sb("w_out", [P, KC, D])
        part_max = [sb(f"part_max{p}", [P, 2, NT]) for p in range(2)]
        row_max = [sb(f"row_max{p}", [P, NT]) for p in range(2)]
        neg_max = [sb(f"neg_max{p}", [NT, P], F32R) for p in range(2)]
        prob = [sb(f"prob{n}", [P, CH]) for n in range(4)]
        v_stack = [sb(f"v_stack{p}", [P, NT, DHB + 1]) for p in range(NB)]
        o_rows = [sb(f"o_rows{p}", [P, CH]) for p in range(2)]
        o_sums = sb("o_sums", [P, NT, HB, DHB + 1])
        inv = [sb(f"inv{p}", [P, HB, 1]) for p in range(DEEP)]
        o = [xT[:, 0, p * D:(p + 1) * D] for p in range(DEEP)]
        o_t = [xT[:, 1, p * D:(p + 1) * D].rearrange("p (c n) -> p c n", c=KC) for p in range(DEEP)]
        consts_in = sem("consts_in")
        same_loaded = sem("same_loaded")
        same_set = sem("same_set")
        w_out_in = sem("w_out_in")
        same_in = sem("same_in")
        after_set = sem("after_set")
        staged = [sem(f"staged{p}") for p in range(NB)]
        s_ready = sem("s_ready")
        s_used = sem("s_used")
        max_ready = sem("max_ready")
        max_out = sem("max_out")
        max_in = sem("max_in")
        t_ready = sem("t_ready")
        t_taken = sem("t_taken")
        pv_done = sem("pv_done")
        kept = sem("kept")
        buffers_set = sem("buffers_set")
        inv_done = sem("inv_done")
        o_done = sem("o_done")
        o_turned = sem("o_turned")
        o_t_done = sem("o_t_done")
        out_done = sem("out_done")
        x_done = sem("x_done")

        s_bank, t_bank, o_bank = bank2, bank[4:6], bank[6:8]
        turn_bank, out_bank = bank[0:DEEP], bank[DEEP:2 * DEEP]
        S_UNITS = [(t, 2 * CH * n, min(2 * CH, (t + 1) * P - 2 * CH * n))
                   for t in reversed(range(NT)) for n in range((t + 8) // 8)]
        T_UNITS = [(c, kb, max(c * CH, kb * P), (c + 1) * CH - max(c * CH, kb * P))
                   for c in range(NCH) for kb in range(4 * (c + 1))]
        NSU, NTU = len(S_UNITS), len(T_UNITS)
        AHEAD = 7
        ENDS = [sum(4 * (k + 1) for k in range(c + 1)) for c in range(NCH)]
        SLOTS = NTU + 1 + NCH

        def order(h):
            todo = [n % NSU for n in range(AHEAD, AHEAD + NSU) if h + 1 + n // NSU < HB]
            columns = sum(S_UNITS[n][2] for n in todo)
            steps, sent, turn_at = [], 0, None
            for n in range(NTU + 2):
                if n < NTU:
                    steps.append(("t", n))
                while len(todo) > (1 if h + 2 < HB else 0) and sent < columns * (n + 1) / (NTU + 2):
                    one = todo.pop(0)
                    sent += S_UNITS[one][2]
                    steps.append(("s", one))
                    if one == NSU - 1:
                        turn_at = n + 3
                if n == turn_at:
                    steps.append(("turn",))
                if n >= 2:
                    steps.append(("weigh", n - 2))
                if n - 4 in ENDS[:-1]:
                    steps.append(("flip", ENDS.index(n - 4)))
            if turn_at is not None and turn_at >= NTU + 2:
                steps.append(("turn",))
            return steps + [("s", n) for n in todo] + [("flip", NCH - 1)]

        def slots(steps):
            return {what: n for n, what in enumerate(w for w in steps if w[0] in ("t", "turn", "flip"))}

        USUAL = order(0)
        TURN = slots(USUAL)[("turn",)]

        with nc.Block() as block:
            @block.sync
            def _(sp):
                sp.dma_start(same[0:2, :, :], arg["b_same"]).then_inc(same_loaded, 16)
                sp.dma_start(after_wide[:], arg["b_after"]).then_inc(consts_in, 16)
                sp.dma_start(w_out[:], arg["b_o_T"].rearrange("(c p) n -> p c n", p=P)).then_inc(w_out_in, 16)

                def stage(h, b):
                    rows = slice(h * DHB, (h + 1) * DHB) if isinstance(h, int) else bass.ds(h * DHB, DHB)
                    for stack, first, name in ((q_stack, 0, "q_hi"), (q_stack, R_LO, "q_lo"), (q_stack, R_HI2, "q_hi"),
                                               (k_stack, 0, "k_hi"), (k_stack, R_LO, "k_hi"), (k_stack, R_HI2, "k_lo")):
                        sp.dma_start(stack[b][first:first + DHB, :].bitcast(F32), stash[name][rows, :]).then_inc(staged[b], 16)
                    sp.dma_start(v_stack[b][:], values[:, h if isinstance(h, int) else bass.ds(h, 1), :, :]).then_inc(staged[b], 16)

                def send_max(h, slot, b):
                    sp.wait_ge(t_taken, slot + 1 + 2)
                    sp.dma_start(max_rows, neg_max[b % 2][:].bitcast(F32)).then_inc(max_out, 16)
                    sp.wait_ge(max_out, h * 16 + 16)
                    sp.dma_start(q_stack[b][R_MAX:R_MAX + 1, :].bitcast(F32),
                                 max_rows.rearrange("t q -> (t q)").unsqueeze(0)).then_inc(max_in, 16)
                    sp.wait_ge(max_in, h * 16 + 16)

                stage(0, 0)
                sp.wait_ge(same_set, 2)
                for b in range(NB):
                    for stack in (q_stack, k_stack):
                        sp.dma_start(stack[b][R_ALIBI:R_MAX + 1, :].bitcast(F32),
                                     stack[NB - 1][0:2, :].bitcast(F32)).then_inc(same_in, 16)
                for h in range(1, NB - 1):
                    stage(h, h)
                sp.wait_ge(same_in, 2 * NB * 16)
                stage(NB - 1, NB - 1)
                send_max(0, 0, 0)
                with sp.Fori(0, HB // NB - 1) as i:
                    for b in range(NB):
                        h = i * NB + b
                        send_max(h + 1, h * SLOTS + 1 + TURN, (b + 1) % NB)
                        sp.wait_ge(pv_done, (h + 1) * NTU + 4)
                        stage(h + NB, b)
                for h in range(HB - NB, HB - 1):
                    send_max(h + 1, h * SLOTS + 1 + slots(order(h))[("turn",)], (h + 1) % NB)

            @block.tensor
            def _(pe):
                pe.sem_inc(pv_done, 4)

                def s_piece(h, b, n, turn):
                    t, k0, w = S_UNITS[n]
                    if n == 0:
                        pe.wait_ge(staged[b], turn * 7 * 16 + 7 * 16)
                    pe.wait_ge(s_used, h * NSU + n + 1)
                    for c in range(0, w, CH):
                        cw = min(CH, w - c)
                        diag = k0 + c + cw == (t + 1) * P
                        if diag:
                            nc.tensor.matmul(s_bank[n % 2][:, c + cw - P:c + cw], ident16[:], after[:, 0, :],
                                             start=True, stop=False, skip_group_check=True)
                        last = nc.tensor.matmul(s_bank[n % 2][:, c:c + cw], q_stack[b][0:R_MAX, t * P:(t + 1) * P],
                                                k_stack[b][0:R_MAX, k0 + c:k0 + c + cw], start=not diag, stop=True,
                                                skip_group_check=True)
                    last.then_inc(s_ready, 1)

                def turn_max(h, b, slot, bank_of):
                    pe.wait_ge(max_ready, h + 1)
                    pe.wait_ge(t_taken, slot + 1)
                    nc.tensor.transpose(bank_of[0:NT, 0:P], row_max[b % 2][:], const["ident"][:]).then_inc(t_ready, 1)

                def t_piece(h, b, n, slot, bank_of):
                    c, kb, q0, w = T_UNITS[n]
                    if n == 0:
                        pe.wait_ge(max_in, h * 16 + 16)
                    pe.wait_ge(t_taken, slot + 1)
                    diag = kb >= 4 * c
                    if diag:
                        nc.tensor.matmul(bank_of[:, 0:P], ident16[:], after[:, 1, :], start=True, stop=False,
                                         skip_group_check=True)
                    last = nc.tensor.matmul(bank_of[:, 0:w], k_stack[b][0:R_MAX + 1, kb * P:(kb + 1) * P],
                                            q_stack[b][0:R_MAX + 1, q0:q0 + w], start=not diag, stop=True,
                                            skip_group_check=True)
                    last.then_inc(t_ready, 1)

                def weigh(h, b, n, slot):
                    c, kb, q0, w = T_UNITS[n]
                    pe.wait_ge(t_taken, slot + 1 + 2)
                    if kb == 0:
                        pe.wait_ge(kept, h * NCH + c + 1)
                    at = q0 - c * CH
                    parts = [(0, P, True), (P, w, False)] if kb >= 4 * c else [(0, w, False)]
                    for first, end, stop in parts:
                        if first < end:
                            last = nc.tensor.matmul(o_bank[c % 2][0:DHB + 1, at + first:at + end], v_stack[b][:, kb, :],
                                                    prob[n % 4][:, first:end], start=kb == 0 and first == 0, stop=stop,
                                                    skip_group_check=True)
                    last.then_inc(pv_done, 1)

                def flip(h, c, slot, bank_of):
                    pe.wait_ge(kept, h * NCH + c + 3)
                    pe.wait_ge(t_taken, slot + 1)
                    for j in range(CH // P):
                        last = nc.tensor.transpose(bank_of[:, j * P:(j + 1) * P], o_rows[c % 2][:, j * P:(j + 1) * P],
                                                   const["ident"][:])
                    last.then_inc(t_ready, 1)

                def step(h, b, turn, steps):
                    place = slots(steps)
                    later = 1
                    for what in steps:
                        slot = h * SLOTS + 1 + place.get(what, 0)
                        if what[0] == "s":
                            if what[1] == 0:
                                later = 2
                            s_piece(h + later, (b + later) % NB, what[1], turn + (b + later) // NB)
                        elif what[0] == "t":
                            t_piece(h, b, what[1], slot, t_bank[(1 + b + place[what]) % 2])
                        elif what[0] == "turn":
                            turn_max(h + 1, b + 1, slot, t_bank[(1 + b + place[what]) % 2])
                        elif what[0] == "flip":
                            flip(h, what[1], slot, t_bank[(1 + b + place[what]) % 2])
                        else:
                            weigh(h, b, what[1], h * SLOTS + 1 + place[("t", what[1])])

                def out_tile(t):
                    pe.wait_ge(o_t_done, t + 1)
                    if t >= DEEP:
                        pe.wait_ge(x_done, t - DEEP + 1)
                    for c in range(KC):
                        last = nc.tensor.matmul(out_bank[t % DEEP][:, 0:D], o_t[t % DEEP][:, c, :], w_out[:, c, :],
                                                start=c == 0, stop=c == KC - 1)
                    last.then_inc(out_done, 1)

                pe.wait_ge(after_set, 2)
                pe.wait_ge(same_in, 2 * NB * 16)
                for n in range(NSU):
                    s_piece(0, 0, n, 0)
                turn_max(0, 0, 0, t_bank[0])
                for n in range(AHEAD):
                    s_piece(1, 1, n, 0)
                with pe.Fori(0, HB // NB - 1) as i:
                    for b in range(NB):
                        step(i * NB + b, b, i, USUAL)
                for h in range(HB - NB, HB):
                    step(h, h % NB, h // NB, order(h))
                pe.wait_ge(w_out_in, 16)
                pe.wait_ge(t_taken, HB * SLOTS + 2)
                pe.wait_ge(s_used, HB * NSU + 2)
                for t in range(NT + 2):
                    if t < NT:
                        pe.wait_ge(o_done, t + 1)
                        if t >= DEEP:
                            pe.wait_ge(o_t_done, t - DEEP + 1)
                        for c in range(KC):
                            last = nc.tensor.transpose(turn_bank[t % DEEP][:, c * P:(c + 1) * P],
                                                       o[t % DEEP][:, c * P:(c + 1) * P], const["ident"][:])
                        last.then_inc(o_turned, 1)
                    if t >= 2:
                        out_tile(t - 2)

            @block.scalar
            def _(act):
                act.sem_inc(t_taken, 2)
                act.sem_inc(kept, 2)
                act.wait_ge(same_loaded, 16)
                for n, stack in enumerate((q_stack, k_stack)):
                    nc.scalar.activation(stack[NB - 1][0:2, :], same[0:2, n, :], ACT.Copy).then_inc(same_set, 1)

                act.wait_ge(buffers_set, 4)

                def negate(b, slot, bank_of):
                    act.wait_ge(t_ready, slot + 1)
                    nc.scalar.activation(neg_max[b % 2][:], bank_of[0:NT, 0:P], ACT.Copy, scale=-1.0).then_inc(t_taken, 1)

                def step(h, b, steps):
                    place = slots(steps)
                    for what in steps:
                        slot, bank_of = h * SLOTS + 1 + place.get(what, 0), t_bank[(1 + b + place.get(what, 0)) % 2]
                        if what[0] == "turn":
                            negate(b + 1, slot, bank_of)
                        elif what[0] == "flip":
                            act.wait_ge(t_ready, slot + 1)
                            nc.scalar.activation(o_sums[:, 4 * what[1]:4 * what[1] + 4, h if isinstance(h, int) else bass.ds(h, 1), :],
                                                 bank_of[:].rearrange("p (j d) -> p j d", d=P)[:, :, 0:DHB + 1],
                                                 ACT.Copy).then_inc(t_taken, 1)
                        elif what[0] == "weigh":
                            if what[1] + 1 in ENDS:
                                c = ENDS.index(what[1] + 1)
                                act.wait_ge(pv_done, h * NTU + ENDS[c] + 4)
                                nc.scalar.activation(o_rows[c % 2][0:DHB + 1, :], o_bank[c % 2][0:DHB + 1, :], ACT.Copy).then_inc(kept, 1)
                        elif what[0] == "t":
                            n = what[1]
                            w = T_UNITS[n][3]
                            act.wait_ge(t_ready, slot + 1)
                            act.wait_ge(pv_done, h * NTU + n + 1)
                            nc.scalar.activation(prob[n % 4][:, 0:w], bank_of[:, 0:w], ACT.Exp).then_inc(t_taken, 1)

                negate(0, 0, t_bank[0])
                with act.Fori(0, HB // NB - 1) as i:
                    for b in range(NB):
                        step(i * NB + b, b, USUAL)
                for h in range(HB - NB, HB):
                    step(h, h % NB, order(h))
                for t in range(NT):
                    act.wait_ge(o_turned, t + 1)
                    if t >= DEEP:
                        act.wait_ge(out_done, t - DEEP + 1)
                    nc.scalar.activation(o_t[t % DEEP], turn_bank[t % DEEP][:, 0:D].rearrange("p (c n) -> p c n", c=KC),
                                         ACT.Copy).then_inc(o_t_done, 1)

            @block.vector
            def _(dve):
                dve.wait_ge(consts_in, 16)
                nc.vector.tensor_copy(after[:], after_wide[:]).then_inc(after_set, 1)
                nc.vector.tensor_copy(ident16[:], const["ident"][:]).then_inc(after_set, 1)
                for p in range(2):
                    nc.vector.memset(part_max[p][:], -BIG).then_inc(buffers_set, 1)
                    nc.vector.memset(o_rows[p][:], 0.0).then_inc(buffers_set, 1)
                dve.wait_ge(buffers_set, 4)
                dve.sem_inc(s_used, 2)

                def maxima(h, b, first, last):
                    for n in range(first, last):
                        t, k0, w = S_UNITS[n]
                        dve.wait_ge(s_ready, h * NSU + n + 1)
                        nc.vector.tensor_reduce(part_max[b % 2][:, k0 // (2 * CH), t:t + 1], s_bank[n % 2][:, 0:w],
                                                AX.X, ALU.max).then_inc(s_used, 1)
                    if last == NSU:
                        dve.wait_ge(s_used, h * NSU + NSU + 2)
                        nc.vector.tensor_tensor(row_max[b % 2][:], part_max[b % 2][:, 0, :], part_max[b % 2][:, 1, :],
                                                ALU.max).then_inc(max_ready, 1)

                def step(h, b, steps):
                    later = 1
                    for what in steps:
                        if what[0] == "s":
                            if what[1] == 0:
                                later = 2
                            maxima(h + later, b + later, what[1], what[1] + 1)

                maxima(0, 0, 0, NSU)
                maxima(1, 1, 0, AHEAD)
                with dve.Fori(0, HB // NB - 1) as i:
                    for b in range(NB):
                        step(i * NB + b, b, USUAL)
                for h in range(HB - NB, HB):
                    step(h, h % NB, order(h))
                dve.wait_ge(t_taken, HB * SLOTS + 2)
                for t in range(NT + LATE):
                    p = t % DEEP
                    if t < NT:
                        nc.vector.reciprocal(inv[p][:], o_sums[:, t, :, DHB:]).then_inc(inv_done, 1)
                    if t >= LATE:
                        dve.wait_ge(out_done, t - LATE + 1)
                        nc.vector.tensor_tensor(x[:, t - LATE, :], x[:, t - LATE, :], out_bank[(t - LATE) % DEEP][:, 0:D],
                                                ALU.add).then_inc(x_done, 1)
                    if t < NT:
                        dve.wait_ge(inv_done, t + 1)
                        if t >= DEEP:
                            dve.wait_ge(o_turned, t - DEEP + 1)
                        nc.vector.tensor_tensor(o[p].rearrange("p (h d) -> p h d", d=DHB), o_sums[:, t, :, 0:DHB],
                                                inv[p][:].to_broadcast([P, HB, DHB]), ALU.mult).then_inc(o_done, 1)


def route(nc, tag, arg, xT, bank, const, rstd, w13, w2, load, slot, gate, owner):
    with Phase(nc, tag) as phase:
        sb, sem = phase.sb, phase.sem

        gate_w = sb("gate_w", [P, KC, E])
        prior = sb("prior", [P, E])
        before = sb("before", [P, P])
        number = sb("number", [P, SLOTS])
        top = sb("top", [P, NT])
        prob = sb("prob", [P, NT, E])
        biased = sb("biased", [P, NT, E])
        better = sb("better", [P, E, NT, E])
        rank = sb("rank", [P, NT, E])
        chosen = sb("chosen", [P, NT, E])
        total = sb("total", [P, NT, E])
        so_far = [sb(f"so_far{n}", [P, NT, E]) for n in range(2)]
        tiles = sb("tiles", [P, E])
        ends = [sb(f"ends{n}", [P, E]) for n in range(2)]
        place = sb("place", [P, NT, E])
        pick = sb("pick", [P, NT, E])
        part = sb("part", [P, NT, E])
        row = sb("row", [P, NT])
        passed = sb("passed", [P, SLOTS, E])
        expert = sb("expert", [P, SLOTS])
        gate_in = sem("gate_in")
        loaded = sem("loaded")
        logits_done = sem("logits_done")
        dve_step = sem("dve_step")
        shifted = sem("shifted")
        exp_done = sem("exp_done")
        chosen_done = sem("chosen_done")
        counted = sem("counted")
        with nc.Block() as block:
            @block.sync
            def _(sp):
                sp.dma_start(gate_w[:], arg["gate_w"].rearrange("(c p) e -> p c e", p=P)).then_inc(gate_in, 16)
                sp.dma_start(prior[:], arg["expert_bias"].partition_broadcast(P)).then_inc(gate_in, 16)
                sp.dma_start(before[:], arg["before"]).then_inc(gate_in, 16)
                sp.dma_start(number[:], arg["slot_number"].partition_broadcast(P)).then_inc(gate_in, 16)
                if load:
                    for c in range(KC):
                        rows = slice(c * P, (c + 1) * P)
                        for n, (routed, shared) in enumerate((("w1", "sw1"), ("w3", "sw3"))):
                            cols = slice(n * HID, (n + 1) * HID)
                            sp.dma_start(w13[:, c, 0:E, cols],
                                         arg[routed][:, rows, :].rearrange("e p f -> p e f")).then_inc(loaded, 16)
                            sp.dma_start(w13[:, c, E, cols], arg[shared][rows, :]).then_inc(loaded, 16)
                    for c in range(2):
                        rows = slice(c * HH, (c + 1) * HH)
                        sp.dma_start(w2[:, c, 0:E, :],
                                     arg["w2"][:, rows, :].rearrange("e p f -> p e f")).then_inc(loaded, 16)
                        sp.dma_start(w2[:, c, E, :], arg["sw2"][rows, :]).then_inc(loaded, 16)
                    sp.wait_ge(loaded, 12 * 16)

            @block.tensor
            def _(pe):
                pe.wait_ge(gate_in, 4 * 16)
                for t in range(NT):
                    for k in range(KC):
                        last = nc.tensor.matmul(bank[7][:, t * E:(t + 1) * E], xT[:, k, t * P:(t + 1) * P],
                                                gate_w[:, k, :], start=k == 0, stop=k == KC - 1)
                last.then_inc(logits_done, 1)
                pe.wait_ge(chosen_done, 1)
                nc.tensor.matmul(bank[6][:, 0:NT * E], before[:], chosen[:].rearrange("p t e -> p (t e)"),
                                 start=True, stop=True).then_inc(counted, 1)
                nc.tensor.matmul(bank[5][:, 0:NT * E], const["mean"][:], chosen[:].rearrange("p t e -> p (t e)"),
                                 start=True, stop=True).then_inc(counted, 1)

            @block.scalar
            def _(act):
                act.wait_ge(shifted, 1)
                nc.scalar.activation(prob[:], prob[:], ACT.Exp).then_inc(exp_done, 1)

            @block.vector
            def _(dve):
                chain = Chain(dve, dve_step)
                step, wait = chain.step, chain.wait
                scalar, tensor, copy, reduce = nc.vector.tensor_scalar, nc.vector.tensor_tensor, nc.vector.tensor_copy, nc.vector.tensor_reduce
                logits = bank[7][:, 0:NT * E].rearrange("p (t e) -> p t e", e=E)
                wide = [P, NT, E]
                dve.wait_ge(logits_done, 1)
                step(reduce(top[:], logits, AX.X, ALU.max))
                wait()
                tensor(prob[:], logits, top[:].unsqueeze(2).to_broadcast(wide), ALU.subtract).then_inc(shifted, 1)
                dve.wait_ge(exp_done, 1)
                step(reduce(top[:], prob[:], AX.X, ALU.add))
                wait()
                step(nc.vector.reciprocal(top[:], top[:]))
                wait()
                step(tensor(prob[:], prob[:], top[:].unsqueeze(2).to_broadcast(wide), ALU.mult))
                wait()
                dve.wait_ge(gate_in, 4 * 16)
                step(tensor(biased[:], prob[:], prior[:].unsqueeze(1).to_broadcast(wide), ALU.add))
                wait()
                for e in range(E):
                    one = biased[:, :, e:e + 1]
                    n = e + 1
                    step(tensor(better[:, e, :, 0:n], one.to_broadcast([P, NT, n]), biased[:, :, 0:n], ALU.is_gt))
                    if n < E:
                        step(tensor(better[:, e, :, n:E], one.to_broadcast([P, NT, E - n]), biased[:, :, n:E], ALU.is_ge))
                wait()
                step(reduce(rank[:], better[:].rearrange("p e t f -> p t f e"), AX.X, ALU.add))
                wait()
                scalar(chosen[:], rank[:], float(TOPK), None, ALU.is_lt).then_inc(chosen_done, 1)
                dve.wait_ge(counted, 2)
                within = bank[6][:, 0:NT * E].rearrange("p (t e) -> p t e", e=E)
                step(scalar(total[:], bank[5][:, 0:NT * E].rearrange("p (t e) -> p t e", e=E), float(S), None, ALU.mult))
                wait()
                step(copy(so_far[0][:], total[:]))
                wait()
                now, then = so_far
                for far in (1, 2, 4, 8):
                    step(tensor(then[:, far:, :], now[:, far:, :], now[:, :NT - far, :], ALU.add))
                    step(copy(then[:, :far, :], now[:, :far, :]))
                    wait()
                    now, then = then, now
                step(scalar(tiles[:], now[:, NT - 1, :], 1.0 / P, (P / 2.0 - 0.5) / P, ALU.mult, ALU.add))
                wait()
                step(scalar(tiles[:], tiles[:], ROUND, None, ALU.add))
                wait()
                step(scalar(tiles[:], tiles[:], ROUND, None, ALU.subtract))
                wait()
                step(copy(ends[0][:], tiles[:]))
                wait()
                end, next_end = ends
                for far in (1, 2, 4):
                    step(tensor(next_end[:, far:], end[:, far:], end[:, :E - far], ALU.add))
                    step(copy(next_end[:, :far], end[:, :far]))
                    wait()
                    end, next_end = next_end, end
                step(tensor(tiles[:], end[:], tiles[:], ALU.subtract))
                step(tensor(place[:], now[:], total[:], ALU.subtract))
                wait()
                step(scalar(tiles[:], tiles[:], float(P), None, ALU.mult))
                step(tensor(place[:], place[:], within, ALU.add))
                wait()
                step(tensor(place[:], place[:], tiles[:].unsqueeze(1).to_broadcast(wide), ALU.add))
                wait()
                for n in range(TOPK):
                    step(scalar(pick[:], rank[:], float(n), None, ALU.is_equal))
                    wait()
                    step(tensor(part[:], pick[:], place[:], ALU.mult))
                    step(tensor(pick[:], pick[:], prob[:], ALU.mult))
                    wait()
                    step(reduce(row[:], part[:], AX.X, ALU.add))
                    step(reduce(gate[:, n, :], pick[:], AX.X, ALU.add))
                    wait()
                    step(copy(slot[:, n, :], row[:]))
                    step(tensor(gate[:, n, :], gate[:, n, :], rstd[:], ALU.mult))
                    wait()
                shape = [P, SLOTS, E]
                step(tensor(passed[:], number[:].unsqueeze(2).to_broadcast(shape), end[:].unsqueeze(1).to_broadcast(shape), ALU.is_ge))
                wait()
                step(reduce(expert[:], passed[:], AX.X, ALU.add))
                wait()
                step(scalar(owner[:], expert[:], E - 1.0, None, ALU.min))
                wait()


def experts(nc, tag, arg, x, xT, bank, const, mean, rstd, w13, w2, load, sent, done, store=None):
    with Phase(nc, tag) as phase:
        sb, sem = phase.sb, phase.sem

        slot = sb("slot", [P, TOPK, NT], U32)
        gate = sb("gate", [P, TOPK, NT])
        owner = sb("owner", [P, SLOTS], U32)
        route(nc, tag + "g", arg, xT, bank, const, rstd, w13, w2, load, slot, gate, owner)

        ALL = NT + SLOTS
        routed = [sb(f"routed{n}", [P, D]) for n in range(4)]
        rows_in = [sb(f"rows_in{n}", [P, D]) for n in range(4)]
        rows_out = [sb(f"rows_out{n}", [P, D]) for n in range(4)]
        back = [[sb(f"back{n}{m}", [P, D]) for m in range(TOPK)] for n in range(4)]
        xs = [sb(f"xs{p}", [P, KC, P]) for p in range(2)]
        silu = [sb(f"silu{p}", [P, HID]) for p in range(2)]
        h = [sb(f"h{p}", [P, HID]) for p in range(2)]
        h_t = [sb(f"h_t{p}", [HH, 2, P]) for p in range(2)]
        routed_ready = sem("routed_ready")
        scattered = [sem(f"scattered{n}") for n in range(4)]
        loaded = [sem(f"loaded{n}") for n in range(4)]
        stored = [sem(f"stored{n}") for n in range(4)]
        gathered = [sem(f"gathered{n}") for n in range(4)]
        flipped = sem("flipped")
        xs_done = sem("xs_done")
        up_done = sem("up_done")
        silu_done = sem("silu_done")
        h_done = sem("h_done")
        turned = sem("turned")
        h_t_done = sem("h_t_done")
        down_done = sem("down_done")
        y_taken = sem("y_taken")
        first_added = sem("first_added")
        added = sem("added")
        written = sem("written")
        up_bank, turn_bank, y_bank, flip_bank = bank[0:2], bank[2:4], bank[4:6], bank[6:8]

        def walk(eng, step):
            for n in range(4):
                step(0, n, n)
            with eng.Fori(1, NT // 4) as i:
                for n in range(4):
                    step(i, n, 4 + n)
            for n in range(8):
                step(NT // 4 + n // 4, n % 4, NT + n)
            with eng.Fori(NT // 4 + 2, ALL // 4) as i:
                for n in range(4):
                    step(i, n, NT + 8 + n)
            for n in range(3):
                step(ALL // 4, n, ALL + n)

        def there(like, lag, first=0, last=ALL):
            return first <= like - lag < last

        def rows(i, n):
            first = (i * 4 + n - NT) * P
            return slice(first, first + P) if isinstance(i, int) else bass.ds(first, P)

        with nc.Block() as block:
            @block.gpsimd
            def _(pool):
                for k in range(TOPK * NT):
                    t, m = divmod(k, TOPK)
                    pool.wait_ge(routed_ready, k + 1)
                    nc.gpsimd.indirect_dma_start(sent, bass.IndirectOffsetOnAxis(ap=slot[:, m, t:t + 1], axis=0),
                                                 routed[k % 4][:], None).then_inc(scattered[k % 4], 16)
                with pool.Fori(NT // 4, ALL // 4) as i:
                    for n in range(4):
                        pool.wait_ge(y_taken, i * 4 + n + 1 + 2)
                        nc.gpsimd.dma_start(done[rows(i, n), :], rows_out[n][:]).then_inc(stored[n], 16)
                for n in range(4):
                    pool.wait_ge(stored[n], SLOTS // 4 * 16)
                for t in range(NT):
                    if t >= 4:
                        pool.wait_ge(added, t - 3)
                    for m in range(TOPK):
                        nc.gpsimd.indirect_dma_start(back[t % 4][m][:], None, done,
                                                     bass.IndirectOffsetOnAxis(ap=slot[:, m, t:t + 1], axis=0)
                                                     ).then_inc(gathered[t % 4], 16)

            @block.sync
            def _(sp):
                def fetch(i, n):
                    sp.wait_ge(flipped, i * 4 + n - NT + 1)
                    sp.dma_start(rows_in[n][:], sent[rows(i, n), :]).then_inc(loaded[n], 16)

                for n in range(4):
                    sp.wait_ge(scattered[n], TOPK * NT // 4 * 16)
                for n in range(4):
                    fetch(NT // 4, n)
                with sp.Fori(NT // 4 + 1, ALL // 4) as i:
                    for n in range(4):
                        fetch(i, n)
                if store is not None:
                    for t in range(NT):
                        sp.wait_ge(added, t + 1)
                        sp.dma_start(store[t * P:(t + 1) * P, :], x[:, t, :]).then_inc(written, 16)
                    sp.wait_ge(written, 16 * NT)
                else:
                    sp.wait_ge(added, NT)

            @block.tensor
            def _(pe):
                owners = {}

                def know(i, like):
                    first, last = max(like - 3, NT), min(like + 2, ALL - 1)
                    if first <= last:
                        one = i * 4 + (first - like) - NT
                        at = slice(one, one + last + 1 - first) if isinstance(one, int) else bass.ds(one, last + 1 - first)
                        _, values = nc.values_load_multi_w_load_instructions(
                            owner[0:1, at], engines=(mybir.EngineType.PE,), min_val=0, max_val=E - 1)
                        owners.clear()
                        owners.update(zip(range(first, last + 1), values))

                def flip(i, n, tile):
                    pe.wait_ge(loaded[n], (i - NT // 4) * 16 + 16)
                    pe.wait_ge(xs_done, tile + 1)
                    for c in range(KC):
                        last = nc.tensor.transpose(flip_bank[n % 2][:, c * P:(c + 1) * P], rows_in[n][:, c * P:(c + 1) * P],
                                                   const["ident"][:])
                    last.then_inc(flipped, 1)

                def up(n, tile, e):
                    pe.wait_ge(xs_done, tile + 1 + 2)
                    pe.wait_ge(h_done, tile + 1)
                    for k in range(KC):
                        last = nc.tensor.matmul(up_bank[n % 2][:, 0:2 * HID], xs[n % 2][:, k, :], w13[:, k, e, :],
                                                start=k == 0, stop=k == KC - 1)
                    last.then_inc(up_done, 1)

                def turn(n, tile):
                    pe.wait_ge(h_done, tile + 1 + 2)
                    pe.wait_ge(h_t_done, tile + 1)
                    for c in range(2):
                        last = nc.tensor.transpose(turn_bank[n % 2][0:HH, c * P:(c + 1) * P],
                                                   h[n % 2][:, c * HH:(c + 1) * HH], const["ident"][:])
                    last.then_inc(turned, 1)

                def down(n, tile, e):
                    pe.wait_ge(h_t_done, tile + 1 + 2)
                    pe.wait_ge(y_taken, tile + 1)
                    for c in range(2):
                        last = nc.tensor.matmul(y_bank[n % 2][:, 0:D], h_t[n % 2][:, c, :], w2[:, c, e, :],
                                                start=c == 0, stop=c == 1)
                    last.then_inc(down_done, 1)

                pe.sem_inc(flipped, 4)
                pe.sem_inc(up_done, 2)
                pe.sem_inc(turned, 2)
                pe.sem_inc(down_done, 2)

                def expert(like):
                    return slice(E, E + 1) if like < NT else bass.ds(owners[like], 1)

                def step(i, n, like):
                    tile = i * 4 + n
                    if n == 0:
                        know(i, like)
                    if there(like, 0, NT):
                        flip(i, n, tile)
                    if there(like, 1):
                        up(n + 1, tile - 1, expert(like - 1))
                    if there(like, 2):
                        turn(n, tile - 2)
                    if there(like, 3):
                        down(n + 1, tile - 3, expert(like - 3))

                walk(pe, step)

            @block.scalar
            def _(act):
                act.sem_inc(xs_done, 2)
                act.sem_inc(h_t_done, 2)

                def place(i, n, tile, shared):
                    if shared:
                        act.wait_ge(up_done, tile + 1)
                        at = slice(tile * P, tile * P + P) if isinstance(i, int) else bass.ds(tile * P, P)
                        have = xT[:, :, at]
                    else:
                        act.wait_ge(flipped, tile - NT + 1 + 4)
                        act.wait_ge(up_done, tile + 1)
                        have = flip_bank[n % 2][:, 0:D].rearrange("p (c n) -> p c n", c=KC)
                    nc.scalar.activation(xs[n % 2][:], have, ACT.Copy).then_inc(xs_done, 1)

                def step(i, n, like):
                    tile = i * 4 + n
                    if there(like, 0):
                        place(i, n, tile, like < NT)
                    if there(like, 1):
                        act.wait_ge(up_done, tile - 1 + 1 + 2)
                        act.wait_ge(h_done, tile - 1 + 1)
                        nc.scalar.activation(silu[(n + 1) % 2][:], up_bank[(n + 1) % 2][:, 0:HID],
                                             ACT.Silu).then_inc(silu_done, 1)
                    if there(like, 2):
                        act.wait_ge(turned, tile - 2 + 1 + 2)
                        act.wait_ge(down_done, tile - 2 + 1)
                        nc.scalar.activation(h_t[n % 2][:], turn_bank[n % 2][0:HH, 0:2 * P].rearrange("p (c n) -> p c n", c=2),
                                             ACT.Copy).then_inc(h_t_done, 1)

                walk(act, step)

            @block.vector
            def _(dve):
                dve.sem_inc(h_done, 2)
                dve.sem_inc(y_taken, 2)

                def send(i, n, tile):
                    for m in range(TOPK):
                        buffer = (n * TOPK + m) % 4
                        at = slice(tile, tile + 1) if isinstance(i, int) else bass.ds(tile, 1)
                        here = x[:, tile, :] if isinstance(i, int) else x[:, bass.ds(tile, 1), :].rearrange("p a d -> p (a d)")
                        used = i * 2 + (n * TOPK + m) // 4
                        if not isinstance(used, int) or used:
                            dve.wait_ge(scattered[buffer], used * 16)
                        nc.vector.tensor_scalar(routed[buffer][:], here, mean[:, at], gate[:, m, at],
                                                ALU.subtract, ALU.mult).then_inc(routed_ready, 1)

                def take(i, n, tile, shared):
                    y = y_bank[n % 2][:, 0:D]
                    dve.wait_ge(down_done, tile + 1 + 2)
                    if shared:
                        at = tile if isinstance(tile, int) else bass.ds(tile, 1)
                        here = x[:, at, :] if isinstance(tile, int) else x[:, at, :].rearrange("p a d -> p (a d)")
                        nc.vector.tensor_tensor(here, here, y, ALU.add).then_inc(y_taken, 1)
                    else:
                        if not isinstance(i, int) or i > NT // 4:
                            dve.wait_ge(stored[n], (i - NT // 4) * 16)
                        nc.vector.tensor_copy(rows_out[n][:], y).then_inc(y_taken, 1)

                def step(i, n, like):
                    tile = i * 4 + n
                    if there(like, 0, 0, NT):
                        send(i, n, tile)
                    if there(like, 1):
                        dve.wait_ge(silu_done, tile - 1 + 1)
                        dve.wait_ge(turned, tile - 1 + 1)
                        nc.vector.tensor_tensor(h[(n + 1) % 2][:], up_bank[(n + 1) % 2][:, HID:2 * HID],
                                                silu[(n + 1) % 2][:], ALU.mult).then_inc(h_done, 1)
                    if there(like, 3):
                        take(i + (n - 3) // 4, (n - 3) % 4, tile - 3, like - 3 < NT)

                walk(dve, step)
                for t in range(NT):
                    dve.wait_ge(gathered[t % 4], (t // 4 + 1) * TOPK * 16)
                    nc.vector.tensor_tensor(x[:, t, :], x[:, t, :], back[t % 4][0][:], ALU.add).then_inc(first_added, 1)
                    dve.wait_ge(first_added, t + 1)
                    nc.vector.tensor_tensor(x[:, t, :], x[:, t, :], back[t % 4][1][:], ALU.add).then_inc(added, 1)


def program(nc, arg, out):
    with ExitStack() as ctx:
        def sb(name, shape, dt=F32, scope=None):
            return (scope or ctx).enter_context(nc.sbuf_tensor(name, shape, dt))

        psum = ctx.enter_context(nc.psum_tensor("psum", [P, 8 * CH], F32))
        bank = [psum[:, n * CH:(n + 1) * CH] for n in range(8)]
        pair = [psum[:, n * 2 * CH:(n + 1) * 2 * CH] for n in range(2)]
        x = sb("x", [P, NT, D])
        xT = sb("xT", [P, KC, S])
        const = {"ident": sb("ident", [P, P]), "causal": sb("causal", [P, P], BF16), "mean": sb("mean", [P, P])}
        causal_wide = sb("causal_wide", [P, P])
        mean, rstd = sb("row_mean", [P, NT]), sb("row_rstd", [P, NT])
        sent = nc.dram_tensor("sent", (SLOTS * P, D), F32, kind="Internal").ap()
        done = nc.dram_tensor("done", (SLOTS * P, D), F32, kind="Internal").ap()
        x_in = ctx.enter_context(nc.semaphore("x_in"))
        with nc.Block() as block:
            @block.sync
            def _(sp):
                sp.dma_start(x[:], arg["hidden"].rearrange("(t p) d -> p t d", p=P)).then_inc(x_in, 16)
                sp.dma_start(const["ident"][:], arg["ident"]).then_inc(x_in, 16)
                sp.dma_start(causal_wide[:], arg["causal"]).then_inc(x_in, 16)
                sp.wait_ge(x_in, 3 * 16)

            @block.vector
            def _(dve):
                nc.vector.memset(const["mean"][:], 1.0 / S)
                dve.wait_ge(x_in, 3 * 16)
                nc.vector.tensor_copy(const["causal"][:], causal_wide[:])

        layernorm(nc, "ln1", x, xT, bank, const["ident"], mean, rstd)
        with ExitStack() as a:
            bias = sb("bias", [P, TRI[NT]], BF16, a)
            empty = sb("empty", [P, NT], F32, a)
            filled = sb("filled", [P, NT], F32, a)
            index_mask(nc, arg, x, xT, bank, const, bias, empty, filled, sent)
            k_hi = sb("ka_hi", [P, S], F32R, a)
            k_lo = sb("ka_lo", [P, S], F32R, a)
            c_stack = sb("c_stack", [P, NT, 2 * RANK], F32R, a)
            w_all = sb("w_all", [P, KC, HA, P], F32, a)
            w_out = sb("wa_out", [P, HA, D], F32, a)
            nowhere = sb("nowhere", [P, D], F32, a)
            rope = sb("rope", [P, 2, NT, HALF], F32, a)
            xT_rows = nc.dram_tensor("xT_rows", (P, KC, S), F32, kind="Internal").ap()
            prepare_a(nc, arg, x, xT, bank, const, k_hi, k_lo, c_stack, w_all, w_out, nowhere, rope, xT_rows)
            attention_a(nc, arg, x, xT, bank, const, k_hi, k_lo, c_stack, bias, empty, filled, w_all, w_out, nowhere, rope,
                        xT_rows)
        w13 = sb("w13", [P, KC, EE, 2 * HID])
        w2 = sb("w2", [HH, 2, EE, D])
        layernorm(nc, "ln2", x, xT, bank, const["ident"], mean, rstd)
        experts(nc, "f1", arg, x, xT, bank, const, mean, rstd, w13, w2, load=True, sent=sent, done=done)
        layernorm(nc, "ln3", x, xT, bank, const["ident"], mean, rstd)
        stash = {name: nc.dram_tensor(f"stash_{name}", (D, S), F32, kind="Internal").ap()
                 for name in ("q_hi", "q_lo", "k_hi", "k_lo")}
        with ExitStack() as b:
            values = sb("values", [P, HB, NT, DHB + 1], F32, b)
            prepare_b(nc, arg, xT, bank, stash, values)
            max_rows = nc.dram_tensor("max_rows", (NT, P), F32, kind="Internal").ap()
            attention_b(nc, arg, x, xT, pair, bank, const, stash, max_rows, values)
        layernorm(nc, "ln4", x, xT, bank, const["ident"], mean, rstd)
        experts(nc, "f2", arg, x, xT, bank, const, mean, rstd, w13, w2, load=False, sent=sent, done=done, store=out)


def kernel(**inputs):
    import numpy as np
    import concourse.bacc as bacc
    from concourse.bass_utils import run_bass_kernel_spmd

    a = {k: np.asarray(v) for k, v in inputs.items()}
    A, B, M = "L0_attn_a_", "L0_attn_b_", "L0_ffn_"
    wq = a[A + "Wq"].reshape(D, HA, DN + DR)
    w_ukv = a[A + "W_ukv"].reshape(RANK, HA, DN + DV)
    lay = {
        "hidden": a[A + "hidden_states"].reshape(S, D),
        "Wq_idx": a[A + "Wq_idx"], "Wk_idx": a[A + "Wk_idx"],
        "bq_idx": a[A + "bq_idx"].reshape(HI, DI).T, "bk_idx": a[A + "bk_idx"].reshape(HI, DI).T,
        "idx_w": a[A + "idx_w"], "w_ctrl": a[A + "w_ctrl"].reshape(KC, P).T, "b_ctrl": a[A + "b_ctrl"].reshape(1),
        "Wq": a[A + "Wq"], "Wq_nope_T": wq[:, :, :DN].transpose(2, 1, 0),
        "W_uk_T": w_ukv[:, :, :DN].transpose(2, 1, 0), "W_uv_T": w_ukv[:, :, DN:].transpose(2, 1, 0),
        "Wo": a[A + "Wo"].reshape(HA, DV, D).transpose(1, 0, 2),
        "W_dkv": a[A + "W_dkv"], "kv_norm_w": a[A + "kv_norm_w"],
        "b_dkv_T": a[B + "w_dkv"].T, "b_q_T": a[B + "w_q"].T, "b_uk_T": a[B + "w_uk"].T,
        "b_uv_T": a[B + "w_uv"].T, "b_o_T": a[B + "w_o"].T,
        "gate_w": a[M + "gate_w"], "expert_bias": a[M + "expert_bias"],
        "w1": a[M + "w1"], "w2": a[M + "w2"], "w3": a[M + "w3"],
        "sw1": a[M + "sw1"], "sw2": a[M + "sw2"], "sw3": a[M + "sw3"],
    }
    inv_freq = (1.0 / 10000.0 ** (np.arange(0, DR, 2, dtype=np.float32) / DR)).astype(np.float32)
    angle = (np.arange(S, dtype=np.float32)[:, None] * inv_freq[None, :]).astype(np.float32)
    table = {"cos": np.cos(angle).astype(np.float32), "sin": np.sin(angle).astype(np.float32)}
    for name, value in table.items():
        tiles = value.reshape(NT, P, HALF).transpose(1, 0, 2)
        lay[name + "_k"] = tiles
        lay[name + "_q"] = (tiles * np.float32(SCALE_A)).astype(np.float32)
    row, col = np.arange(P)[:, None], np.arange(P)[None, :]
    lay["ident"] = np.eye(P, dtype=np.float32)
    lay["before"] = np.where(row < col, 1.0, 0.0).astype(np.float32)
    lay["slot_number"] = np.arange(SLOTS, dtype=np.float32)
    lay["causal"] = np.where(col <= row, 0.0, NEG).astype(np.float32)
    lay["b_after"] = np.stack([np.where(col > row, HIDE, 0.0), np.where(row > col, HIDE, 0.0)], axis=1).astype(np.float32)
    ones, zeros = np.ones(S, np.float32), np.zeros(S, np.float32)
    lay["b_same"] = np.stack([np.stack([ones, zeros]), np.stack([np.float32(SLOPE) * np.arange(S, dtype=np.float32), ones])],
                             axis=1)

    nc = bacc.Bacc("TRN2", target_bir_lowering=False, num_devices=1)
    arrays, arg = {}, {}
    for name, value in lay.items():
        value = np.ascontiguousarray(value)
        arrays[f"in_{name}"] = value
        arg[name] = nc.dram_tensor(f"in_{name}", value.shape, mybir.dt.from_np(value.dtype), kind="ExternalInput").ap()
    out = nc.dram_tensor("out", (S, D), F32, kind="ExternalOutput").ap()
    program(nc, arg, out)
    result = run_bass_kernel_spmd(nc, [arrays], core_ids=[0])
    return result.results[0]["out"].reshape(1, S, D)
```
